# Optimizing a Trainium2 kernel written in Bass

```python
import numpy as np
import jax
import jax.numpy as jnp

def _softmax(x, axis=-1):
    return jax.nn.softmax(x, axis=axis)

def _gelu(x):
    return jax.nn.gelu(x, approximate=True)

def _silu(x):
    return jax.nn.silu(x)

def _sigmoid(x):
    return jax.nn.sigmoid(x)

def _layernorm(x, axis=-1, eps=1e-05):
    m = jnp.mean(x, axis=axis, keepdims=True)
    v = jnp.var(x, axis=axis, keepdims=True)
    return (x - m) / jnp.sqrt(v + eps)

def _scatter_add(tgt, idx, src, axis=0):
    return tgt.at[idx].add(src)

def _segment_sum(src, seg, n):
    return jax.ops.segment_sum(src, seg, n)
kernel_name = 'mk_gnn_ffn_d1_gnn_r8_29a998'

def setup_inputs(seed: int=0):
    np.random.seed(seed)
    _w = jnp.asarray

    def _rec_inputs():
        import jax
        import jax.numpy as jnp
        _gk = jax.random.key(seed)
        x = -0.0006008 + 1.001 * jax.random.normal(jax.random.fold_in(_gk, 1), (6250, 512), jnp.float32)
        src = jax.random.randint(jax.random.fold_in(_gk, 2), (100000,), 0, 6250, jnp.int32)
        dst = jax.random.randint(jax.random.fold_in(_gk, 3), (100000,), 0, 6250, jnp.int32)
        _o = jnp.argsort(dst, stable=True)
        src = src[_o]
        dst = dst[_o]
        edge_attr_20 = jax.random.uniform(jax.random.fold_in(_gk, 12), (100000, 20), jnp.float32, 0.0, 0.999999)
        edge_attr_3 = -0.0005747 + 0.998114 * jax.random.normal(jax.random.fold_in(_gk, 13), (100000, 3), jnp.float32)
        edge_weight = jax.random.uniform(jax.random.fold_in(_gk, 14), (100000,), jnp.float32, 0.0, 0.999973)
        return (x, src, dst, edge_attr_20, edge_attr_3, edge_weight)
    x, src, dst, edge_attr_20, edge_attr_3, edge_weight = _rec_inputs()

    def _L0_gnn_setup():
        import jax, jax.numpy as jnp
        import numpy as np
        N_ATOMS = 625
        N_EDGES = 6250
        C = 128
        F = 128
        N_RBF = 20
        LOG2 = float(np.log(2.0))
        Y0 = float(1.0 / np.sqrt(4.0 * np.pi))
        Y1_SCALE = float(np.sqrt(3.0 / (4.0 * np.pi)))

        def shifted_softplus(x):
            return jax.nn.softplus(x) - LOG2

        def _forward(x, idx_i, idx_j, f_ij, rcut_ij, r_ij, W_in2f_s, W_in2f_v, Wf1, bf1, Wf2, bf2, W1_s, W1_v, W2_s, W2_v):
            n = x.shape[0]
            e = r_ij.shape[0]
            xs = x[:, :C] @ (W_in2f_s / np.sqrt(C))
            xv = jnp.einsum('nci,cf->nfi', x[:, C:].reshape(n, C, 3), W_in2f_v) / np.sqrt(C)
            sj = xs[idx_j]
            vj = xv[idx_j]
            u = r_ij / jnp.linalg.norm(r_ij, axis=-1, keepdims=True)
            Yv = Y1_SCALE * u
            o0a = sj * Y0
            o0b = jnp.einsum('efi,ei->ef', vj, Yv) / np.sqrt(3.0)
            s2 = jnp.stack([o0a, o0b], axis=-1).reshape(e, 2 * F)
            ova = sj[:, :, None] * Yv[:, None, :]
            ovb = vj * Y0
            v2 = jnp.stack([ova, ovb], axis=2)
            w1 = jnp.cross(vj, Yv[:, None, :]) / np.sqrt(2.0)
            ax, ay, az = (vj[..., 0], vj[..., 1], vj[..., 2])
            bx, by, bz = (Yv[:, None, 0], Yv[:, None, 1], Yv[:, None, 2])
            t = jnp.stack([(ax * by + ay * bx) / np.sqrt(2.0), (ay * bz + az * by) / np.sqrt(2.0), (2.0 * az * bz - ax * bx - ay * by) / np.sqrt(6.0), (az * bx + ax * bz) / np.sqrt(2.0), (ax * bx - ay * by) / np.sqrt(2.0)], axis=-1)
            h = shifted_softplus(f_ij @ Wf1 + bf1)
            W = (h @ Wf2 + bf2) * rcut_ij[:, None]
            m_s = s2 * W[:, :2 * F]
            m_v = (v2.reshape(e, 2 * F, 3) * W[:, 2 * F:4 * F, None]).reshape(e, 6 * F)
            m_w = (w1 * W[:, 4 * F:5 * F, None]).reshape(e, 3 * F)
            m_t = (t * W[:, 5 * F:6 * F, None]).reshape(e, 5 * F)
            x_ij = jnp.concatenate([m_s, m_v, m_w, m_t], axis=1)
            agg = jax.ops.segment_sum(x_ij, idx_i, num_segments=n)
            S = agg[:, :2 * F] @ (W1_s / np.sqrt(2 * F))
            V = jnp.einsum('nmi,mc->nci', agg[:, 2 * F:8 * F].reshape(n, 2 * F, 3), W1_v) / np.sqrt(2 * F)
            S = shifted_softplus(S)
            S = S @ (W2_s / np.sqrt(C))
            V = jnp.einsum('nci,cd->ndi', V, W2_v) / np.sqrt(C)
            return jnp.concatenate([S, V.reshape(n, 3 * C)], axis=1)
        key = jax.random.key(seed)
        ks = jax.random.split(key, 16)
        f32 = jnp.float32
        x = jax.random.normal(ks[0], (N_ATOMS, 4 * C), f32)
        idx_i = jnp.sort(jax.random.randint(ks[1], (N_EDGES,), 0, N_ATOMS))
        idx_j = jax.random.randint(ks[2], (N_EDGES,), 0, N_ATOMS)
        f_ij = jax.random.uniform(ks[3], (N_EDGES, N_RBF), f32)
        rcut_ij = jax.random.uniform(ks[4], (N_EDGES,), f32)
        r_ij = jax.random.normal(ks[5], (N_EDGES, 3), f32)
        W_in2f_s = jax.random.normal(ks[6], (C, F), f32)
        W_in2f_v = jax.random.normal(ks[7], (C, F), f32)
        Wf1 = jax.random.normal(ks[8], (N_RBF, F), f32) / np.sqrt(N_RBF)
        bf1 = 0.1 * jax.random.normal(ks[9], (F,), f32)
        Wf2 = jax.random.normal(ks[10], (F, 6 * F), f32) / np.sqrt(F)
        bf2 = 0.1 * jax.random.normal(ks[11], (6 * F,), f32)
        W1_s = jax.random.normal(ks[12], (2 * F, C), f32)
        W1_v = jax.random.normal(ks[13], (2 * F, C), f32)
        W2_s = jax.random.normal(ks[14], (C, C), f32)
        W2_v = jax.random.normal(ks[15], (C, C), f32)
        return dict(x=x, idx_i=idx_i, idx_j=idx_j, f_ij=f_ij, rcut_ij=rcut_ij, r_ij=r_ij, W_in2f_s=W_in2f_s, W_in2f_v=W_in2f_v, Wf1=Wf1, bf1=bf1, Wf2=Wf2, bf2=bf2, W1_s=W1_s, W1_v=W1_v, W2_s=W2_s, W2_v=W2_v)
    _L0_gnn_all = _L0_gnn_setup()
    _L0_gnn_in = {k: v for k, v in _L0_gnn_all.items() if k in ('W_in2f_s', 'W_in2f_v', 'Wf1', 'bf1', 'Wf2', 'bf2', 'W1_s', 'W1_v', 'W2_s', 'W2_v')}
    del _L0_gnn_all

    def _L0_ffn_setup():
        import jax, jax.numpy as jnp
        import numpy as np
        MARK_AX, OP_ADD, OP_SUB = (0, 1, 2)
        ALU_LO, ALU_HI = (16, 32)
        AX_CARRY_LO, AX_CARRY_HI = (48, 64)
        OPCODE_BASE = 80
        OUTPUT_LO, OUTPUT_HI, CARRY = (128, 144, 160)
        NIB_A, NIB_B, OP_START = (0, 1, 10)
        RESULT, CARRY_OUT = (100, 101)
        GE_POS, GE_DIM = (8, 160)
        OPC_ADD, OPC_SUB = (25, 26)
        B, S, D = (8, 512, 512)

        def _decode_nibble(x, base):
            return jnp.argmax(x[..., base:base + 16] > 0.5, axis=-1).astype(x.dtype)

        def _pipeline(h, W, b):
            for i in range(3):
                h = jnp.einsum('bspd,od->bspo', h, W[i]) + b[i]
                if i < 2:
                    h = jax.nn.relu(h)
            return h
        key = jax.random.key(seed)
        kx, k1, k2, k3, k4 = jax.random.split(key, 5)
        x_bd = jax.random.uniform(kx, (B, S, D), dtype=jnp.float32)
        Wa = jax.random.normal(k1, (3, GE_DIM, GE_DIM), dtype=jnp.float32) * 0.05
        ba = jax.random.normal(k2, (3, GE_DIM), dtype=jnp.float32) * 0.05
        Ws = jax.random.normal(k3, (3, GE_DIM, GE_DIM), dtype=jnp.float32) * 0.05
        bs = jax.random.normal(k4, (3, GE_DIM), dtype=jnp.float32) * 0.05
        return {'x_bd': x_bd, 'Wa': Wa, 'ba': ba, 'Ws': Ws, 'bs': bs}
    _L0_ffn_all = _L0_ffn_setup()
    _L0_ffn_in = {k: v for k, v in _L0_ffn_all.items() if k in ('Wa', 'ba', 'Ws', 'bs')}
    del _L0_ffn_all
    return {'x': x, 'src': src, 'dst': dst, 'edge_attr_20': edge_attr_20, 'edge_attr_3': edge_attr_3, 'edge_weight': edge_weight, 'L0_gnn_W_in2f_s': _L0_gnn_in['W_in2f_s'], 'L0_gnn_W_in2f_v': _L0_gnn_in['W_in2f_v'], 'L0_gnn_Wf1': _L0_gnn_in['Wf1'], 'L0_gnn_bf1': _L0_gnn_in['bf1'], 'L0_gnn_Wf2': _L0_gnn_in['Wf2'], 'L0_gnn_bf2': _L0_gnn_in['bf2'], 'L0_gnn_W1_s': _L0_gnn_in['W1_s'], 'L0_gnn_W1_v': _L0_gnn_in['W1_v'], 'L0_gnn_W2_s': _L0_gnn_in['W2_s'], 'L0_gnn_W2_v': _L0_gnn_in['W2_v'], 'L0_ffn_Wa': _L0_ffn_in['Wa'], 'L0_ffn_ba': _L0_ffn_in['ba'], 'L0_ffn_Ws': _L0_ffn_in['Ws'], 'L0_ffn_bs': _L0_ffn_in['bs']}

def reference(x, src, dst, edge_attr_20, edge_attr_3, edge_weight, L0_gnn_W_in2f_s, L0_gnn_W_in2f_v, L0_gnn_Wf1, L0_gnn_bf1, L0_gnn_Wf2, L0_gnn_bf2, L0_gnn_W1_s, L0_gnn_W1_v, L0_gnn_W2_s, L0_gnn_W2_v, L0_ffn_Wa, L0_ffn_ba, L0_ffn_Ws, L0_ffn_bs):
    import jax
    import jax.numpy as jnp

    def _L0_gnn_ref(x, idx_i, idx_j, f_ij, rcut_ij, r_ij, W_in2f_s, W_in2f_v, Wf1, bf1, Wf2, bf2, W1_s, W1_v, W2_s, W2_v):
        import jax, jax.numpy as jnp
        import numpy as np
        N_ATOMS = 625
        N_EDGES = 6250
        C = 128
        F = 128
        N_RBF = 20
        LOG2 = float(np.log(2.0))
        Y0 = float(1.0 / np.sqrt(4.0 * np.pi))
        Y1_SCALE = float(np.sqrt(3.0 / (4.0 * np.pi)))

        def shifted_softplus(x):
            return jax.nn.softplus(x) - LOG2

        def _forward(x, idx_i, idx_j, f_ij, rcut_ij, r_ij, W_in2f_s, W_in2f_v, Wf1, bf1, Wf2, bf2, W1_s, W1_v, W2_s, W2_v):
            n = x.shape[0]
            e = r_ij.shape[0]
            xs = x[:, :C] @ (W_in2f_s / np.sqrt(C))
            xv = jnp.einsum('nci,cf->nfi', x[:, C:].reshape(n, C, 3), W_in2f_v) / np.sqrt(C)
            sj = xs[idx_j]
            vj = xv[idx_j]
            u = r_ij / jnp.linalg.norm(r_ij, axis=-1, keepdims=True)
            Yv = Y1_SCALE * u
            o0a = sj * Y0
            o0b = jnp.einsum('efi,ei->ef', vj, Yv) / np.sqrt(3.0)
            s2 = jnp.stack([o0a, o0b], axis=-1).reshape(e, 2 * F)
            ova = sj[:, :, None] * Yv[:, None, :]
            ovb = vj * Y0
            v2 = jnp.stack([ova, ovb], axis=2)
            w1 = jnp.cross(vj, Yv[:, None, :]) / np.sqrt(2.0)
            ax, ay, az = (vj[..., 0], vj[..., 1], vj[..., 2])
            bx, by, bz = (Yv[:, None, 0], Yv[:, None, 1], Yv[:, None, 2])
            t = jnp.stack([(ax * by + ay * bx) / np.sqrt(2.0), (ay * bz + az * by) / np.sqrt(2.0), (2.0 * az * bz - ax * bx - ay * by) / np.sqrt(6.0), (az * bx + ax * bz) / np.sqrt(2.0), (ax * bx - ay * by) / np.sqrt(2.0)], axis=-1)
            h = shifted_softplus(f_ij @ Wf1 + bf1)
            W = (h @ Wf2 + bf2) * rcut_ij[:, None]
            m_s = s2 * W[:, :2 * F]
            m_v = (v2.reshape(e, 2 * F, 3) * W[:, 2 * F:4 * F, None]).reshape(e, 6 * F)
            m_w = (w1 * W[:, 4 * F:5 * F, None]).reshape(e, 3 * F)
            m_t = (t * W[:, 5 * F:6 * F, None]).reshape(e, 5 * F)
            x_ij = jnp.concatenate([m_s, m_v, m_w, m_t], axis=1)
            agg = jax.ops.segment_sum(x_ij, idx_i, num_segments=n)
            S = agg[:, :2 * F] @ (W1_s / np.sqrt(2 * F))
            V = jnp.einsum('nmi,mc->nci', agg[:, 2 * F:8 * F].reshape(n, 2 * F, 3), W1_v) / np.sqrt(2 * F)
            S = shifted_softplus(S)
            S = S @ (W2_s / np.sqrt(C))
            V = jnp.einsum('nci,cd->ndi', V, W2_v) / np.sqrt(C)
            return jnp.concatenate([S, V.reshape(n, 3 * C)], axis=1)
        return _forward(x, idx_i, idx_j, f_ij, rcut_ij, r_ij, W_in2f_s, W_in2f_v, Wf1, bf1, Wf2, bf2, W1_s, W1_v, W2_s, W2_v)

    def _L0_ffn_ref(x_bd, Wa, ba, Ws, bs):
        import jax, jax.numpy as jnp
        import numpy as np
        MARK_AX, OP_ADD, OP_SUB = (0, 1, 2)
        ALU_LO, ALU_HI = (16, 32)
        AX_CARRY_LO, AX_CARRY_HI = (48, 64)
        OPCODE_BASE = 80
        OUTPUT_LO, OUTPUT_HI, CARRY = (128, 144, 160)
        NIB_A, NIB_B, OP_START = (0, 1, 10)
        RESULT, CARRY_OUT = (100, 101)
        GE_POS, GE_DIM = (8, 160)
        OPC_ADD, OPC_SUB = (25, 26)
        B, S, D = (8, 512, 512)

        def _decode_nibble(x, base):
            return jnp.argmax(x[..., base:base + 16] > 0.5, axis=-1).astype(x.dtype)

        def _pipeline(h, W, b):
            for i in range(3):
                h = jnp.einsum('bspd,od->bspo', h, W[i]) + b[i]
                if i < 2:
                    h = jax.nn.relu(h)
            return h
        x = x_bd
        Bsz, seq, _ = x.shape
        x_ge = jnp.zeros((Bsz, seq, GE_POS, GE_DIM), dtype=x.dtype)
        x_ge = x_ge.at[..., 0, NIB_A].set(_decode_nibble(x, ALU_LO))
        x_ge = x_ge.at[..., 1, NIB_A].set(_decode_nibble(x, ALU_HI))
        x_ge = x_ge.at[..., 0, NIB_B].set(_decode_nibble(x, AX_CARRY_LO))
        x_ge = x_ge.at[..., 1, NIB_B].set(_decode_nibble(x, AX_CARRY_HI))
        x_ge = x_ge.at[..., :, OP_START + OPC_ADD].set(x[..., OPCODE_BASE + OPC_ADD][..., None])
        x_ge = x_ge.at[..., :, OP_START + OPC_SUB].set(x[..., OPCODE_BASE + OPC_SUB][..., None])
        mark = x[..., MARK_AX] > 0.5
        m_add = mark & (x[..., OP_ADD] > 0.5)
        m_sub = mark & ~(x[..., OP_ADD] > 0.5) & (x[..., OP_SUB] > 0.5)
        active = (m_add | m_sub).astype(x.dtype)
        y_add = _pipeline(x_ge, Wa, ba)
        y_sub = _pipeline(x_ge, Ws, bs)
        y = jnp.where(m_add[..., None, None], y_add, jnp.where(m_sub[..., None, None], y_sub, x_ge))
        res_lo = jnp.clip(jnp.round(y[..., 0, RESULT]), 0, 15).astype(jnp.int32)
        res_hi = jnp.clip(jnp.round(y[..., 1, RESULT]), 0, 15).astype(jnp.int32)
        oh_lo = jax.nn.one_hot(res_lo, 16, dtype=x.dtype) * active[..., None]
        oh_hi = jax.nn.one_hot(res_hi, 16, dtype=x.dtype) * active[..., None]
        carry = (jnp.round(y[..., 1, CARRY_OUT]) > 0.5).astype(x.dtype) * active
        out = x
        out = out.at[..., OUTPUT_LO:OUTPUT_LO + 16].add(2.0 * oh_lo)
        out = out.at[..., OUTPUT_HI:OUTPUT_HI + 16].add(2.0 * oh_hi)
        out = out.at[..., CARRY].add(carry)
        return out
    x = x + _L0_gnn_ref(_layernorm(x, axis=-1), src, dst, edge_attr_20, edge_weight, edge_attr_3, L0_gnn_W_in2f_s, L0_gnn_W_in2f_v, L0_gnn_Wf1, L0_gnn_bf1, L0_gnn_Wf2, L0_gnn_bf2, L0_gnn_W1_s, L0_gnn_W1_v, L0_gnn_W2_s, L0_gnn_W2_v)
    x = x + _L0_ffn_ref(_layernorm(x, axis=-1)[None], L0_ffn_Wa, L0_ffn_ba, L0_ffn_Ws, L0_ffn_bs)[0]
    return x

_drawn_inputs = setup_inputs


def setup_inputs(seed=0):
    import zlib

    import numpy as np

    out = dict(_drawn_inputs(seed))
    spreads = {}
    factors = {}
    for name, (base, spread) in spreads.items():
        noise = np.random.default_rng([zlib.crc32(name.encode()), seed]).standard_normal(out[name].shape)
        drawn = base * np.exp(spread * noise) if base else spread * noise
        out[name] = jnp.asarray(drawn.astype(out[name].dtype))
    for name, factor in factors.items():
        out[name] = (out[name] * factor).astype(out[name].dtype)
    return out
```

```python
from contextlib import ExitStack

import numpy as np

import concourse.bass as bass
from concourse import mybir

F32 = mybir.dt.float32
BF16 = mybir.dt.bfloat16
F16 = mybir.dt.float16
I32 = mybir.dt.int32
ALU = mybir.AluOpType
ACT = mybir.ActivationFunctionType
AX = mybir.AxisListType

N = 6250
E = 100000
C = 128
D = 4 * C
NRBF = 20
P = 125
TPG = 4
GE = TPG * P
NG = E // GE
NT = N // P
WIN = 64
MAXP = (N + WIN - 1) // WIN
NP = N + WIN
EPS = 1e-5
Y0 = float(1.0 / np.sqrt(4.0 * np.pi))
Y1 = float(np.sqrt(3.0 / (4.0 * np.pi)))
RC = float(1.0 / np.sqrt(C))
R2F = float(1.0 / np.sqrt(2 * C))
BUCKET = 16
HIGHS = (N - 1) // (4 * BUCKET) + 1
LOWS = 4
SRC, RCUT, UNIT, DST = C, C + 1, C + 2, C + 5
ROW = C + 6


class Steps:

    def __init__(self, sem, ahead=0):
        self.sem, self.ahead = sem, ahead

    def start(self, eng):
        if self.ahead:
            eng.sem_inc(self.sem, self.ahead)

    def wait(self, eng, step):
        eng.wait_ge(self.sem, step + 1 + self.ahead)

    def wait_apart(self, eng, step, passed):
        self.wait(eng, step)
        eng.sem_inc(passed, 1)


class Item:

    def __init__(self, g, it, slot, use, total):
        self.g, self.it, self.slot, self.use, self.total = g, it, slot, use, total
        self.first = isinstance(g, int) and g == 0
        self.fresh = isinstance(g, int) and g < 4

    def later(self, n):
        if isinstance(self.g, int) and self.g + n >= self.total:
            return None
        s = self.slot + n
        return Item(self.g + n, self.it + n, s % 4, self.use + s // 4, self.total)


def item(k, i, s, total):
    return Item(i * 4 + s, k * total + i * 4 + s, s % 4, k * (total // 4) + i + s // 4, total)


def over(eng, k, total, reach, body, lead=1):
    for s in range(lead):
        body(item(k, 0, s, total))
    turns = (total - lead - reach) // 4
    with eng.Fori(0, turns) as i:
        for s in range(4):
            body(item(k, i, s + lead, total))
    for s in range(total - lead - 4 * turns):
        body(item(k, turns, s + lead, total))


def alloc(nc, ctx):
    def sb(name, shape, dt=F32):
        return ctx.enter_context(nc.sbuf_tensor(name, shape, dt))

    def ps(name, shape, dt=F32):
        return ctx.enter_context(nc.psum_tensor(name, shape, dt))

    def sem(name):
        return ctx.enter_context(nc.semaphore(name))

    return sb, ps, sem


def setup_and_nodes(nc, a, keep):
    with ExitStack() as ctx:
        sb, ps, sem = alloc(nc, ctx)
        src = sb("src", [P, E // P], I32)
        dst = sb("dst", [P, E // P], I32)
        bucket = sb("bucket", [P, E // P], I32)
        high = sb("high", [P, E // P], I32)
        low = sb("low", [P, E // P], I32)
        rvec = sb("rvec", [P, 3, E // P])
        rsq = sb("rsq", [P, 3, E // P])
        rnorm = sb("rnorm", [P, E // P])
        rcut = sb("rcut", [P, E // P])
        wf2_raw = sb("wf2_raw", [C, D])
        bf2_raw = sb("bf2_raw", [1, D])
        bf2_split = sb("bf2_split", [1, 3, D], BF16)
        bf2_rest = sb("bf2_rest", [1, 2, D])
        w_in = sb("w_in", [C, 2, C])
        w_in_s = sb("w_in_s", [C, 2, C])
        w1_raw = sb("w1_raw", [C, 4, C])
        w2_raw = sb("w2_raw", [C, 2, C])
        x_t = sb("x_t", [P, 4, D])
        xn = sb("xn", [P, 2, D])
        xT = sb("xT", [C, 2, 4, P])
        rows = sb("rows", [P, 4, D])
        stats = sb("stats", [P, 4, 6])
        mv = sb("mv", [P, 4, 2])
        std = sb("std", [P, 4])
        rstd = sb("rstd", [P, 4])
        eps = sb("eps", [P, 1])
        ident = keep["ident"]
        psT = [ps(f"psT{s}", [C, 4, P]) for s in range(2)]
        psR = [ps(f"psR{s}", [P, 4, C]) for s in range(2)]

        s_edge = sem("s_edge")
        s_w = sem("s_w")
        s_x = [sem(f"s_x{s}") for s in range(4)]
        s_rn = sem("s_rn")
        s_sqrt = sem("s_sqrt")
        s_setup = sem("s_setup")
        s_split = sem("s_split")
        s_bias = sem("s_bias")
        s_ready = sem("s_ready")
        s_v = sem("s_v")
        s_a = sem("s_a")
        s_id = sem("s_id")
        s_gate = sem("n_gate")
        s_win = sem("s_win")
        s_rows_out = [sem(f"s_rows_out{s}") for s in range(4)]
        stat = Steps(sem("stat"))
        aggr = Steps(sem("aggr"))
        var = Steps(sem("var"))
        root = Steps(sem("root"))
        inv = Steps(sem("inv"))
        normed = Steps(sem("normed"), 2)
        turned = Steps(sem("turned"), 2)
        copied = Steps(sem("copied"), 2)
        projected = Steps(sem("projected"), 2)
        drained = Steps(sem("drained"), 2)

        block = ctx.enter_context(nc.Block())

        @block.sync
        def _(sp):
            for s in range(4):
                sp.sem_inc(s_rows_out[s], 16)
                sp.dma_start(x_t[:, s, :], a["x"][s * P:(s + 1) * P, :]).then_inc(s_x[s], 16)
            sp.dma_start(w_in[:, 0, :], a["W_in2f_s"]).then_inc(s_w, 16)
            sp.dma_start(w_in[:, 1, :], a["W_in2f_v"]).then_inc(s_w, 16)
            sp.dma_start(src[:, :], a["src"]).then_inc(s_edge, 16)
            sp.dma_start(dst[:, :], a["dst"]).then_inc(s_edge, 16)
            sp.dma_start(rvec[:, :, :], a["edge_attr_3"]).then_inc(s_edge, 16)
            sp.dma_start(rcut[:, :], a["edge_weight"]).then_inc(s_edge, 16)
            def move(tile):
                nxt = tile.later(4)
                if nxt:
                    normed.wait(sp, tile.it)
                    sp.dma_start(x_t[:, tile.slot, :], a["x"][bass.ds(nxt.g * P, P), :]).then_inc(s_x[tile.slot], 16)
                drained.wait(sp, tile.it)
                sp.dma_start(a["table"][bass.ds(tile.g * P, P), :], rows[:, tile.slot, :]).then_inc(s_rows_out[tile.slot], 16)
            over(sp, 0, NT, 4, move)
            for s in range(4):
                sp.wait_ge(s_rows_out[s], 16 * (NT // 4 + (s < NT % 4)) + 16)
            sp.wait_ge(s_split, 3)
            for r in range(3):
                sp.dma_start(keep["bias3"][r:r + 1, :], bf2_split[:, r, :]).then_inc(s_bias, 16)
            sp.wait_ge(s_bias, 48)

        @block.gpsimd
        def _(pool):
            pool.memset(ident[:, :], 0.0).then_inc(s_id, 1)
            pool.wait_ge(s_id, 1)
            pool.affine_select(out=ident[:, :], in_=ident[:, :], compare_op=ALU.not_equal, fill=1.0, base=0,
                               pattern=[[-1, C]], channel_multiplier=1).then_inc(s_id, 1)
            pool.iota(keep["win_iota_int"][:, :], pattern=[[1, WIN]], base=0, channel_multiplier=0).then_inc(s_win, 1)
            for name, pattern, mult in (("earlier", [[-1, C]], 1), ("lower", [[1, C]], -1)):
                pool.memset(keep[name][:, :], 1.0).then_inc(s_id, 1)
            pool.wait_ge(s_id, 4)
            for name, pattern, mult in (("earlier", [[-1, C]], 1), ("lower", [[1, C]], -1)):
                pool.affine_select(out=keep[name][:, :], in_=keep[name][:, :], compare_op=ALU.is_gt, fill=0.0, base=0,
                                   pattern=pattern, channel_multiplier=mult).then_inc(s_id, 1)
            pool.iota(keep["row_iota_int"][:, :], pattern=[[1, C]], base=0, channel_multiplier=0).then_inc(s_win, 1)
            pool.iota(keep["part_iota_int"][:, :], pattern=[[0, 1]], base=0, channel_multiplier=1).then_inc(s_win, 1)
            pool.iota(keep["ends_iota_int"][:, :, :], pattern=[[GE - 1, 2], [GE, NG]], base=0, channel_multiplier=0).then_inc(s_win, 1)
            pool.dma_start(keep["wf1"][0:NRBF, :], a["Wf1"]).then_inc(s_ready, 16)
            pool.dma_start(keep["wf1"][NRBF:NRBF + 1, :], a["bf1"]).then_inc(s_ready, 16)
            pool.wait_ge(s_ready, 32)

        @block.scalar
        def _(act):
            act.dma_start(wf2_raw[:, :], a["Wf2"][:, 0:D]).then_inc(s_w, 16)
            act.dma_start(bf2_raw[:, :], a["bf2"][:, 0:D]).then_inc(s_w, 16)
            act.dma_start(w1_raw[:, 0:2, :], a["W1_s"].rearrange("(f h) c -> f h c", h=2)).then_inc(s_w, 16)
            act.dma_start(w1_raw[:, 2:4, :], a["W1_v"].rearrange("(f h) c -> f h c", h=2)).then_inc(s_w, 16)
            act.dma_start(w2_raw[:, 0, :], a["W2_s"]).then_inc(s_w, 16)
            act.dma_start(w2_raw[:, 1, :], a["W2_v"]).then_inc(s_w, 16)
            copied.start(act)
            act.wait_ge(s_w, 16 * 8)
            nc.scalar.mul(w_in_s[:, :, :], w_in[:, :, :], RC).then_inc(s_setup, 1)
            for n, first in enumerate((0, 2 * C, 1, 2 * C + 1)):
                nc.scalar.copy(keep["wf2"][:, n, :], wf2_raw[:, first:first + 2 * C - 1:2])
            for n, f in enumerate((Y0 * R2F, Y1 * R2F / float(np.sqrt(3.0)), Y1 * R2F, Y0 * R2F)):
                nc.scalar.mul(keep["w1"][:, n, :], w1_raw[:, n, :], f)
            nc.scalar.mul(keep["w2"][:, :, :], w2_raw[:, :, :], RC)
            act.wait_ge(s_rn, 1)
            nc.scalar.activation(rnorm[:, :], rsq[:, 0, :], ACT.Sqrt).then_inc(s_sqrt, 1)

            def roots(tile):
                var.wait(act, tile.it)
                nc.scalar.activation(std[:, tile.slot:tile.slot + 1], mv[:, tile.slot, 1:2], ACT.Sqrt,
                                     bias=eps[:, 0:1]).then_inc(root.sem, 1)

            def body(tile):
                if tile.later(2):
                    roots(tile.later(2))
                turned.wait(act, tile.it)
                projected.wait(act, tile.it - 2)
                nc.scalar.copy(xT[:, tile.slot % 2, :, :], psT[tile.slot % 2][:, :, :]).then_inc(copied.sem, 1)
            roots(item(0, 0, 0, NT))
            roots(item(0, 0, 1, NT))
            over(act, 0, NT, 4, body)

        @block.tensor
        def _(pe):
            turned.start(pe)
            projected.start(pe)
            pe.wait_ge(s_id, 2)
            pe.wait_ge(s_setup, 1)

            def turn(tile):
                normed.wait(pe, tile.it)
                copied.wait(pe, tile.it - 2)
                for b in range(4):
                    part = xn[:, tile.slot % 2, 0:C] if b == 0 else xn[:, tile.slot % 2, C + b - 1:C + b - 1 + 3 * C - 2:3]
                    last = nc.tensor.transpose(psT[tile.slot % 2][:, b, :], part, ident[0:P, 0:P])
                last.then_inc(turned.sem, 1)

            def body(tile):
                if tile.later(1):
                    turn(tile.later(1))
                copied.wait(pe, tile.it)
                drained.wait(pe, tile.it - 2)
                for b in range(4):
                    last = nc.tensor.matmul(psR[tile.slot % 2][:, b, :], xT[:, tile.slot % 2, b, :],
                                            w_in_s[:, min(b, 1), :], start=True, stop=True)
                last.then_inc(projected.sem, 1)
            turn(item(0, 0, 0, NT))
            over(pe, 0, NT, 4, body)

        @block.vector
        def _(dve):
            chain = [0]

            def link(ins):
                chain[0] += 1
                ins.then_inc(s_v, 1)
                dve.wait_ge(s_v, chain[0])

            normed.start(dve)
            drained.start(dve)
            nc.vector.memset(keep["bias3"][:, :], 0.0)
            nc.vector.memset(keep["ones3"][:, :], 1.0)
            nc.vector.memset(keep["half"][:, :], 0.5)
            link(nc.vector.memset(eps[:, :], EPS))
            dve.wait_ge(s_win, 4)
            nc.vector.tensor_copy(keep["win_iota"][:, :], keep["win_iota_int"][:, :])
            nc.vector.tensor_copy(keep["row_iota"][:, :], keep["row_iota_int"][:, :])
            nc.vector.tensor_copy(keep["part_iota"][:, :], keep["part_iota_int"][:, :])
            nc.vector.tensor_copy(keep["ends_iota"][:, :, :], keep["ends_iota_int"][:, :, :])
            dve.wait_ge(s_id, 2)
            nc.vector.tensor_copy(keep["ident16"][:, :], ident[:, :])
            dve.wait_ge(s_edge, 64)
            nc.vector.tensor_scalar(bucket[:, :], src[:, :], 4, None, ALU.arith_shift_right)
            nc.vector.tensor_scalar(high[:, :], src[:, :], 6, None, ALU.arith_shift_right)
            link(nc.vector.tensor_scalar(low[:, :], src[:, :], 4, 3, ALU.arith_shift_right, ALU.bitwise_and))
            nc.vector.tensor_copy(keep["keys"][:, :, 0], bucket[:, :])
            nc.vector.tensor_copy(keep["keys"][:, :, 1], high[:, :])
            for j in range(LOWS):
                nc.vector.tensor_scalar(keep["low_hot"][:, :, j], low[:, :], float(j), None, ALU.is_equal)
            link(nc.vector.tensor_tensor(rsq[:, :, :], rvec[:, :, :], rvec[:, :, :], ALU.mult))
            link(nc.vector.tensor_tensor(rsq[:, 0, :], rsq[:, 0, :], rsq[:, 1, :], ALU.add))
            nc.vector.tensor_tensor(rsq[:, 0, :], rsq[:, 0, :], rsq[:, 2, :], ALU.add).then_inc(s_rn, 1)
            dve.wait_ge(s_w, 16 * 8)
            raw = bf2_raw[:, :].rearrange("p (w f h) -> p w h f", w=2, h=2)

            def permuted(t):
                return t.rearrange("p (h w f) -> p w h f", h=2, w=2)

            nc.vector.tensor_copy(permuted(bf2_rest[:, 0, :])[:, 0], raw[:, 0])
            link(nc.vector.tensor_copy(permuted(bf2_rest[:, 0, :])[:, 1], raw[:, 1]))
            link(nc.vector.tensor_copy(bf2_split[:, 0, :], bf2_rest[:, 0, :]))
            link(nc.vector.tensor_tensor(bf2_rest[:, 1, :], bf2_rest[:, 0, :], bf2_split[:, 0, :], ALU.subtract))
            link(nc.vector.tensor_copy(bf2_split[:, 1, :], bf2_rest[:, 1, :]))
            link(nc.vector.tensor_tensor(bf2_rest[:, 0, :], bf2_rest[:, 1, :], bf2_split[:, 1, :], ALU.subtract))
            nc.vector.tensor_copy(bf2_split[:, 2, :], bf2_rest[:, 0, :]).then_inc(s_split, 3)
            edge = keep["edge"]
            nc.vector.tensor_copy(edge[:, :, SRC - C], src[:, :])
            nc.vector.tensor_copy(edge[:, :, DST - C], dst[:, :])
            nc.vector.tensor_copy(edge[:, :, RCUT - C], rcut[:, :])
            dve.wait_ge(s_sqrt, 1)
            link(nc.vector.reciprocal(rsq[:, 1, :], rnorm[:, :]))
            for i in range(3):
                nc.vector.tensor_tensor(edge[:, :, UNIT - C + i], rvec[:, i, :], rsq[:, 1, :], ALU.mult)

            def moments(tile):
                dve.wait_ge(s_x[tile.slot], tile.use * 16 + 16)
                nc.vector.bn_stats(stats[:, tile.slot, :], x_t[:, tile.slot, :]).then_inc(stat.sem, 1)
                stat.wait_apart(dve, tile.it, s_gate)
                nc.vector.bn_aggr(mv[:, tile.slot, :], stats[:, tile.slot, :]).then_inc(var.sem, 1)

            def normalise(tile):
                c = tile.slot
                root.wait(dve, tile.it)
                nc.vector.reciprocal(rstd[:, c:c + 1], std[:, c:c + 1]).then_inc(inv.sem, 1)
                inv.wait(dve, tile.it)
                turned.wait(dve, tile.it - 2)
                nc.vector.tensor_scalar(xn[:, c % 2, :], x_t[:, c, :], mv[:, c, 0:1], rstd[:, c:c + 1],
                                        ALU.subtract, ALU.mult).then_inc(normed.sem, 1)

            def body(tile):
                if tile.later(2):
                    moments(tile.later(2))
                if tile.later(1):
                    normalise(tile.later(1))
                projected.wait(dve, tile.it)
                dve.wait_ge(s_rows_out[tile.slot], tile.use * 16 + 16)
                nc.vector.tensor_copy(rows[:, tile.slot, :], psR[tile.slot % 2][:, :, :].rearrange("p b c -> p (b c)")
                                      ).then_inc(drained.sem, 1)
            moments(item(0, 0, 0, NT))
            moments(item(0, 0, 1, NT))
            normalise(item(0, 0, 0, NT))
            over(dve, 0, NT, 4, body)


def count_edges(nc, a, keep):
    with ExitStack() as ctx:
        sb, ps, sem = alloc(nc, ctx)
        high_hot = [sb(f"high_hot{s}", [P, TPG, HIGHS], BF16) for s in range(2)]
        counts = sb("counts", [HIGHS, LOWS, E // P])
        BLK = 25
        NB = E // P // BLK
        of_block = sb("of_block", [HIGHS, LOWS, NB])
        total = sb("total", [HIGHS, LOWS])
        row_total = sb("row_total", [HIGHS, 1])
        start = sb("start", [HIGHS, LOWS])
        end = sb("end", [HIGHS, LOWS])
        ended = sb("ended", [HIGHS, 2, NG])
        ones = sb("ones", [HIGHS, P])
        first_bucket = sb("first_bucket", [1, NG])
        spread = sb("spread", [1, NG])
        widest = sb("widest", [1, 1], I32)
        widest_div = sb("widest_div", [1, 1], I32)
        ps_c = [ps(f"ps_c{s}", [HIGHS, 512]) for s in range(2)]
        ps_start = ps("ps_start", [HIGHS, 512])
        ps_base = ps("ps_base", [P, 512])
        hot_made = Steps(sem("c_hot_made"))
        counted = Steps(sem("counted"), 2)
        stored = Steps(sem("stored"), 2)
        s_gate = sem("c_gate")
        s_v = sem("c_v")
        s_row = sem("c_row")
        s_start = sem("c_start")
        s_ended = sem("c_ended")
        s_base = sem("c_base")
        s_within = sem("c_within")
        s_across = sem("c_across")
        block = ctx.enter_context(nc.Block())

        @block.scalar
        def _(act):
            stored.start(act)

            def store(gr):
                counted.wait_apart(act, gr.it, s_gate)
                nc.scalar.copy(counts[:, :, bass.ds(gr.g * TPG, TPG)],
                               ps_c[gr.slot % 2][:, 0:TPG * LOWS].rearrange("p (t l) -> p l t", l=LOWS)).then_inc(stored.sem, 1)
            over(act, 0, NG, 3, store)

        @block.tensor
        def _(pe):
            counted.start(pe)

            def count(gr):
                hot_made.wait(pe, gr.it)
                stored.wait(pe, gr.it - 2)
                for t in range(TPG):
                    last = nc.tensor.matmul(ps_c[gr.slot % 2][:, t * LOWS:(t + 1) * LOWS], high_hot[gr.slot % 2][:, t, :],
                                            keep["low_hot"][:, bass.ds(gr.g * TPG + t, 1), :].rearrange("p a l -> p (a l)"),
                                            start=True, stop=True)
                last.then_inc(counted.sem, 1)
            over(pe, 0, NG, 3, count)
            pe.wait_ge(s_row, 1)
            nc.tensor.matmul(ps_start[:, 0:1], keep["lower"][0:HIGHS, 0:HIGHS], row_total[:, :], start=True, stop=True).then_inc(s_start, 1)
            pe.wait_ge(s_ended, 1)
            nc.tensor.matmul(ps_base[:, 0:2 * NG], ones[:, :], ended[:, :, :].rearrange("p e g -> p (e g)"),
                             start=True, stop=True).then_inc(s_base, 1)

        @block.vector
        def _(dve):
            chain = [0]

            def link(ins):
                chain[0] += 1
                ins.then_inc(s_v, 1)
                dve.wait_ge(s_v, chain[0])

            nc.vector.memset(ones[:, :], 1.0)
            nc.vector.memset(ended[:, :, :], 0.0)

            def one_hots(gr):
                counted.wait(dve, gr.it - 2)
                nc.vector.tensor_tensor(high_hot[gr.slot % 2][:, :, :],
                                        keep["keys"][:, bass.ds(gr.g * TPG, TPG), 1:2].to_broadcast([P, TPG, HIGHS]),
                                        keep["row_iota"][0:P, 0:HIGHS].unsqueeze(1).to_broadcast([P, TPG, HIGHS]),
                                        ALU.is_equal).then_inc(hot_made.sem, 1)
            over(dve, 0, NG, 3, one_hots)

            stored.wait(dve, NG - 1)
            c4 = counts[:, :, :].rearrange("p l (b j) -> p l b j", j=BLK)
            with dve.Fori(0, BLK - 1) as j:
                nc.vector.tensor_tensor(c4[:, :, :, bass.ds(j + 1, 1)], c4[:, :, :, bass.ds(j + 1, 1)], c4[:, :, :, bass.ds(j, 1)],
                                        ALU.add).then_inc(s_within, 1)
                dve.wait_ge(s_within, j + 1)
            nc.vector.memset(of_block[:, :, 0:1], 0.0).then_inc(s_across, 1)
            dve.wait_ge(s_across, 1)
            with dve.Fori(0, NB - 1) as k:
                nc.vector.tensor_tensor(of_block[:, :, bass.ds(k + 1, 1)], of_block[:, :, bass.ds(k, 1)],
                                        counts[:, :, bass.ds(k * BLK + (BLK - 1), 1)], ALU.add).then_inc(s_across, 1)
                dve.wait_ge(s_across, k + 2)
            link(nc.vector.tensor_tensor(total[:, :], of_block[:, :, NB - 1], c4[:, :, NB - 1, BLK - 1], ALU.add))
            nc.vector.tensor_reduce(row_total[:, :], total[:, :], AX.X, ALU.add).then_inc(s_row, 1)
            dve.wait_ge(s_start, 1)
            link(nc.vector.tensor_copy(start[:, 0:1], ps_start[:, 0:1]))
            for j in range(1, LOWS):
                link(nc.vector.tensor_tensor(start[:, j:j + 1], start[:, j - 1:j], total[:, j - 1:j], ALU.add))
            link(nc.vector.tensor_tensor(end[:, :], start[:, :], total[:, :], ALU.add))
            for j in range(LOWS):
                ins = nc.vector.scalar_tensor_tensor(out=ended[:, :, :], in0=keep["ends_iota"][0:HIGHS, :, :], scalar=end[:, j:j + 1],
                                                     in1=ended[:, :, :], op0=ALU.is_ge, op1=ALU.add)
                if j < LOWS - 1:
                    link(ins)
            ins.then_inc(s_ended, 1)
            link(nc.vector.tensor_tensor(of_block[:, :, :], of_block[:, :, :], start[:, :].unsqueeze(2).to_broadcast([HIGHS, LOWS, NB]), ALU.add))
            p4 = keep["places"][:, :, :].rearrange("p l (b j) -> p l b j", j=BLK)
            nc.vector.tensor_copy(p4[:, :, :, 0], of_block[:, :, :])
            for j in range(LOWS):
                nc.vector.tensor_tensor(p4[:, j, :, 1:BLK], c4[:, j, :, 0:BLK - 1],
                                        of_block[:, j, :].unsqueeze(2).to_broadcast([HIGHS, NB, BLK - 1]), ALU.add)
            dve.wait_ge(s_base, 1)
            nc.vector.tensor_scalar(keep["base_all"][:, :], ps_base[:, 0:NG], float(BUCKET), None, ALU.mult)
            nc.vector.tensor_scalar(keep["base"][:, :], ps_base[0:1, 0:NG], float(BUCKET), None, ALU.mult)
            link(nc.vector.tensor_copy(first_bucket[:, :], ps_base[0:1, 0:NG]))
            link(nc.vector.tensor_tensor(spread[:, :], ps_base[0:1, NG:2 * NG], first_bucket[:, :], ALU.subtract))
            link(nc.vector.tensor_reduce(widest[:, :], spread[:, :], AX.X, ALU.max))
            link(nc.vector.tensor_scalar(widest_div[:, :], widest[:, :], 2, None, ALU.arith_shift_right))
            link(nc.vector.tensor_scalar(keep["passes"][:, :], widest_div[:, :], 1.0, None, ALU.add))
            assert WIN == 4 * BUCKET


def place_edges(nc, a, keep):
    with ExitStack() as ctx:
        sb, ps, sem = alloc(nc, ctx)
        fT = [sb(f"fT{s}", [NRBF + 1, GE]) for s in range(4)]
        size = [sb(f"size{s}", [P, TPG, C]) for s in range(2)]
        keys4 = [sb(f"keys4{s}", [P, TPG, 2], F16) for s in range(4)]
        keyf = [sb(f"keyf{s}", [P, TPG]) for s in range(4)]
        high_T = [sb(f"high_T{s}", [HIGHS, GE]) for s in range(2)]
        same = [sb(f"same{s}", [P, TPG, P], BF16) for s in range(2)]
        rank = [sb(f"rank{s}", [P, TPG]) for s in range(2)]
        picked = [sb(f"picked{s}", [P, TPG, LOWS]) for s in range(2)]
        first_of = [sb(f"first_of{s}", [P, TPG]) for s in range(2)]
        place = [sb(f"place{s}", [P, TPG], I32) for s in range(4)]
        rows = [sb(f"rows{s}", [P, TPG, ROW]) for s in range(4)]
        ps_h = [ps(f"p_h{s}", [P, TPG, C]) for s in range(2)]
        ps_key = [ps(f"ps_key{s}", [C, 512]) for s in range(2)]
        ps_high = [ps(f"ps_high{s}", [C, 512]) for s in range(2)]
        ps_look = ps("ps_look", [P, 512])

        s_f = [sem(f"p_f{s}") for s in range(4)]
        s_out = [sem(f"p_out{s}") for s in range(4)]
        s_gate = sem("p_gate")
        s_ones = sem("p_ones")
        keys_made = Steps(sem("keys_made"), 4)
        keyf_made = Steps(sem("keyf_made"))
        spread_out = Steps(sem("spread_out"), 4)
        high_made = Steps(sem("high_made"), 2)
        size_made = Steps(sem("size_made"), 2)
        exp_made = Steps(sem("exp_made"))
        log_made = Steps(sem("log_made"))
        ranked = Steps(sem("ranked"), 2)
        looked = Steps(sem("looked"), 2)
        picked_made = Steps(sem("picked_made"), 2)
        first_made = Steps(sem("first_made"))
        row_made = Steps(sem("row_made"), 2)

        block = ctx.enter_context(nc.Block())

        @block.sync
        def _(sp):
            sp.wait_ge(s_ones, 1)

            def load(gr):
                spread_out.wait(sp, gr.it - 4)
                sp.dma_start(fT[gr.slot][0:NRBF, :], a["edge_attr_20"][:, bass.ds(gr.g * GE, GE)]).then_inc(s_f[gr.slot], 16)
            over(sp, 0, NG, 2, load)

        @block.gpsimd
        def _(pool):
            def scatter(gr):
                row_made.wait_apart(pool, gr.it, s_gate)
                for t in range(TPG):
                    pool.indirect_dma_start(a["sorted"], bass.IndirectOffsetOnAxis(ap=place[gr.slot][:, t:t + 1], axis=0),
                                            rows[gr.slot][:, t, :], None).then_inc(s_out[gr.slot], 16)
            over(pool, 0, NG, 2, scatter)
            for s in range(4):
                pool.wait_ge(s_out[s], 64 * (NG // 4))

        @block.scalar
        def _(act):
            def body(gr):
                b = size[gr.slot % 2]
                size_made.wait(act, gr.it)
                nc.scalar.activation(b[:, :, :], b[:, :, :], ACT.Exp, scale=-1.0).then_inc(exp_made.sem, 1)
                exp_made.wait(act, gr.it)
                nc.scalar.activation(b[:, :, :], b[:, :, :], ACT.Ln, scale=0.5, bias=keep["half"][0:P, 0:1]).then_inc(log_made.sem, 1)
            over(act, 0, NG, 2, body)

        @block.tensor
        def _(pe):
            spread_out.start(pe)
            looked.start(pe)

            def spread(gr):
                pe.wait_ge(s_f[gr.slot], gr.use * 16 + 16)
                row_made.wait(pe, gr.it - 2)
                for t in range(TPG):
                    nc.tensor.matmul(ps_h[gr.slot % 2][:, t, :], fT[gr.slot][:, t * P:(t + 1) * P], keep["wf1"][:, :],
                                     start=True, stop=True)
                keys_made.wait(pe, gr.it)
                ranked.wait(pe, gr.it - 2)
                high_made.wait(pe, gr.it - 2)
                for i, out in enumerate((ps_key[gr.slot % 2], ps_high[gr.slot % 2])):
                    for t in range(TPG):
                        last = nc.tensor.matmul(out[:, t * P:(t + 1) * P], keys4[gr.slot][:, t, i:i + 1].to_broadcast([P, C]),
                                                keep["ident16"][0:P, 0:P], start=True, stop=True)
                last.then_inc(spread_out.sem, 1)

            def look_up(gr):
                high_made.wait(pe, gr.it)
                picked_made.wait(pe, gr.it - 1)
                for t in range(TPG):
                    last = nc.tensor.matmul(ps_look[:, t * LOWS:(t + 1) * LOWS], high_T[gr.slot % 2][:, t * P:(t + 1) * P],
                                            keep["places"][:, :, bass.ds(gr.g * TPG + t, 1)].rearrange("p l a -> p (l a)"),
                                            start=True, stop=True)
                last.then_inc(looked.sem, 1)

            spread(item(0, 0, 0, NG))

            def body(gr):
                if gr.later(1):
                    spread(gr.later(1))
                look_up(gr)
            over(pe, 0, NG, 2, body)

        @block.vector
        def _(dve):
            for st in (keys_made, high_made, size_made, ranked, picked_made, row_made):
                st.start(dve)
            for s in range(4):
                ins = nc.vector.memset(fT[s][:, :], 1.0)
            ins.then_inc(s_ones, 1)

            def keys(gr):
                spread_out.wait(dve, gr.it - 4)
                nc.vector.tensor_copy(keyf[gr.slot][:, :], keep["keys"][:, bass.ds(gr.g * TPG, TPG), 0]).then_inc(keyf_made.sem, 1)
                nc.vector.tensor_copy(keys4[gr.slot][:, :, :], keep["keys"][:, bass.ds(gr.g * TPG, TPG), :]).then_inc(keys_made.sem, 1)

            def from_psum(gr):
                c = gr.slot % 2
                spread_out.wait(dve, gr.it)
                looked.wait(dve, gr.it - 2)
                nc.vector.tensor_scalar(high_T[c][:, :], ps_high[c][0:HIGHS, 0:GE], keep["part_iota"][0:HIGHS, 0:1], None,
                                        ALU.is_equal).then_inc(high_made.sem, 1)
                nc.vector.tensor_scalar(size[c][:, :, :].bitcast(I32), ps_h[c][:, :, :].bitcast(I32), 0x7FFFFFFF, None,
                                        ALU.bitwise_and).then_inc(size_made.sem, 1)

            def rank_and_place(gr):
                c = gr.slot % 2
                keyf_made.wait(dve, gr.it)
                for t in range(TPG):
                    ins = nc.vector.scalar_tensor_tensor(out=same[c][:, t, :], in0=ps_key[c][0:P, t * P:(t + 1) * P],
                                                         scalar=keyf[gr.slot][:, t:t + 1], in1=keep["earlier"][0:P, 0:P],
                                                         op0=ALU.is_equal, op1=ALU.mult, accum_out=rank[c][:, t:t + 1])
                ins.then_inc(ranked.sem, 1)
                looked.wait(dve, gr.it)
                nc.vector.tensor_tensor(picked[c][:, :, :], ps_look[:, 0:TPG * LOWS].rearrange("p (t l) -> p t l", l=LOWS),
                                        keep["low_hot"][:, bass.ds(gr.g * TPG, TPG), :], ALU.mult).then_inc(picked_made.sem, 1)
                picked_made.wait(dve, gr.it)
                nc.vector.tensor_reduce(first_of[c][:, :], picked[c][:, :, :], AX.X, ALU.add).then_inc(first_made.sem, 1)
                if not gr.fresh:
                    dve.wait_ge(s_out[gr.slot], gr.use * 64)
                log_made.wait(dve, gr.it)
                r = rows[gr.slot]
                nc.vector.scalar_tensor_tensor(out=r[:, :, 0:C], in0=ps_h[c][:, :, :], scalar=0.0, in1=size[c][:, :, :],
                                               op0=ALU.max, op1=ALU.add)
                nc.vector.tensor_copy(r[:, :, C:ROW], keep["edge"][:, bass.ds(gr.g * TPG, TPG), :])
                ranked.wait(dve, gr.it)
                first_made.wait(dve, gr.it)
                nc.vector.tensor_tensor(place[gr.slot][:, :], first_of[c][:, :], rank[c][:, :], ALU.add).then_inc(row_made.sem, 1)

            keys(item(0, 0, 0, NG))
            keys(item(0, 0, 1, NG))
            from_psum(item(0, 0, 0, NG))

            def body(gr):
                if gr.later(2):
                    keys(gr.later(2))
                if gr.later(1):
                    from_psum(gr.later(1))
                rank_and_place(gr)
            over(dve, 0, NG, 2, body, lead=4)


def sum_edges(nc, a, keep):
    with ExitStack() as ctx:
        sb, ps, sem = alloc(nc, ctx)
        rows = [sb(f"erows{s}", [P, TPG, ROW]) for s in range(4)]
        hT = [sb(f"hT{s}", [C, GE]) for s in range(2)]
        dst4 = [sb(f"dst4{s}", [P, TPG], I32) for s in range(4)]
        got = [sb(f"got{s}", [P, TPG, 4, C]) for s in range(4)]
        col = [sb(f"col{s}", [P, TPG]) for s in range(2)]
        cut_unit = [sb(f"cut_unit{s}", [P, TPG, 3]) for s in range(2)]
        vu = sb("vu", [P, TPG, 3, C])
        dot2 = sb("dot2", [P, TPG, C])
        dot = [sb(f"dot{s}", [P, TPG, C]) for s in range(2)]
        hot = [sb(f"hot{s}", [P, TPG, 4, WIN]) for s in range(2)]
        msg = [sb(f"msg{s}", [P, 6, C]) for s in range(2)]
        sums = [sb(f"sums{s}", [C, 8, WIN]) for s in range(2)]
        ps_h = ps("ps_h", [C, 512])
        ps_w = [ps(f"ps_w{t}", [P, 4, C]) for t in range(TPG)]
        ps_sum = [ps(f"ps_sum{s}", [C, 8, WIN]) for s in range(2)]
        ps_out = ps("ps_out", [C, 8, WIN])

        s_rows = [sem(f"s_rows{s}") for s in range(4)]
        s_got = [sem(f"s_got{s}") for s in range(4)]
        s_gate = sem("s_gate")
        s_base = sem("s_base")
        s_zero = sem("s_zero")
        s_zero_v = sem("s_zero_v")
        h_turned = Steps(sem("h_turned"), 2)
        h_done = Steps(sem("h_done"), 2)
        w_made = Steps(sem("w_made"), 8)
        num_made = Steps(sem("num_made"), 4)
        dst_made = Steps(sem("dst_made"))
        hot_made = Steps(sem("hot_made"), 4)
        vu_made = Steps(sem("vu_made"), 4)
        dot_half = Steps(sem("dot_half"))
        dot_made = Steps(sem("dot_made"), 1)
        msg_made = Steps(sem("msg_made"), 16)
        sum_made = Steps(sem("sum_made"), 16)
        sum_copied = Steps(sem("sum_copied"), 2)
        out_made = Steps(sem("out_made"), 2)
        added = Steps(sem("added"), 1)

        block = ctx.enter_context(nc.Block())

        def passes(eng):
            return eng.Fori(0, eng.value_load(keep["passes"][0:1, 0:1], min_val=1, max_val=MAXP))

        @block.sync
        def _(sp):
            by_group = a["sorted"].rearrange("(g p t) r -> p g (t r)", p=P, t=TPG)
            with passes(sp) as k:
                def load(gr):
                    sum_made.wait(sp, (gr.it - 4) * TPG + 3)
                    sp.dma_start(rows[gr.slot][:, :, :].rearrange("p t r -> p (t r)"),
                                 by_group[:, bass.ds(gr.g, 1), :].rearrange("p a r -> p (a r)")).then_inc(s_rows[gr.slot], 16)
                over(sp, k, NG, 3, load)

        @block.gpsimd
        def _(pool):
            nc.gpsimd.memset(keep["node_sums"][:, 2:4, :], 0.0).then_inc(s_zero, 1)
            pool.wait_ge(s_zero, 1)
            dot_made.start(pool)

            def wait(steps, step):
                steps.wait_apart(pool, step, s_gate)

            with passes(pool) as k:
                def gather(gr):
                    wait(msg_made, (gr.it - 4) * TPG + 3)
                    pool.wait_ge(s_rows[gr.slot], gr.use * 16 + 16)
                    pool.sem_inc(s_gate, 1)
                    pool.tensor_copy(dst4[gr.slot][:, :], rows[gr.slot][:, :, DST]).then_inc(dst_made.sem, 1)
                    wait(dst_made, gr.it)
                    for t in range(TPG):
                        pool.indirect_dma_start(got[gr.slot][:, t, :, :].rearrange("p b c -> p (b c)"), None, a["table"],
                                                bass.IndirectOffsetOnAxis(ap=dst4[gr.slot][:, t:t + 1], axis=0)
                                                ).then_inc(s_got[gr.slot], 16)

                def dots(gr):
                    wait(vu_made, gr.it)
                    wait(msg_made, (gr.it - 2) * TPG + 3)
                    pool.tensor_tensor(dot2[:, :, :], vu[:, :, 0, :], vu[:, :, 1, :], ALU.add).then_inc(dot_half.sem, 1)
                    wait(dot_half, gr.it)
                    pool.tensor_tensor(dot[gr.slot % 2][:, :, :], dot2[:, :, :], vu[:, :, 2, :], ALU.add).then_inc(dot_made.sem, 1)

                g0 = item(k, 0, 0, NG)
                gather(g0)
                gather(g0.later(1))
                dots(g0)

                def body(gr):
                    if gr.later(2):
                        gather(gr.later(2))
                    if gr.later(1):
                        dots(gr.later(1))
                over(pool, k, NG, 2, body)

        @block.scalar
        def _(act):
            vu_made.start(act)
            h_done.start(act)
            sum_copied.start(act)
            with passes(act) as k:
                def copy_hidden(gr):
                    h_turned.wait(act, gr.it)
                    w_made.wait(act, (gr.it - 2) * TPG + 3)
                    nc.scalar.copy(hT[gr.slot % 2][:, :], ps_h[:, 0:GE]).then_inc(h_done.sem, 1)

                def turn(gr):
                    act.wait_ge(s_got[gr.slot], gr.use * 64 + 64)
                    act.wait_ge(s_rows[gr.slot], gr.use * 16 + 16)
                    dot_made.wait(act, gr.it - 1)
                    for t in range(TPG):
                        for i in range(3):
                            last = nc.scalar.activation(vu[:, t, i, :], got[gr.slot][:, t, 1 + i, :], ACT.Copy,
                                                        scale=rows[gr.slot][:, t, UNIT + i:UNIT + i + 1])
                    last.then_inc(vu_made.sem, 1)

                def copy_sums(gr, it):
                    sum_made.wait(act, it * TPG + 3)
                    out_made.wait(act, it - 2)
                    nc.scalar.copy(sums[gr][:, :, :], ps_sum[gr][:, :, :]).then_inc(sum_copied.sem, 1)

                g0 = item(k, 0, 0, NG)
                turn(g0)
                copy_hidden(g0)

                def body(gr):
                    nxt = gr.later(1)
                    if nxt:
                        copy_hidden(nxt)
                    if not gr.first:
                        copy_sums((gr.slot + 1) % 2, gr.it - 1)
                    if nxt:
                        turn(nxt)
                over(act, k, NG, 2, body)
                copy_sums(1, k * NG + NG - 1)

        @block.tensor
        def _(pe):
            h_turned.start(pe)
            w_made.start(pe)
            sum_made.start(pe)
            out_made.start(pe)
            with passes(pe) as k:
                def hidden(gr):
                    pe.wait_ge(s_rows[gr.slot], gr.use * 16 + 16)
                    h_done.wait(pe, gr.it - 1)
                    for t in range(TPG):
                        last = nc.tensor.transpose(ps_h[:, t * P:(t + 1) * P], rows[gr.slot][:, t, 0:C], keep["ident"][0:P, 0:P])
                    last.then_inc(h_turned.sem, 1)

                def weights(gr, t):
                    if t == 0:
                        h_done.wait(pe, gr.it)
                    msg_made.wait(pe, (gr.it - 1) * TPG + t)
                    w = ps_w[t][:, :, :].rearrange("p b c -> p (b c)")
                    nc.tensor.matmul(w, keep["ones3"][:, :], keep["bias3"][:, :], start=True, stop=False)
                    nc.tensor.matmul(w, hT[gr.slot % 2][:, t * P:(t + 1) * P],
                                     keep["wf2"][:, :, :].rearrange("p b c -> p (b c)"),
                                     start=False, stop=True).then_inc(w_made.sem, 1)

                def add_up(slot, it, t):
                    msg_made.wait(pe, it * TPG + t)
                    if t == 0:
                        hot_made.wait(pe, it)
                        sum_copied.wait(pe, it - 2)
                    m, o, acc = msg[t % 2], hot[slot % 2], ps_sum[slot % 2]
                    for b, cols, hots in ((0, slice(0, 1), slice(0, 1)), (1, slice(2, 5), slice(1, 4)),
                                          (2, slice(1, 2), slice(0, 1)), (3, slice(5, 6), slice(0, 1)),
                                          (4, slice(6, 7), slice(0, 1)), (5, slice(7, 8), slice(0, 1))):
                        last = nc.tensor.matmul(acc[:, cols, :].rearrange("p b w -> p (b w)"), m[:, b, :],
                                                o[:, t, hots, :].rearrange("p b w -> p (b w)"),
                                                start=(t == 0 and b == 0), stop=(t == TPG - 1 and b == 5),
                                                skip_group_check=True)
                    last.then_inc(sum_made.sem, 1)

                def through_w1(slot, it):
                    sum_copied.wait(pe, it)
                    added.wait(pe, it - 1)
                    s = sums[slot % 2]
                    w1 = keep["w1"]
                    nc.tensor.matmul(ps_out[:, 0, :], w1[:, 0, :], s[:, 0, :], start=True, stop=False, skip_group_check=True)
                    nc.tensor.matmul(ps_out[:, 0, :], w1[:, 1, :], s[:, 1, :], start=False, stop=False, skip_group_check=True)
                    v = ps_out[:, 1:4, :].rearrange("p b w -> p (b w)")
                    nc.tensor.matmul(v, w1[:, 2, :], s[:, 2:5, :].rearrange("p b w -> p (b w)"), start=False, stop=False,
                                     skip_group_check=True)
                    nc.tensor.matmul(v, w1[:, 3, :], s[:, 5:8, :].rearrange("p b w -> p (b w)"), start=False, stop=True,
                                     skip_group_check=True).then_inc(out_made.sem, 1)

                hidden(item(k, 0, 0, NG))

                def body(gr):
                    for t in range(TPG):
                        weights(gr, t)
                        if t >= 2:
                            add_up(gr.slot, gr.it, t - 2)
                        elif not gr.first:
                            add_up(gr.slot + 1, gr.it - 1, t + 2)
                        if t == 0 and gr.later(1):
                            hidden(gr.later(1))
                        if t == 2 and not gr.first:
                            through_w1(gr.slot + 1, gr.it - 1)
                over(pe, k, NG, 2, body)
                for t in (2, 3):
                    add_up(1, k * NG + NG - 1, t)
                through_w1(1, k * NG + NG - 1)

        @block.vector
        def _(dve):
            for s in (num_made, hot_made, msg_made, added):
                s.start(dve)
            nc.vector.memset(keep["node_sums"][:, 0:2, :], 0.0).then_inc(s_zero_v, 1)
            dve.wait_ge(s_zero_v, 1)
            dve.wait_ge(s_zero, 1)
            with passes(dve) as k:
                def numbers(gr):
                    dve.wait_ge(s_rows[gr.slot], gr.use * 16 + 16)
                    c, r = gr.slot % 2, rows[gr.slot]
                    nc.vector.tensor_tensor(cut_unit[c][:, :, :], r[:, :, UNIT:UNIT + 3], r[:, :, RCUT:RCUT + 1].to_broadcast([P, TPG, 3]),
                                            ALU.mult)
                    nc.vector.tensor_tensor(col[c][:, :], r[:, :, SRC], keep["base_all"][:, bass.ds(gr.g, 1)].to_broadcast([P, TPG]),
                                            ALU.subtract).then_inc(num_made.sem, 1)

                def one_hots(gr, tiles):
                    num_made.wait(dve, gr.it)
                    sum_made.wait(dve, (gr.it - 2) * TPG + 3)
                    c, r = gr.slot % 2, rows[gr.slot]
                    for t in tiles:
                        for i in range(4):
                            by = r[:, t, RCUT:RCUT + 1] if i == 0 else cut_unit[c][:, t, i - 1:i]
                            last = nc.vector.tensor_scalar(hot[c][:, t, i, :], keep["win_iota"][:, :], col[c][:, t:t + 1], by,
                                                           ALU.is_equal, ALU.mult)
                    if TPG - 1 in tiles:
                        last.then_inc(hot_made.sem, 1)

                def messages(gr, t):
                    if t == 0:
                        dve.wait_ge(s_got[gr.slot], gr.use * 64 + 64)
                        dot_made.wait(dve, gr.it)
                    w_made.wait(dve, gr.it * TPG + t)
                    sum_made.wait(dve, gr.it * TPG + (t - 2))
                    m, w, x = msg[t % 2], ps_w[t], got[gr.slot]
                    nc.vector.tensor_tensor(m[:, 0:2, :], w[:, 0:2, :], x[:, t, 0:1, :].to_broadcast([P, 2, C]), ALU.mult)
                    nc.vector.tensor_tensor(m[:, 2, :], w[:, 2, :], dot[gr.slot % 2][:, t, :], ALU.mult)
                    nc.vector.tensor_tensor(m[:, 3:6, :], w[:, 3:4, :].to_broadcast([P, 3, C]), x[:, t, 1:4, :],
                                            ALU.mult).then_inc(msg_made.sem, 1)

                def add_window(g, it):
                    start = dve.value_load(keep["base"][0:1, bass.ds(g, 1)] if not isinstance(g, int) else keep["base"][0:1, g:g + 1],
                                           min_val=0, max_val=N)
                    out_made.wait(dve, it)
                    added.wait(dve, it - 1)
                    part = keep["node_sums"][:, :, bass.ds(start, WIN)]
                    nc.vector.tensor_tensor(part, ps_out[:, 0:4, :], part, ALU.add).then_inc(added.sem, 1)

                g0 = item(k, 0, 0, NG)
                numbers(g0)
                one_hots(g0, range(TPG))

                def body(gr):
                    for t in range(TPG):
                        messages(gr, t)
                        if gr.later(1):
                            if t == 0:
                                numbers(gr.later(1))
                            else:
                                one_hots(gr.later(1), ((0,), (1, 2), (3,))[t - 1])
                    if not gr.first:
                        add_window(gr.g - 1, gr.it - 1)
                over(dve, k, NG, 2, body)
                add_window(NG - 1, k * NG + NG - 1)
                e, b = keep["base_all"], keep["base"]
                nc.vector.tensor_scalar(e[:, :], e[:, :], float(WIN), None, ALU.add).then_inc(s_base, 1)
                nc.vector.tensor_scalar(b[:, :], b[:, :], float(WIN), float(N), ALU.add, ALU.min).then_inc(s_base, 1)
                dve.wait_ge(s_base, k * 2 + 2)


NCH = 25
TPC = NT // NCH
NC_ = TPC * P
GE_DIM = 160
HI = GE_DIM - C
RESULT, CARRY_OUT = 100, 101
FLAG = 105
FLAG_IN = 35
NIB = 16
OUTPUT = 128
N_WEIGHTS = 36
NF = 5


def finish(nc, a, keep):
    with ExitStack() as ctx:
        sb, ps, sem = alloc(nc, ctx)
        x = sb("x", [P, 4, TPC, D])
        xl = sb("xl", [P, 4, TPC, D])
        st = [sb(f"st{s}", [C, 4, NC_]) for s in range(2)]
        soft = [sb(f"fsoft{s}", [C, NC_]) for s in range(2)]
        stats = sb("fstats", [P, 4, TPC, 6])
        mv = sb("fmv", [P, 4, TPC, 2])
        std = sb("fstd", [P, 4, TPC])
        rstd = sb("frstd", [P, 4, TPC])
        eps = sb("feps", [P, 1])
        weight16 = sb("weight16", [P, 4, 16])
        iota16 = sb("iota16", [P, 16])
        iota16_int = sb("iota16_int", [P, 16], I32)
        score = sb("score", [P, 2, TPC, 4, 16])
        best = sb("best", [P, 2, TPC, 4])
        any16 = sb("any16", [P, 2, TPC, 4])
        flags = sb("flags", [P, 2, TPC, 3])
        feats = sb("feats", [P, 2, TPC, 2, NF])
        mask = sb("mask", [P, 4, TPC, 4])
        fT = sb("ffT", [C, 2, 4 * P])
        h1 = sb("h1", [C, 3, 4 * P])
        h2 = sb("h2", [C, 2, 3, 4 * P])
        b3 = sb("b3", [P, 4])
        y = sb("y", [P, TPC, 2, 4])
        yy = sb("yy", [P, TPC, 2, 4])
        ym = sb("ym", [P, TPC, 2, 2])
        yr = sb("yr", [P, TPC, 2])
        yc = sb("yc", [P, TPC])
        hot = sb("fhot", [P, TPC, 2, 16])
        l1 = sb("l1", [C, 3, C])
        l2 = sb("l2", [C, 7, C])
        l3 = sb("l3", [C, 3, 4])
        b2 = sb("b2", [C, 3])
        ps_x = [ps(f"ps_x{t}", [P, 4, C]) for t in range(TPC)]
        ps_f = ps("ps_f", [C, 512])
        ps_l = [ps(f"ps_l{b}", [C, 512]) for b in range(3)]
        ps_y = ps("ps_y", [P, 512])
        y_ps = ps_y[:, 0:TPC * 2 * 4].rearrange("p (t q o) -> p t q o", q=2, o=4)

        s_zero = sem("f_zero")
        s_w = sem("f_w")
        s_iota = sem("f_iota")
        s_gate = sem("f_gate")
        s_gate_v = sem("f_gate_v")
        s_v = sem("f_v")
        s_x = [sem(f"f_x{s}") for s in range(4)]
        s_out = [sem(f"f_out{s}") for s in range(4)]
        sums_here = Steps(sem("sums_here"))
        act_abs = Steps(sem("act_abs"))
        act_exp = Steps(sem("act_exp"))
        act_ln = Steps(sem("act_ln"))
        soft_done = Steps(sem("soft_done"), 2)
        w2_done = Steps(sem("w2_done"), 2)
        x1_done = Steps(sem("x1_done"), 1)
        stat = Steps(sem("f_stat"))
        var = Steps(sem("f_var"))
        root = Steps(sem("f_root"))
        inv = Steps(sem("f_inv"))
        normed = Steps(sem("f_normed"))
        feats_done = Steps(sem("feats_done"))
        turned = Steps(sem("f_turned"), 2)
        f_copied = Steps(sem("f_copied"), 1)
        l1_done = Steps(sem("l1_done"), 2)
        r1_done = Steps(sem("r1_done"), 1)
        l2_done = Steps(sem("l2_done"), 3)
        r2_done = Steps(sem("r2_done"), 3)
        l3_done = Steps(sem("l3_done"), 2)
        y_read = Steps(sem("y_read"), 1)
        added = Steps(sem("f_added"))
        done = Steps(sem("f_done"))
        dve_front = Steps(sem("dve_front"))
        dve_tail = Steps(sem("dve_tail"))

        s_hot = sem("f_hot")
        s_hot_scaled = sem("f_hot_scaled")

        block = ctx.enter_context(nc.Block())
        rows_of = a["x"].rearrange("(n t p) d -> n p t d", t=TPC, p=P)
        out_rows = a["out"].rearrange("(n t p) d -> n p t d", t=TPC, p=P)

        @block.sync
        def _(sp):
            for s in range(4):
                sp.dma_start(x[:, s, :, :], rows_of[s]).then_inc(s_x[s], 16)
            sp.wait_ge(s_zero, 1)
            wa, ws = a["Wa"], a["Ws"]
            weights = []
            for w, col in ((wa, (0, 0, C, 2, 0)), (ws, (1, 1, C, 2, HI))):
                first_block, _, _, rest_block, at = col
                for r, rows in ((0, slice(0, 2)), (2, slice(FLAG_IN, FLAG_IN + 2))):
                    weights.append((l1[r:r + 2, first_block, :], w[0, rows, 0:C]))
                    weights.append((l1[r:r + 2, rest_block, at:at + HI], w[0, rows, C:GE_DIM]))
            for m, bias in ((0, a["ba"]), (1, a["bs"])):
                weights.append((l1[4:5, m, :], bias[0:1, 0:C]))
                weights.append((l1[4:5, 2, m * HI:(m + 1) * HI], bias[0:1, C:GE_DIM]))
                weights.append((b2[:, m:m + 1], bias[1:2, 0:C].rearrange("a c -> c a")))
                weights.append((b2[m * HI:(m + 1) * HI, 2:3], bias[1:2, C:GE_DIM].rearrange("a c -> c a")))
                for o, q in ((0, RESULT), (2, CARRY_OUT)):
                    weights.append((b3[:, o + m:o + m + 1], bias[2:3, q:q + 1].to_broadcast([P, 1])))
            for m, w in ((0, wa), (1, ws)):
                weights.append((l2[:, 2 * m, :], w[1, 0:C, 0:C]))
                weights.append((l2[m * HI:(m + 1) * HI, 2 * m + 1, :], w[1, C:GE_DIM, 0:C]))
                weights.append((l2[:, 4 + m, m * HI:(m + 1) * HI], w[1, 0:C, C:GE_DIM]))
                weights.append((l2[m * HI:(m + 1) * HI, 6, m * HI:(m + 1) * HI], w[1, C:GE_DIM, C:GE_DIM]))
                for o, q in ((0, RESULT), (2, CARRY_OUT)):
                    weights.append((l3[:, m, o + m:o + m + 1], w[2, 0:C, q:q + 1]))
                    weights.append((l3[m * HI:(m + 1) * HI, 2, o + m:o + m + 1], w[2, C:GE_DIM, q:q + 1]))
            with nc.allow_non_contiguous_dma(reason="a few columns of the weights"):
                for dst, src in weights:
                    sp.dma_start(dst, src).then_inc(s_w, 16)
            assert len(weights) == N_WEIGHTS

            def move(ch):
                done.wait(sp, ch.it)
                sp.dma_start(out_rows[bass.ds(ch.g, 1)].rearrange("a p t d -> (a p) t d") if not isinstance(ch.g, int) else out_rows[ch.g],
                             x[:, ch.slot, :, :]).then_inc(s_out[ch.slot], 16)
                nxt = ch.later(4)
                if nxt:
                    sp.wait_ge(s_out[ch.slot], ch.use * 16 + 16)
                    sp.dma_start(x[:, ch.slot, :, :],
                                 rows_of[bass.ds(nxt.g, 1)].rearrange("a p t d -> (a p) t d") if not isinstance(nxt.g, int) else rows_of[nxt.g]
                                 ).then_inc(s_x[ch.slot], 16)
            over(sp, 0, NCH, 4, move)
            for s in range(4):
                sp.wait_ge(s_out[s], 16 * (NCH // 4 + (s < NCH % 4)))

        @block.gpsimd
        def _(pool):
            def wait(steps, step):
                steps.wait_apart(pool, step, s_gate)

            pool.iota(iota16_int[:, :], pattern=[[1, 16]], base=0, channel_multiplier=0).then_inc(s_iota, 1)

            def fetch(ch):
                wait(w2_done, ch.it - 2)
                pool.tensor_copy(st[ch.slot % 2][:, :, :], keep["node_sums"][:, :, bass.ds(ch.g * NC_, NC_)]).then_inc(sums_here.sem, 1)

            def body(ch):
                if ch.later(3):
                    fetch(ch.later(3))
                wait(normed, ch.it)
                wait(feats_done, ch.it)
                pool.tensor_tensor(x[:, ch.slot, :, :], x[:, ch.slot, :, :], xl[:, ch.slot, :, :], ALU.add).then_inc(added.sem, 1)
            for s in range(3):
                fetch(item(0, 0, s, NCH))
            over(pool, 0, NCH, 4, body)

        @block.scalar
        def _(act):
            f_copied.start(act)
            r1_done.start(act)
            r2_done.start(act)

            def softplus(ch):
                c = ch.slot % 2
                sums_here.wait(act, ch.it)
                soft_done.wait(act, ch.it - 2)
                nc.scalar.activation(soft[c][:, :], st[c][:, 0, :], ACT.Abs).then_inc(act_abs.sem, 1)
                act_abs.wait(act, ch.it)
                nc.scalar.activation(soft[c][:, :], soft[c][:, :], ACT.Exp, scale=-1.0).then_inc(act_exp.sem, 1)
                act_exp.wait(act, ch.it)
                nc.scalar.activation(soft[c][:, :], soft[c][:, :], ACT.Ln, scale=0.5, bias=keep["half"][:, 0:1]).then_inc(act_ln.sem, 1)

            def roots(ch):
                var.wait(act, ch.it)
                nc.scalar.activation(std[:, ch.slot, :], mv[:, ch.slot, :, 1], ACT.Sqrt, bias=eps[:, 0:1]).then_inc(root.sem, 1)

            def copy_feats(ch):
                turned.wait(act, ch.it)
                l1_done.wait(act, ch.it - 2)
                nc.scalar.copy(fT[0:NF, ch.slot % 2, :], ps_f[0:NF, 0:4 * P]).then_inc(f_copied.sem, 1)

            def relus(ch):
                l1_done.wait(act, ch.it)
                l2_done.wait(act, ch.it * 3 - 1)
                for b in range(3):
                    last = nc.scalar.activation(h1[:, b, :], ps_l[b][:, 0:4 * P], ACT.Relu)
                last.then_inc(r1_done.sem, 1)
                l3_done.wait(act, ch.it - 2)
                for b in range(3):
                    l2_done.wait(act, ch.it * 3 + b)
                    nc.scalar.activation(h2[:, ch.slot % 2, b, :], ps_l[b][:, 0:4 * P], ACT.Relu, bias=b2[:, b:b + 1]).then_inc(r2_done.sem, 1)

            softplus(item(0, 0, 0, NCH))
            roots(item(0, 0, 0, NCH))
            softplus(item(0, 0, 1, NCH))
            copy_feats(item(0, 0, 0, NCH))

            def body(ch):
                if ch.later(1):
                    roots(ch.later(1))
                if ch.later(2):
                    softplus(ch.later(2))
                relus(ch)
                if ch.later(1):
                    copy_feats(ch.later(1))
            act.wait_ge(s_w, 16 * N_WEIGHTS)
            over(act, 0, NCH, 4, body)

        @block.tensor
        def _(pe):
            for s in (w2_done, turned, l1_done, l2_done, l3_done):
                s.start(pe)

            def through_w2(ch):
                soft_done.wait(pe, ch.it)
                x1_done.wait(pe, ch.it - 1)
                for t in range(TPC):
                    for b in range(4):
                        last = nc.tensor.matmul(ps_x[t][:, b, :], st[ch.slot % 2][:, b, t * P:(t + 1) * P],
                                                keep["w2"][:, min(b, 1), :], start=True, stop=True)
                last.then_inc(w2_done.sem, 1)

            def turn(ch):
                feats_done.wait(pe, ch.it)
                f_copied.wait(pe, ch.it - 1)
                for q in range(2):
                    for t in range(TPC):
                        last = nc.tensor.transpose(ps_f[0:NF, (q * TPC + t) * P:(q * TPC + t + 1) * P],
                                                   feats[:, ch.slot % 2, t, q, :], keep["ident"][0:P, 0:P])
                last.then_inc(turned.sem, 1)

            def layer1(ch):
                f_copied.wait(pe, ch.it)
                r2_done.wait(pe, ch.it * 3 - 1)
                for b in range(3):
                    last = nc.tensor.matmul(ps_l[b][:, 0:4 * P], l1[:, b, :], fT[:, ch.slot % 2, :], start=True, stop=True)
                last.then_inc(l1_done.sem, 1)

            def layer2(ch):
                r1_done.wait(pe, ch.it)
                for b, ins in enumerate((((0, 0), (2, 1)), ((1, 2), (2, 3)), ((0, 4), (1, 5), (2, 6)))):
                    for n, (i, w) in enumerate(ins):
                        last = nc.tensor.matmul(ps_l[b][:, 0:4 * P], l2[:, w, :], h1[:, i, :],
                                                start=(n == 0), stop=(n == len(ins) - 1))
                    last.then_inc(l2_done.sem, 1)

            def layer3(ch):
                r2_done.wait(pe, ch.it * 3 + 2)
                y_read.wait(pe, ch.it - 1)
                for q in range(2):
                    for t in range(TPC):
                        for b in range(3):
                            at = (q * TPC + t) * P
                            last = nc.tensor.matmul(y_ps[:, t, q, :], h2[:, ch.slot % 2, b, at:at + P], l3[:, b, :],
                                                    start=(b == 0), stop=(b == 2))
                last.then_inc(l3_done.sem, 1)

            def before(ch):
                s = (ch.slot - 1) % 4
                return Item(None, ch.it - 1, s, None, NCH)

            def body(ch):
                layer1(ch)
                if ch.later(1):
                    turn(ch.later(1))
                if not ch.first:
                    layer3(before(ch))
                layer2(ch)
                if ch.later(2):
                    through_w2(ch.later(2))

            pe.wait_ge(s_w, 16 * N_WEIGHTS)
            pe.wait_ge(s_zero, 2)
            through_w2(item(0, 0, 0, NCH))
            through_w2(item(0, 0, 1, NCH))
            turn(item(0, 0, 0, NCH))
            over(pe, 0, NCH, 4, body)
            layer3(item(0, NCH // 4, 0, NCH))

        @block.vector
        def _(dve):
            for s in (soft_done, x1_done, y_read):
                s.start(dve)
            for t in (l1, l2, l3):
                nc.vector.memset(t[:, :, :], 0.0)
            nc.vector.memset(b2[:, :], 0.0).then_inc(s_zero, 1)
            nc.vector.memset(feats[:, :, :, :, :], 1.0)
            nc.vector.memset(eps[:, :], EPS)
            nc.vector.memset(fT[:, :, :], 0.0).then_inc(s_zero, 1)
            dve.wait_ge(s_zero, 2)
            dve.wait_ge(s_iota, 1)
            nc.vector.tensor_copy(iota16[:, :], iota16_int[:, :]).then_inc(s_v, 1)
            dve.wait_ge(s_v, 1)
            nc.vector.tensor_scalar(weight16[:, :, :], iota16[:, :].unsqueeze(1).to_broadcast([P, 4, 16]), -1.0, 16.0,
                                    ALU.mult, ALU.add).then_inc(s_v, 1)
            dve.wait_ge(s_v, 2)
            dve.wait_ge(s_w, 16 * N_WEIGHTS)
            FRONT, TAIL = 4, 5

            def finish_soft(ch):
                c = ch.slot % 2
                act_ln.wait(dve, ch.it)
                nc.vector.scalar_tensor_tensor(out=st[c][:, 0, :], in0=st[c][:, 0, :], scalar=0.0, in1=soft[c][:, :],
                                               op0=ALU.max, op1=ALU.add).then_inc(soft_done.sem, 1)

            def add_rows(ch):
                c = ch.slot
                dve.wait_ge(s_x[c], ch.use * 16 + 16)
                w2_done.wait(dve, ch.it)
                for t in range(TPC):
                    nc.vector.tensor_tensor(x[:, c, t, 0:C], x[:, c, t, 0:C], ps_x[t][:, 0, :], ALU.add)
                    v = x[:, c, t, C:D].rearrange("p (d i) -> p d i", i=3)
                    last = nc.vector.tensor_tensor(v, v, ps_x[t][:, 1:4, :].rearrange("p i d -> p d i"), ALU.add)
                last.then_inc(x1_done.sem, 1)
                x1_done.wait(dve, ch.it)
                for t in range(TPC):
                    last = nc.vector.bn_stats(stats[:, c, t, :], x[:, c, t, :])
                last.then_inc(stat.sem, 1)
                stat.wait_apart(dve, ch.it, s_gate_v)
                for t in range(TPC):
                    last = nc.vector.bn_aggr(mv[:, c, t, :], stats[:, c, t, :])
                last.then_inc(var.sem, 1)

            def decode(ch):
                c, h = ch.slot, ch.slot % 2
                root.wait(dve, ch.it)
                nc.vector.reciprocal(rstd[:, c, :], std[:, c, :]).then_inc(inv.sem, 1)
                inv.wait(dve, ch.it)
                for t in range(TPC):
                    last = nc.vector.tensor_scalar(xl[:, c, t, :], x[:, c, t, :], mv[:, c, t, 0:1], rstd[:, c, t:t + 1],
                                                   ALU.subtract, ALU.mult)
                last.then_inc(normed.sem, 1)
                normed.wait(dve, ch.it)
                nc.vector.scalar_tensor_tensor(out=score[:, h].rearrange("p t n j -> p t (n j)"), in0=xl[:, c, :, NIB:NIB + 64],
                                               scalar=0.5, in1=weight16[:, :, :].rearrange("p n j -> p (n j)").unsqueeze(1).to_broadcast([P, TPC, 64]),
                                               op0=ALU.is_gt, op1=ALU.mult)
                nc.vector.tensor_scalar(flags[:, h], xl[:, c, :, 0:3], 0.5, None, ALU.is_gt)
                turned.wait(dve, ch.it - 2)
                nc.vector.tensor_copy(feats[:, h, :, :, 2:4], xl[:, c, :, FLAG:FLAG + 2].unsqueeze(2).to_broadcast([P, TPC, 2, 2])
                                      ).then_inc(dve_front.sem, 1)
                dve_front.wait(dve, ch.it * FRONT)
                nc.vector.tensor_reduce(best[:, h], score[:, h], AX.X, ALU.max)
                nc.vector.tensor_tensor(mask[:, c, :, 0], flags[:, h, :, 0], flags[:, h, :, 1], ALU.mult).then_inc(dve_front.sem, 1)
                dve_front.wait(dve, ch.it * FRONT + 1)
                nc.vector.tensor_scalar(any16[:, h], best[:, h], 0.0, 16.0, ALU.is_gt, ALU.mult)
                nc.vector.tensor_tensor(mask[:, c, :, 3], flags[:, h, :, 0], mask[:, c, :, 0], ALU.subtract).then_inc(dve_front.sem, 1)
                dve_front.wait(dve, ch.it * FRONT + 2)
                nc.vector.tensor_tensor(mask[:, c, :, 1], mask[:, c, :, 3], flags[:, h, :, 2], ALU.mult).then_inc(dve_front.sem, 1)
                dve_front.wait(dve, ch.it * FRONT + 3)
                nc.vector.tensor_tensor(mask[:, c, :, 2], mask[:, c, :, 0], mask[:, c, :, 1], ALU.add)
                nc.vector.tensor_tensor(feats[:, h, :, :, 0:2].rearrange("p t q f -> p t f q"),
                                        any16[:, h].rearrange("p t (f q) -> p t f q", q=2),
                                        best[:, h].rearrange("p t (f q) -> p t f q", q=2), ALU.subtract).then_inc(feats_done.sem, 1)

            def outputs(it, c):
                def step(n, ins):
                    ins.then_inc(dve_tail.sem, 1)
                    dve_tail.wait(dve, it * TAIL + n)

                l3_done.wait(dve, it)
                nc.vector.tensor_tensor(y[:, :, :, :], y_ps, b3[:, :].unsqueeze(1).unsqueeze(1).to_broadcast([P, TPC, 2, 4]),
                                        ALU.add).then_inc(y_read.sem, 1)
                y_read.wait(dve, it)
                for t in range(TPC):
                    ins = nc.vector.tensor_tensor(yy[:, t].rearrange("p q (o m) -> p q o m", m=2), y[:, t].rearrange("p q (o m) -> p q o m", m=2),
                                                  mask[:, c, t, 0:2].unsqueeze(1).unsqueeze(1).to_broadcast([P, 2, 2, 2]), ALU.mult)
                step(0, ins)
                step(1, nc.vector.tensor_tensor(ym[:, :, :, :], yy[:, :, :, 0:4:2], yy[:, :, :, 1:4:2], ALU.add))
                nc.vector.tensor_scalar(yr[:, :, :], ym[:, :, :, 0], 0.0, 15.0, ALU.max, ALU.min)
                step(2, nc.vector.scalar_tensor_tensor(out=yc[:, :], in0=ym[:, :, 1, 1], scalar=0.5, in1=mask[:, c, :, 2],
                                                       op0=ALU.is_gt, op1=ALU.mult))
                nc.vector.tensor_scalar(yr[:, :, :], yr[:, :, :], float(2 ** 23), None, ALU.add).then_inc(dve_tail.sem, 1)
                dve_tail.wait(dve, it * TAIL + 3)
                nc.vector.tensor_scalar(yr[:, :, :], yr[:, :, :], float(2 ** 23), None, ALU.subtract).then_inc(dve_tail.sem, 1)
                dve_tail.wait(dve, it * TAIL + 4)
                nc.vector.tensor_tensor(hot[:, :, :, :], iota16[:, :].unsqueeze(1).unsqueeze(1).to_broadcast([P, TPC, 2, 16]),
                                        yr[:, :, :].unsqueeze(3).to_broadcast([P, TPC, 2, 16]), ALU.is_equal).then_inc(hot_made.sem, 1)
                hot_made.wait(dve, it)
                for t in range(TPC):
                    ins = nc.vector.tensor_scalar(hot[:, t, :, :], hot[:, t, :, :], mask[:, c, t, 2:3], 2.0, ALU.mult, ALU.mult)
                ins.then_inc(hot_scaled.sem, 1)
                hot_scaled.wait(dve, it)
                added.wait(dve, it)
                o = x[:, c, :, OUTPUT:OUTPUT + 32]
                nc.vector.tensor_tensor(o, o, hot[:, :, :, :].rearrange("p t q j -> p t (q j)"), ALU.add)
                o = x[:, c, :, OUTPUT + 32]
                nc.vector.tensor_tensor(o, o, yc[:, :], ALU.add).then_inc(done.sem, 1)

            hot_made = Steps(s_hot)
            hot_scaled = Steps(s_hot_scaled)
            c0, c1, c2 = (item(0, 0, s, NCH) for s in range(3))
            finish_soft(c0)
            add_rows(c0)
            finish_soft(c1)
            decode(c0)

            def body(ch):
                if ch.later(1):
                    add_rows(ch.later(1))
                if ch.later(2):
                    finish_soft(ch.later(2))
                if ch.later(1):
                    decode(ch.later(1))
                if not ch.first:
                    outputs(ch.it - 1, (ch.slot - 1) % 4)
            over(dve, 0, NCH, 4, body)
            outputs(NCH - 1, (NCH - 1) % 4)


def build(nc, a):
    with ExitStack() as ctx:
        sb, ps, sem = alloc(nc, ctx)
        keep = {
            "ident": sb("ident", [C, C]),
            "w2": sb("w2", [C, 2, C]),
            "half": sb("half", [C, 1]),
        }
        keep.update({
            "base": sb("base", [1, NG], I32),
            "base_all": sb("base_all", [P, NG]),
            "passes": sb("passes", [1, 1], I32),
            "win_iota_int": sb("win_iota_int", [P, WIN], I32),
            "win_iota": sb("win_iota", [P, WIN]),
            "wf2": sb("wf2", [C, 4, C]),
            "bias3": sb("bias3", [C, D], BF16),
            "ones3": sb("ones3", [C, P], BF16),
            "w1": sb("w1", [C, 4, C]),
        })
        with ExitStack() as place_ctx:
            sb, ps, sem = alloc(nc, place_ctx)
            keep.update({
                "edge": sb("edge", [P, E // P, ROW - C]),
                "keys": sb("keys", [P, E // P, 2], F16),
                "low_hot": sb("low_hot", [P, E // P, LOWS], BF16),
                "places": sb("places", [HIGHS, LOWS, E // P]),
                "wf1": sb("wf1", [NRBF + 1, C]),
                "ident16": sb("ident16", [C, C], F16),
                "earlier": sb("earlier", [C, C]),
                "lower": sb("lower", [C, C]),
                "row_iota_int": sb("row_iota_int", [C, C], I32),
                "row_iota": sb("row_iota", [C, C], F16),
                "part_iota_int": sb("part_iota_int", [C, 1], I32),
                "part_iota": sb("part_iota", [C, 1]),
                "ends_iota_int": sb("ends_iota_int", [C, 2, NG], I32),
                "ends_iota": sb("ends_iota", [C, 2, NG]),
            })
            setup_and_nodes(nc, a, keep)
            count_edges(nc, a, keep)
            place_edges(nc, a, keep)
        sb, ps, sem = alloc(nc, ctx)
        keep["node_sums"] = ctx.enter_context(nc.sbuf_tensor("node_sums", [C, 4, NP], F32))
        sum_edges(nc, a, keep)
        finish(nc, a, keep)


def kernel(**inputs):
    import concourse.bacc as bacc
    from concourse.bass_utils import run_bass_kernel_spmd

    def tiles(v):
        v = np.asarray(v).reshape(E // P, P, -1)
        return np.ascontiguousarray(v.transpose(1, 2, 0).squeeze(1) if v.shape[2] == 1 else v.transpose(1, 2, 0))

    given = {
        "x": np.asarray(inputs["x"]),
        "src": tiles(inputs["src"]),
        "dst": tiles(inputs["dst"]),
        "edge_attr_20": np.ascontiguousarray(np.asarray(inputs["edge_attr_20"]).T),
        "edge_attr_3": tiles(inputs["edge_attr_3"]),
        "edge_weight": tiles(inputs["edge_weight"]),
    }
    for name in ("W_in2f_s", "W_in2f_v", "Wf1", "Wf2", "W1_s", "W1_v", "W2_s", "W2_v"):
        given[name] = np.asarray(inputs["L0_gnn_" + name])
    for name in ("bf1", "bf2"):
        given[name] = np.asarray(inputs["L0_gnn_" + name]).reshape(1, -1)
    for name in ("Wa", "Ws"):
        given[name] = np.ascontiguousarray(np.asarray(inputs["L0_ffn_" + name]).transpose(0, 2, 1))
    for name in ("ba", "bs"):
        given[name] = np.asarray(inputs["L0_ffn_" + name])

    nc = bacc.Bacc("TRN2", target_bir_lowering=False, num_devices=1)
    arrays, a = {}, {}
    for name, value in given.items():
        arrays["in_" + name] = value
        a[name] = nc.dram_tensor("in_" + name, value.shape, mybir.dt.from_np(value.dtype), kind="ExternalInput").ap()
    a["out"] = nc.dram_tensor("out", (N, D), F32, kind="ExternalOutput").ap()
    a["table"] = nc.dram_tensor("table", (N, D), F32, kind="Internal").ap()
    a["sorted"] = nc.dram_tensor("sorted", (E, ROW), F32, kind="Internal").ap()
    build(nc, a)
    r = run_bass_kernel_spmd(nc, [arrays], core_ids=[0])
    return r.results[0]["out"]
```

```python
from contextlib import ExitStack

import numpy as np

import concourse.bass as bass
from concourse import mybir

F32 = mybir.dt.float32
BF16 = mybir.dt.bfloat16
F16 = mybir.dt.float16
I32 = mybir.dt.int32
ALU = mybir.AluOpType
ACT = mybir.ActivationFunctionType
AX = mybir.AxisListType

N = 6250
E = 100000
C = 128
D = 4 * C
NRBF = 20
P = 125
TPG = 4
GE = TPG * P
NG = E // GE
NT = N // P
WIN = 48
MAXP = (N + WIN - 1) // WIN
NP = N + WIN
EPS = 1e-5
Y0 = float(1.0 / np.sqrt(4.0 * np.pi))
Y1 = float(np.sqrt(3.0 / (4.0 * np.pi)))
RC = float(1.0 / np.sqrt(C))
R2F = float(1.0 / np.sqrt(2 * C))
BUCKET_BITS = 3
BUCKET = 1 << BUCKET_BITS
LOW_BITS = 3
LOWS = 1 << LOW_BITS
HIGHS = ((N - 1) >> (BUCKET_BITS + LOW_BITS)) + 1
SRC, RCUT, UNIT, DST = C, C + 1, C + 2, C + 5
ROW = C + 6


class Steps:

    def __init__(self, sem, ahead=0):
        self.sem, self.ahead = sem, ahead

    def start(self, eng):
        if self.ahead:
            eng.sem_inc(self.sem, self.ahead)

    def wait(self, eng, step):
        eng.wait_ge(self.sem, step + 1 + self.ahead)

    def wait_apart(self, eng, step, passed):
        self.wait(eng, step)
        eng.sem_inc(passed, 1)


class Item:

    def __init__(self, g, it, slot, use, total):
        self.g, self.it, self.slot, self.use, self.total = g, it, slot, use, total
        self.first = isinstance(g, int) and g == 0
        self.fresh = isinstance(g, int) and g < 4

    def later(self, n):
        if isinstance(self.g, int) and self.g + n >= self.total:
            return None
        s = self.slot + n
        return Item(self.g + n, self.it + n, s % 4, self.use + s // 4, self.total)


def item(k, i, s, total):
    return Item(i * 4 + s, k * total + i * 4 + s, s % 4, k * (total // 4) + i + s // 4, total)


def over(eng, k, total, reach, body, lead=1):
    for s in range(lead):
        body(item(k, 0, s, total))
    turns = (total - lead - reach) // 4
    with eng.Fori(0, turns) as i:
        for s in range(4):
            body(item(k, i, s + lead, total))
    for s in range(total - lead - 4 * turns):
        body(item(k, turns, s + lead, total))


def alloc(nc, ctx):
    def sb(name, shape, dt=F32):
        return ctx.enter_context(nc.sbuf_tensor(name, shape, dt))

    def ps(name, shape, dt=F32):
        return ctx.enter_context(nc.psum_tensor(name, shape, dt))

    def sem(name):
        return ctx.enter_context(nc.semaphore(name))

    return sb, ps, sem


def setup_and_nodes(nc, a, keep):
    with ExitStack() as ctx:
        sb, ps, sem = alloc(nc, ctx)
        src = sb("src", [P, E // P], I32)
        dst = sb("dst", [P, E // P], I32)
        bucket = sb("bucket", [P, E // P], I32)
        high = sb("high", [P, E // P], I32)
        low = sb("low", [P, E // P], I32)
        rvec = sb("rvec", [P, 3, E // P])
        rsq = sb("rsq", [P, 3, E // P])
        rnorm = sb("rnorm", [P, E // P])
        rcut = sb("rcut", [P, E // P])
        wf2_raw = sb("wf2_raw", [C, D])
        bf2_raw = sb("bf2_raw", [1, D])
        bf2_split = sb("bf2_split", [1, 3, D], BF16)
        bf2_rest = sb("bf2_rest", [1, 2, D])
        w_in = sb("w_in", [C, 2, C])
        w_in_s = sb("w_in_s", [C, 2, C])
        w1_raw = sb("w1_raw", [C, 4, C])
        w2_raw = sb("w2_raw", [C, 2, C])
        x_t = sb("x_t", [P, 4, D])
        xn = sb("xn", [P, 4, D])
        xT = sb("xT", [C, 4, 4, P])
        rows = sb("rows", [P, 4, D])
        stats = sb("stats", [P, 4, 6])
        mv = sb("mv", [P, 4, 2])
        std = sb("std", [P, 4])
        rstd = sb("rstd", [P, 4])
        eps = sb("eps", [P, 1])
        ident = keep["ident"]
        psT = [ps(f"psT{s}", [C, 4, P]) for s in range(4)]
        psR = [ps(f"psR{s}", [P, 4, C]) for s in range(4)]

        s_edge = sem("s_edge")
        s_w = sem("s_w")
        s_x = [sem(f"s_x{s}") for s in range(4)]
        s_rn = sem("s_rn")
        s_sqrt = sem("s_sqrt")
        s_setup = sem("s_setup")
        s_split = sem("s_split")
        s_bias = sem("s_bias")
        s_ready = sem("s_ready")
        s_v = sem("s_v")
        s_a = sem("s_a")
        s_id = sem("s_id")
        s_gate = sem("n_gate")
        s_win = sem("s_win")
        s_rows_out = [sem(f"s_rows_out{s}") for s in range(4)]
        stat = Steps(sem("stat"))
        aggr = Steps(sem("aggr"))
        var = Steps(sem("var"))
        root = Steps(sem("root"))
        inv = Steps(sem("inv"))
        normed = Steps(sem("normed"), 4)
        turned = Steps(sem("turned"), 4)
        copied = Steps(sem("copied"), 4)
        projected = Steps(sem("projected"), 4)
        drained = Steps(sem("drained"), 4)

        block = ctx.enter_context(nc.Block())

        @block.sync
        def _(sp):
            for s in range(4):
                sp.sem_inc(s_rows_out[s], 16)
                sp.dma_start(x_t[:, s, :], a["x"][s * P:(s + 1) * P, :]).then_inc(s_x[s], 16)
            sp.dma_start(w_in[:, 0, :], a["W_in2f_s"]).then_inc(s_w, 16)
            sp.dma_start(w_in[:, 1, :], a["W_in2f_v"]).then_inc(s_w, 16)
            sp.dma_start(src[:, :], a["src"]).then_inc(s_edge, 16)
            sp.dma_start(dst[:, :], a["dst"]).then_inc(s_edge, 16)
            sp.dma_start(rvec[:, :, :], a["edge_attr_3"]).then_inc(s_edge, 16)
            sp.dma_start(rcut[:, :], a["edge_weight"]).then_inc(s_edge, 16)
            def move(tile):
                nxt = tile.later(4)
                if nxt:
                    normed.wait(sp, tile.it)
                    sp.dma_start(x_t[:, tile.slot, :], a["x"][bass.ds(nxt.g * P, P), :]).then_inc(s_x[tile.slot], 16)
                drained.wait(sp, tile.it)
                sp.dma_start(a["table"][bass.ds(tile.g * P, P), :], rows[:, tile.slot, :]).then_inc(s_rows_out[tile.slot], 16)
            over(sp, 0, NT, 4, move)
            for s in range(4):
                sp.wait_ge(s_rows_out[s], 16 * (NT // 4 + (s < NT % 4)) + 16)
            sp.wait_ge(s_split, 3)
            for r in range(3):
                sp.dma_start(keep["bias3"][r:r + 1, :], bf2_split[:, r, :]).then_inc(s_bias, 16)
            sp.wait_ge(s_bias, 48)

        @block.gpsimd
        def _(pool):
            pool.memset(ident[:, :], 0.0).then_inc(s_id, 1)
            pool.wait_ge(s_id, 1)
            pool.affine_select(out=ident[:, :], in_=ident[:, :], compare_op=ALU.not_equal, fill=1.0, base=0,
                               pattern=[[-1, C]], channel_multiplier=1).then_inc(s_id, 1)
            pool.iota(keep["win_iota_int"][:, :], pattern=[[1, WIN]], base=0, channel_multiplier=0).then_inc(s_win, 1)
            for name, pattern, mult in (("earlier", [[-1, C]], 1), ("lower", [[1, C]], -1)):
                pool.memset(keep[name][:, :], 1.0).then_inc(s_id, 1)
            pool.wait_ge(s_id, 4)
            for name, pattern, mult in (("earlier", [[-1, C]], 1), ("lower", [[1, C]], -1)):
                pool.affine_select(out=keep[name][:, :], in_=keep[name][:, :], compare_op=ALU.is_gt, fill=0.0, base=0,
                                   pattern=pattern, channel_multiplier=mult).then_inc(s_id, 1)
            pool.iota(keep["row_iota_int"][:, :], pattern=[[1, C]], base=0, channel_multiplier=0).then_inc(s_win, 1)
            pool.iota(keep["part_iota_int"][:, :], pattern=[[0, 1]], base=0, channel_multiplier=1).then_inc(s_win, 1)
            pool.iota(keep["ends_iota_int"][:, :, :], pattern=[[GE - 1, 2], [GE, NG]], base=0, channel_multiplier=0).then_inc(s_win, 1)
            pool.dma_start(keep["wf1"][0:NRBF, :], a["Wf1"]).then_inc(s_ready, 16)
            pool.dma_start(keep["wf1"][NRBF:NRBF + 1, :], a["bf1"]).then_inc(s_ready, 16)
            pool.wait_ge(s_ready, 32)

        @block.scalar
        def _(act):
            act.dma_start(wf2_raw[:, :], a["Wf2"][:, 0:D]).then_inc(s_w, 16)
            act.dma_start(bf2_raw[:, :], a["bf2"][:, 0:D]).then_inc(s_w, 16)
            act.dma_start(w1_raw[:, 0:2, :], a["W1_s"].rearrange("(f h) c -> f h c", h=2)).then_inc(s_w, 16)
            act.dma_start(w1_raw[:, 2:4, :], a["W1_v"].rearrange("(f h) c -> f h c", h=2)).then_inc(s_w, 16)
            act.dma_start(w2_raw[:, 0, :], a["W2_s"]).then_inc(s_w, 16)
            act.dma_start(w2_raw[:, 1, :], a["W2_v"]).then_inc(s_w, 16)
            copied.start(act)
            act.wait_ge(s_w, 16 * 8)
            nc.scalar.mul(w_in_s[:, :, :], w_in[:, :, :], RC).then_inc(s_setup, 1)
            for n, first in enumerate((0, 2 * C, 1, 2 * C + 1)):
                nc.scalar.copy(keep["wf2"][:, n, :], wf2_raw[:, first:first + 2 * C - 1:2])
            for n, f in enumerate((Y0 * R2F, Y1 * R2F / float(np.sqrt(3.0)), Y1 * R2F, Y0 * R2F)):
                nc.scalar.mul(keep["w1"][:, n, :], w1_raw[:, n, :], f)
            nc.scalar.mul(keep["w2"][:, :, :], w2_raw[:, :, :], RC)
            act.wait_ge(s_rn, 1)
            nc.scalar.activation(rnorm[:, :], rsq[:, 0, :], ACT.Sqrt).then_inc(s_sqrt, 1)

            def roots(tile):
                var.wait(act, tile.it)
                nc.scalar.activation(std[:, tile.slot:tile.slot + 1], mv[:, tile.slot, 1:2], ACT.Sqrt,
                                     bias=eps[:, 0:1]).then_inc(root.sem, 1)

            def body(tile):
                if tile.later(3):
                    roots(tile.later(3))
                if tile.later(1):
                    copy(tile.later(1))

            def copy(tile):
                turned.wait(act, tile.it)
                projected.wait(act, tile.it - 4)
                nc.scalar.copy(xT[:, tile.slot, :, :], psT[tile.slot][:, :, :]).then_inc(copied.sem, 1)
            for s in range(3):
                roots(item(0, 0, s, NT))
            copy(item(0, 0, 0, NT))
            over(act, 0, NT, 4, body)

        @block.tensor
        def _(pe):
            turned.start(pe)
            projected.start(pe)
            pe.wait_ge(s_id, 2)
            pe.wait_ge(s_setup, 1)

            def turn(tile):
                normed.wait(pe, tile.it)
                copied.wait(pe, tile.it - 4)
                for b in range(4):
                    part = xn[:, tile.slot, 0:C] if b == 0 else xn[:, tile.slot, C + b - 1:C + b - 1 + 3 * C - 2:3]
                    last = nc.tensor.transpose(psT[tile.slot][:, b, :], part, ident[0:P, 0:P])
                last.then_inc(turned.sem, 1)

            def body(tile):
                if tile.later(1):
                    turn(tile.later(1))
                copied.wait(pe, tile.it)
                drained.wait(pe, tile.it - 4)
                for b in range(4):
                    last = nc.tensor.matmul(psR[tile.slot][:, b, :], xT[:, tile.slot, b, :],
                                            w_in_s[:, min(b, 1), :], start=True, stop=True)
                last.then_inc(projected.sem, 1)
            turn(item(0, 0, 0, NT))
            over(pe, 0, NT, 4, body)

        @block.vector
        def _(dve):
            chain = [0]

            def link(ins):
                chain[0] += 1
                ins.then_inc(s_v, 1)
                dve.wait_ge(s_v, chain[0])

            normed.start(dve)
            drained.start(dve)
            nc.vector.memset(keep["bias3"][:, :], 0.0)
            nc.vector.memset(keep["ones3"][:, :], 1.0)
            nc.vector.memset(keep["half"][:, :], 0.5)
            link(nc.vector.memset(eps[:, :], EPS))
            dve.wait_ge(s_win, 4)
            nc.vector.tensor_copy(keep["win_iota"][:, :], keep["win_iota_int"][:, :])
            nc.vector.tensor_copy(keep["row_iota"][:, :], keep["row_iota_int"][:, :])
            nc.vector.tensor_copy(keep["part_iota"][:, :], keep["part_iota_int"][:, :])
            nc.vector.tensor_copy(keep["ends_iota"][:, :, :], keep["ends_iota_int"][:, :, :])
            dve.wait_ge(s_id, 2)
            nc.vector.tensor_copy(keep["ident16"][:, :], ident[:, :])
            dve.wait_ge(s_edge, 64)
            nc.vector.tensor_scalar(bucket[:, :], src[:, :], BUCKET_BITS, None, ALU.arith_shift_right)
            nc.vector.tensor_scalar(high[:, :], src[:, :], BUCKET_BITS + LOW_BITS, None, ALU.arith_shift_right)
            link(nc.vector.tensor_scalar(low[:, :], src[:, :], BUCKET_BITS, LOWS - 1, ALU.arith_shift_right, ALU.bitwise_and))
            nc.vector.tensor_copy(keep["keys"][:, :, 0], bucket[:, :])
            nc.vector.tensor_copy(keep["keys"][:, :, 1], high[:, :])
            for j in range(LOWS):
                nc.vector.tensor_scalar(keep["low_hot"][:, :, j], low[:, :], float(j), None, ALU.is_equal)
            link(nc.vector.tensor_tensor(rsq[:, :, :], rvec[:, :, :], rvec[:, :, :], ALU.mult))
            link(nc.vector.tensor_tensor(rsq[:, 0, :], rsq[:, 0, :], rsq[:, 1, :], ALU.add))
            nc.vector.tensor_tensor(rsq[:, 0, :], rsq[:, 0, :], rsq[:, 2, :], ALU.add).then_inc(s_rn, 1)
            dve.wait_ge(s_w, 16 * 8)
            raw = bf2_raw[:, :].rearrange("p (w f h) -> p w h f", w=2, h=2)

            def permuted(t):
                return t.rearrange("p (h w f) -> p w h f", h=2, w=2)

            nc.vector.tensor_copy(permuted(bf2_rest[:, 0, :])[:, 0], raw[:, 0])
            link(nc.vector.tensor_copy(permuted(bf2_rest[:, 0, :])[:, 1], raw[:, 1]))
            link(nc.vector.tensor_copy(bf2_split[:, 0, :], bf2_rest[:, 0, :]))
            link(nc.vector.tensor_tensor(bf2_rest[:, 1, :], bf2_rest[:, 0, :], bf2_split[:, 0, :], ALU.subtract))
            link(nc.vector.tensor_copy(bf2_split[:, 1, :], bf2_rest[:, 1, :]))
            link(nc.vector.tensor_tensor(bf2_rest[:, 0, :], bf2_rest[:, 1, :], bf2_split[:, 1, :], ALU.subtract))
            nc.vector.tensor_copy(bf2_split[:, 2, :], bf2_rest[:, 0, :]).then_inc(s_split, 3)
            edge = keep["edge"]
            nc.vector.tensor_copy(edge[:, :, SRC - C], src[:, :])
            nc.vector.tensor_copy(edge[:, :, DST - C], dst[:, :])
            nc.vector.tensor_copy(edge[:, :, RCUT - C], rcut[:, :])
            dve.wait_ge(s_sqrt, 1)
            link(nc.vector.reciprocal(rsq[:, 1, :], rnorm[:, :]))
            for i in range(3):
                nc.vector.tensor_tensor(edge[:, :, UNIT - C + i], rvec[:, i, :], rsq[:, 1, :], ALU.mult)

            def moments(tile):
                dve.wait_ge(s_x[tile.slot], tile.use * 16 + 16)
                nc.vector.bn_stats(stats[:, tile.slot, :], x_t[:, tile.slot, :]).then_inc(stat.sem, 1)
                stat.wait_apart(dve, tile.it, s_gate)
                nc.vector.bn_aggr(mv[:, tile.slot, :], stats[:, tile.slot, :]).then_inc(var.sem, 1)

            def normalise(tile):
                c = tile.slot
                root.wait(dve, tile.it)
                nc.vector.reciprocal(rstd[:, c:c + 1], std[:, c:c + 1]).then_inc(inv.sem, 1)
                inv.wait(dve, tile.it)
                turned.wait(dve, tile.it - 4)
                nc.vector.tensor_scalar(xn[:, c, :], x_t[:, c, :], mv[:, c, 0:1], rstd[:, c:c + 1],
                                        ALU.subtract, ALU.mult).then_inc(normed.sem, 1)

            def body(tile):
                if tile.later(3):
                    moments(tile.later(3))
                if tile.later(2):
                    normalise(tile.later(2))
                projected.wait(dve, tile.it)
                dve.wait_ge(s_rows_out[tile.slot], tile.use * 16 + 16)
                nc.vector.tensor_copy(rows[:, tile.slot, :], psR[tile.slot][:, :, :].rearrange("p b c -> p (b c)")
                                      ).then_inc(drained.sem, 1)
            for s in range(3):
                moments(item(0, 0, s, NT))
            for s in range(2):
                normalise(item(0, 0, s, NT))
            over(dve, 0, NT, 4, body)


def count_edges(nc, a, keep):
    with ExitStack() as ctx:
        sb, ps, sem = alloc(nc, ctx)
        high_hot = [sb(f"high_hot{s}", [P, TPG, HIGHS], BF16) for s in range(4)]
        counts = sb("counts", [HIGHS, LOWS, E // P])
        BLK = 25
        NB = E // P // BLK
        of_block = sb("of_block", [HIGHS, LOWS, NB])
        total = sb("total", [HIGHS, LOWS])
        row_total = sb("row_total", [HIGHS, 1])
        start = sb("start", [HIGHS, LOWS])
        end = sb("end", [HIGHS, LOWS])
        ended = sb("ended", [HIGHS, 2, NG])
        ones = sb("ones", [HIGHS, P])
        first_bucket = sb("first_bucket", [1, NG])
        spread = sb("spread", [1, NG])
        widest = sb("widest", [1, 1], I32)
        scaled = sb("scaled", [1, 1], I32)
        widest_div = sb("widest_div", [1, 1], I32)
        ps_c = [ps(f"ps_c{s}", [HIGHS, 512]) for s in range(4)]
        ps_start = ps("ps_start", [HIGHS, 512])
        ps_base = ps("ps_base", [P, 512])
        hot_made = Steps(sem("c_hot_made"))
        counted = Steps(sem("counted"), 4)
        stored = Steps(sem("stored"), 4)
        s_gate = sem("c_gate")
        s_v = sem("c_v")
        s_row = sem("c_row")
        s_start = sem("c_start")
        s_ended = sem("c_ended")
        s_base = sem("c_base")
        s_within = sem("c_within")
        s_across = sem("c_across")
        block = ctx.enter_context(nc.Block())

        @block.scalar
        def _(act):
            stored.start(act)

            def store(gr):
                counted.wait_apart(act, gr.it, s_gate)
                nc.scalar.copy(counts[:, :, bass.ds(gr.g * TPG, TPG)],
                               ps_c[gr.slot][:, 0:TPG * LOWS].rearrange("p (t l) -> p l t", l=LOWS)).then_inc(stored.sem, 1)
            over(act, 0, NG, 3, store)

        @block.tensor
        def _(pe):
            counted.start(pe)

            def count(gr):
                hot_made.wait(pe, gr.it)
                stored.wait(pe, gr.it - 4)
                for t in range(TPG):
                    last = nc.tensor.matmul(ps_c[gr.slot][:, t * LOWS:(t + 1) * LOWS], high_hot[gr.slot][:, t, :],
                                            keep["low_hot"][:, bass.ds(gr.g * TPG + t, 1), :].rearrange("p a l -> p (a l)"),
                                            start=True, stop=True)
                last.then_inc(counted.sem, 1)
            over(pe, 0, NG, 3, count)
            pe.wait_ge(s_row, 1)
            nc.tensor.matmul(ps_start[:, 0:1], keep["lower"][0:HIGHS, 0:HIGHS], row_total[:, :], start=True, stop=True).then_inc(s_start, 1)
            pe.wait_ge(s_ended, 1)
            nc.tensor.matmul(ps_base[:, 0:2 * NG], ones[:, :], ended[:, :, :].rearrange("p e g -> p (e g)"),
                             start=True, stop=True).then_inc(s_base, 1)

        @block.vector
        def _(dve):
            chain = [0]

            def link(ins):
                chain[0] += 1
                ins.then_inc(s_v, 1)
                dve.wait_ge(s_v, chain[0])

            nc.vector.memset(ones[:, :], 1.0)
            nc.vector.memset(ended[:, :, :], 0.0)

            def one_hots(gr):
                counted.wait(dve, gr.it - 4)
                nc.vector.tensor_tensor(high_hot[gr.slot][:, :, :],
                                        keep["keys"][:, bass.ds(gr.g * TPG, TPG), 1:2].to_broadcast([P, TPG, HIGHS]),
                                        keep["row_iota"][0:P, 0:HIGHS].unsqueeze(1).to_broadcast([P, TPG, HIGHS]),
                                        ALU.is_equal).then_inc(hot_made.sem, 1)
            over(dve, 0, NG, 3, one_hots)

            stored.wait(dve, NG - 1)
            c4 = counts[:, :, :].rearrange("p l (b j) -> p l b j", j=BLK)
            with dve.Fori(0, BLK - 1) as j:
                nc.vector.tensor_tensor(c4[:, :, :, bass.ds(j + 1, 1)], c4[:, :, :, bass.ds(j + 1, 1)], c4[:, :, :, bass.ds(j, 1)],
                                        ALU.add).then_inc(s_within, 1)
                dve.wait_ge(s_within, j + 1)
            nc.vector.memset(of_block[:, :, 0:1], 0.0).then_inc(s_across, 1)
            dve.wait_ge(s_across, 1)
            with dve.Fori(0, NB - 1) as k:
                nc.vector.tensor_tensor(of_block[:, :, bass.ds(k + 1, 1)], of_block[:, :, bass.ds(k, 1)],
                                        counts[:, :, bass.ds(k * BLK + (BLK - 1), 1)], ALU.add).then_inc(s_across, 1)
                dve.wait_ge(s_across, k + 2)
            link(nc.vector.tensor_tensor(total[:, :], of_block[:, :, NB - 1], c4[:, :, NB - 1, BLK - 1], ALU.add))
            nc.vector.tensor_reduce(row_total[:, :], total[:, :], AX.X, ALU.add).then_inc(s_row, 1)
            dve.wait_ge(s_start, 1)
            link(nc.vector.tensor_copy(start[:, 0:1], ps_start[:, 0:1]))
            for j in range(1, LOWS):
                link(nc.vector.tensor_tensor(start[:, j:j + 1], start[:, j - 1:j], total[:, j - 1:j], ALU.add))
            link(nc.vector.tensor_tensor(end[:, :], start[:, :], total[:, :], ALU.add))
            for j in range(LOWS):
                ins = nc.vector.scalar_tensor_tensor(out=ended[:, :, :], in0=keep["ends_iota"][0:HIGHS, :, :], scalar=end[:, j:j + 1],
                                                     in1=ended[:, :, :], op0=ALU.is_ge, op1=ALU.add)
                if j < LOWS - 1:
                    link(ins)
            ins.then_inc(s_ended, 1)
            link(nc.vector.tensor_tensor(of_block[:, :, :], of_block[:, :, :], start[:, :].unsqueeze(2).to_broadcast([HIGHS, LOWS, NB]), ALU.add))
            p4 = keep["places"][:, :, :].rearrange("p l (b j) -> p l b j", j=BLK)
            nc.vector.tensor_copy(p4[:, :, :, 0], of_block[:, :, :])
            for j in range(LOWS):
                nc.vector.tensor_tensor(p4[:, j, :, 1:BLK], c4[:, j, :, 0:BLK - 1],
                                        of_block[:, j, :].unsqueeze(2).to_broadcast([HIGHS, NB, BLK - 1]), ALU.add)
            dve.wait_ge(s_base, 1)
            nc.vector.tensor_scalar(keep["base_all"][:, :], ps_base[:, 0:NG], float(BUCKET), None, ALU.mult)
            nc.vector.tensor_scalar(keep["base"][:, :], ps_base[0:1, 0:NG], float(BUCKET), None, ALU.mult)
            link(nc.vector.tensor_copy(first_bucket[:, :], ps_base[0:1, 0:NG]))
            link(nc.vector.tensor_tensor(spread[:, :], ps_base[0:1, NG:2 * NG], first_bucket[:, :], ALU.subtract))
            link(nc.vector.tensor_reduce(widest[:, :], spread[:, :], AX.X, ALU.max))
            link(nc.vector.tensor_scalar(scaled[:, :], widest[:, :], 683.0, None, ALU.mult))
            link(nc.vector.tensor_scalar(widest_div[:, :], scaled[:, :], 12, None, ALU.arith_shift_right))
            link(nc.vector.tensor_scalar(keep["passes"][:, :], widest_div[:, :], 1.0, None, ALU.add))
            assert WIN == 6 * BUCKET and N <= 2048 * BUCKET


def place_edges(nc, a, keep):
    with ExitStack() as ctx:
        sb, ps, sem = alloc(nc, ctx)
        fT = [sb(f"fT{s}", [NRBF + 1, GE]) for s in range(4)]
        size = [sb(f"size{s}", [P, TPG, C]) for s in range(2)]
        keys4 = [sb(f"keys4{s}", [P, TPG, 2], F16) for s in range(4)]
        keyf = [sb(f"keyf{s}", [P, TPG]) for s in range(4)]
        high_T = [sb(f"high_T{s}", [HIGHS, GE]) for s in range(2)]
        same = [sb(f"same{s}", [P, TPG, P], BF16) for s in range(2)]
        rank = [sb(f"rank{s}", [P, TPG]) for s in range(2)]
        picked = [sb(f"picked{s}", [P, TPG, LOWS]) for s in range(2)]
        first_of = [sb(f"first_of{s}", [P, TPG]) for s in range(2)]
        place = [sb(f"place{s}", [P, TPG], I32) for s in range(4)]
        rows = [sb(f"rows{s}", [P, TPG, ROW]) for s in range(4)]
        ps_h = [ps(f"p_h{s}", [P, TPG, C]) for s in range(2)]
        ps_key = [ps(f"ps_key{s}", [C, 512]) for s in range(2)]
        ps_high = [ps(f"ps_high{s}", [C, 512]) for s in range(2)]
        ps_look = ps("ps_look", [P, 512])

        s_f = [sem(f"p_f{s}") for s in range(4)]
        s_out = [sem(f"p_out{s}") for s in range(4)]
        s_gate = sem("p_gate")
        s_ones = sem("p_ones")
        keys_made = Steps(sem("keys_made"), 4)
        keyf_made = Steps(sem("keyf_made"))
        spread_out = Steps(sem("spread_out"), 4)
        high_made = Steps(sem("high_made"), 2)
        size_made = Steps(sem("size_made"))
        hidden_read = Steps(sem("hidden_read"), 2)
        exp_made = Steps(sem("exp_made"))
        log_made = Steps(sem("log_made"))
        ranked = Steps(sem("ranked"), 2)
        looked = Steps(sem("looked"), 2)
        picked_made = Steps(sem("picked_made"), 2)
        first_made = Steps(sem("first_made"))
        row_made = Steps(sem("row_made"), 2)

        block = ctx.enter_context(nc.Block())

        @block.sync
        def _(sp):
            sp.wait_ge(s_ones, 1)

            def load(gr):
                spread_out.wait(sp, gr.it - 4)
                sp.dma_start(fT[gr.slot][0:NRBF, :], a["edge_attr_20"][:, bass.ds(gr.g * GE, GE)]).then_inc(s_f[gr.slot], 16)
            over(sp, 0, NG, 2, load)

        @block.gpsimd
        def _(pool):
            def scatter(gr):
                row_made.wait_apart(pool, gr.it, s_gate)
                for t in range(TPG):
                    pool.indirect_dma_start(a["sorted"], bass.IndirectOffsetOnAxis(ap=place[gr.slot][:, t:t + 1], axis=0),
                                            rows[gr.slot][:, t, :], None).then_inc(s_out[gr.slot], 16)
            over(pool, 0, NG, 2, scatter)
            for s in range(4):
                pool.wait_ge(s_out[s], 64 * (NG // 4))

        @block.scalar
        def _(act):
            hidden_read.start(act)
            nc.scalar.preload_act_table_set("natural_log_exp_and_others")

            def body(gr):
                b, c = size[gr.slot % 2], gr.slot % 2
                spread_out.wait(act, gr.it)
                row_made.wait(act, gr.it - 2)
                nc.scalar.activation(b[:, :, :], ps_h[c][:, :, :], ACT.Abs).then_inc(size_made.sem, 1)
                if not gr.fresh:
                    act.wait_ge(s_out[gr.slot], gr.use * 64)
                nc.scalar.activation(rows[gr.slot][:, :, 0:C], ps_h[c][:, :, :], ACT.Relu).then_inc(hidden_read.sem, 1)
                size_made.wait(act, gr.it)
                nc.scalar.activation(b[:, :, :], b[:, :, :], ACT.Exp, scale=-1.0).then_inc(exp_made.sem, 1)
                exp_made.wait(act, gr.it)
                nc.scalar.activation(b[:, :, :], b[:, :, :], ACT.Ln, scale=0.5, bias=keep["half"][0:P, 0:1]).then_inc(log_made.sem, 1)
            over(act, 0, NG, 2, body, lead=4)

        @block.tensor
        def _(pe):
            spread_out.start(pe)
            looked.start(pe)

            def spread(gr):
                pe.wait_ge(s_f[gr.slot], gr.use * 16 + 16)
                hidden_read.wait(pe, gr.it - 2)
                for t in range(TPG):
                    nc.tensor.matmul(ps_h[gr.slot % 2][:, t, :], fT[gr.slot][:, t * P:(t + 1) * P], keep["wf1"][:, :],
                                     start=True, stop=True)
                keys_made.wait(pe, gr.it)
                ranked.wait(pe, gr.it - 2)
                high_made.wait(pe, gr.it - 2)
                for i, out in enumerate((ps_key[gr.slot % 2], ps_high[gr.slot % 2])):
                    for t in range(TPG):
                        last = nc.tensor.matmul(out[:, t * P:(t + 1) * P], keys4[gr.slot][:, t, i:i + 1].to_broadcast([P, C]),
                                                keep["ident16"][0:P, 0:P], start=True, stop=True)
                last.then_inc(spread_out.sem, 1)

            def look_up(gr):
                high_made.wait(pe, gr.it)
                picked_made.wait(pe, gr.it - 1)
                for t in range(TPG):
                    last = nc.tensor.matmul(ps_look[:, t * LOWS:(t + 1) * LOWS], high_T[gr.slot % 2][:, t * P:(t + 1) * P],
                                            keep["places"][:, :, bass.ds(gr.g * TPG + t, 1)].rearrange("p l a -> p (l a)"),
                                            start=True, stop=True)
                last.then_inc(looked.sem, 1)

            spread(item(0, 0, 0, NG))

            def body(gr):
                if gr.later(1):
                    spread(gr.later(1))
                look_up(gr)
            over(pe, 0, NG, 2, body)

        @block.vector
        def _(dve):
            for st in (keys_made, high_made, ranked, picked_made, row_made):
                st.start(dve)
            for s in range(4):
                ins = nc.vector.memset(fT[s][:, :], 1.0)
            ins.then_inc(s_ones, 1)

            def keys(gr):
                spread_out.wait(dve, gr.it - 4)
                nc.vector.tensor_copy(keyf[gr.slot][:, :], keep["keys"][:, bass.ds(gr.g * TPG, TPG), 0]).then_inc(keyf_made.sem, 1)
                nc.vector.tensor_copy(keys4[gr.slot][:, :, :], keep["keys"][:, bass.ds(gr.g * TPG, TPG), :]).then_inc(keys_made.sem, 1)

            def from_psum(gr):
                c = gr.slot % 2
                spread_out.wait(dve, gr.it)
                looked.wait(dve, gr.it - 2)
                nc.vector.tensor_scalar(high_T[c][:, :], ps_high[c][0:HIGHS, 0:GE], keep["part_iota"][0:HIGHS, 0:1], None,
                                        ALU.is_equal).then_inc(high_made.sem, 1)
                keyf_made.wait(dve, gr.it)
                row_made.wait(dve, gr.it - 2)
                for t in range(TPG):
                    ins = nc.vector.scalar_tensor_tensor(out=same[c][:, t, :], in0=ps_key[c][0:P, t * P:(t + 1) * P],
                                                         scalar=keyf[gr.slot][:, t:t + 1], in1=keep["earlier"][0:P, 0:P],
                                                         op0=ALU.is_equal, op1=ALU.mult, accum_out=rank[c][:, t:t + 1])
                ins.then_inc(ranked.sem, 1)

            def to_row(gr):
                c = gr.slot % 2
                looked.wait(dve, gr.it)
                nc.vector.tensor_tensor(picked[c][:, :, :], ps_look[:, 0:TPG * LOWS].rearrange("p (t l) -> p t l", l=LOWS),
                                        keep["low_hot"][:, bass.ds(gr.g * TPG, TPG), :], ALU.mult).then_inc(picked_made.sem, 1)
                picked_made.wait(dve, gr.it)
                nc.vector.tensor_reduce(first_of[c][:, :], picked[c][:, :, :], AX.X, ALU.add).then_inc(first_made.sem, 1)
                log_made.wait(dve, gr.it)
                r = rows[gr.slot]
                nc.vector.tensor_tensor(r[:, :, 0:C], r[:, :, 0:C], size[c][:, :, :], ALU.add)
                nc.vector.tensor_copy(r[:, :, C:ROW], keep["edge"][:, bass.ds(gr.g * TPG, TPG), :])
                ranked.wait(dve, gr.it)
                first_made.wait(dve, gr.it)
                nc.vector.tensor_tensor(place[gr.slot][:, :], first_of[c][:, :], rank[c][:, :], ALU.add).then_inc(row_made.sem, 1)

            keys(item(0, 0, 0, NG))
            keys(item(0, 0, 1, NG))
            from_psum(item(0, 0, 0, NG))

            def body(gr):
                if gr.later(2):
                    keys(gr.later(2))
                if gr.later(1):
                    from_psum(gr.later(1))
                to_row(gr)
            over(dve, 0, NG, 2, body, lead=4)


def sum_edges(nc, a, keep):
    with ExitStack() as ctx:
        sb, ps, sem = alloc(nc, ctx)
        rows = [sb(f"erows{s}", [P, TPG, ROW]) for s in range(4)]
        hT = [sb(f"hT{s}", [C, GE]) for s in range(2)]
        dst4 = [sb(f"dst4{s}", [P, TPG], I32) for s in range(4)]
        got = [sb(f"got{s}", [P, TPG, 4, C]) for s in range(4)]
        col = [sb(f"col{s}", [P, TPG]) for s in range(2)]
        cut = [sb(f"cut{s}", [P, TPG, 4]) for s in range(2)]
        eq = sb("eq", [P, TPG, WIN])
        vu = sb("vu", [P, TPG, 3, C])
        dot2 = sb("dot2", [P, TPG, C])
        dot = [sb(f"dot{s}", [P, TPG, C]) for s in range(2)]
        hot = [sb(f"hot{s}", [P, TPG, 4, WIN]) for s in range(2)]
        msg = [sb(f"msg{s}", [P, 6, C]) for s in range(TPG)]
        sums = [sb(f"sums{s}", [C, 8, WIN]) for s in range(2)]
        ps_h = ps("ps_h", [C, 512])
        ps_w = [ps(f"ps_w{t}", [P, 4, C]) for t in range(TPG)]
        ps_sum = [ps(f"ps_sum{s}", [C, 8, WIN]) for s in range(2)]
        ps_out = ps("ps_out", [C, 8, WIN])

        s_rows = [sem(f"s_rows{s}") for s in range(4)]
        s_got = [sem(f"s_got{s}") for s in range(4)]
        s_gate = sem("s_gate")
        s_base = sem("s_base")
        s_zero = sem("s_zero")
        s_zero_v = sem("s_zero_v")
        h_turned = Steps(sem("h_turned"), 2)
        h_done = Steps(sem("h_done"), 2)
        w_made = Steps(sem("w_made"), 8)
        num_made = Steps(sem("num_made"), 4)
        dst_made = Steps(sem("dst_made"))
        eq_made = Steps(sem("eq_made"))
        hot_made = Steps(sem("hot_made"), 4)
        vu_made = Steps(sem("vu_made"), 4)
        dot_half = Steps(sem("dot_half"))
        dot_made = Steps(sem("dot_made"), 1)
        msg_made = Steps(sem("msg_made"), 16)
        sum_made = Steps(sem("sum_made"), 16)
        sum_copied = Steps(sem("sum_copied"), 2)
        out_made = Steps(sem("out_made"), 2)
        added = Steps(sem("added"), 1)

        block = ctx.enter_context(nc.Block())

        def passes(eng):
            return eng.Fori(0, eng.value_load(keep["passes"][0:1, 0:1], min_val=1, max_val=MAXP))

        @block.sync
        def _(sp):
            by_group = a["sorted"].rearrange("(g p t) r -> p g (t r)", p=P, t=TPG)
            with passes(sp) as k:
                def load(gr):
                    sum_made.wait(sp, (gr.it - 4) * TPG + 3)
                    sp.dma_start(rows[gr.slot][:, :, :].rearrange("p t r -> p (t r)"),
                                 by_group[:, bass.ds(gr.g, 1), :].rearrange("p a r -> p (a r)")).then_inc(s_rows[gr.slot], 16)
                over(sp, k, NG, 3, load)

        @block.gpsimd
        def _(pool):
            nc.gpsimd.memset(keep["node_sums"][:, 2:4, :], 0.0).then_inc(s_zero, 1)
            pool.wait_ge(s_zero, 1)
            dot_made.start(pool)

            def wait(steps, step):
                steps.wait_apart(pool, step, s_gate)

            with passes(pool) as k:
                def gather(gr):
                    wait(msg_made, (gr.it - 4) * TPG + 3)
                    pool.wait_ge(s_rows[gr.slot], gr.use * 16 + 16)
                    pool.sem_inc(s_gate, 1)
                    pool.tensor_copy(dst4[gr.slot][:, :], rows[gr.slot][:, :, DST]).then_inc(dst_made.sem, 1)
                    wait(dst_made, gr.it)
                    for t in range(TPG):
                        pool.indirect_dma_start(got[gr.slot][:, t, :, :].rearrange("p b c -> p (b c)"), None, a["table"],
                                                bass.IndirectOffsetOnAxis(ap=dst4[gr.slot][:, t:t + 1], axis=0)
                                                ).then_inc(s_got[gr.slot], 16)

                def dots(gr):
                    wait(vu_made, gr.it)
                    wait(msg_made, (gr.it - 2) * TPG + 3)
                    pool.tensor_tensor(dot2[:, :, :], vu[:, :, 0, :], vu[:, :, 1, :], ALU.add).then_inc(dot_half.sem, 1)
                    wait(dot_half, gr.it)
                    pool.tensor_tensor(dot[gr.slot % 2][:, :, :], dot2[:, :, :], vu[:, :, 2, :], ALU.add).then_inc(dot_made.sem, 1)

                g0 = item(k, 0, 0, NG)
                gather(g0)
                gather(g0.later(1))
                dots(g0)

                def body(gr):
                    if gr.later(2):
                        gather(gr.later(2))
                    if gr.later(1):
                        dots(gr.later(1))
                over(pool, k, NG, 2, body)

        @block.scalar
        def _(act):
            vu_made.start(act)
            h_done.start(act)
            sum_copied.start(act)
            with passes(act) as k:
                def copy_hidden(gr):
                    h_turned.wait(act, gr.it)
                    w_made.wait(act, (gr.it - 2) * TPG + 3)
                    nc.scalar.copy(hT[gr.slot % 2][:, :], ps_h[:, 0:GE]).then_inc(h_done.sem, 1)

                def turn(gr):
                    act.wait_ge(s_got[gr.slot], gr.use * 64 + 64)
                    act.wait_ge(s_rows[gr.slot], gr.use * 16 + 16)
                    dot_made.wait(act, gr.it - 1)
                    for t in range(TPG):
                        for i in range(3):
                            last = nc.scalar.activation(vu[:, t, i, :], got[gr.slot][:, t, 1 + i, :], ACT.Copy,
                                                        scale=rows[gr.slot][:, t, UNIT + i:UNIT + i + 1])
                    last.then_inc(vu_made.sem, 1)

                def copy_sums(gr, it):
                    sum_made.wait(act, it * TPG + 3)
                    out_made.wait(act, it - 2)
                    nc.scalar.copy(sums[gr][:, :, :], ps_sum[gr][:, :, :]).then_inc(sum_copied.sem, 1)

                g0 = item(k, 0, 0, NG)
                turn(g0)
                copy_hidden(g0)

                def body(gr):
                    nxt = gr.later(1)
                    if nxt:
                        copy_hidden(nxt)
                    if not gr.first:
                        copy_sums((gr.slot + 1) % 2, gr.it - 1)
                    if nxt:
                        turn(nxt)
                over(act, k, NG, 2, body)
                copy_sums(1, k * NG + NG - 1)

        @block.tensor
        def _(pe):
            h_turned.start(pe)
            w_made.start(pe)
            sum_made.start(pe)
            out_made.start(pe)
            with passes(pe) as k:
                def hidden(gr):
                    pe.wait_ge(s_rows[gr.slot], gr.use * 16 + 16)
                    h_done.wait(pe, gr.it - 1)
                    for t in range(TPG):
                        last = nc.tensor.transpose(ps_h[:, t * P:(t + 1) * P], rows[gr.slot][:, t, 0:C], keep["ident"][0:P, 0:P])
                    last.then_inc(h_turned.sem, 1)

                def weights(gr, t):
                    if t == 0:
                        h_done.wait(pe, gr.it)
                    msg_made.wait(pe, (gr.it - 1) * TPG + t)
                    w = ps_w[t][:, :, :].rearrange("p b c -> p (b c)")
                    nc.tensor.matmul(w, keep["ones3"][:, :], keep["bias3"][:, :], start=True, stop=False)
                    nc.tensor.matmul(w, hT[gr.slot % 2][:, t * P:(t + 1) * P],
                                     keep["wf2"][:, :, :].rearrange("p b c -> p (b c)"),
                                     start=False, stop=True).then_inc(w_made.sem, 1)

                def add_up(slot, it, t):
                    msg_made.wait(pe, it * TPG + t)
                    if t == 0:
                        hot_made.wait(pe, it)
                        sum_copied.wait(pe, it - 2)
                    m, o, acc = msg[t], hot[slot % 2], ps_sum[slot % 2]
                    for b, cols, hots in ((0, slice(0, 1), slice(0, 1)), (1, slice(2, 5), slice(1, 4)),
                                          (2, slice(1, 2), slice(0, 1)), (3, slice(5, 6), slice(0, 1)),
                                          (4, slice(6, 7), slice(0, 1)), (5, slice(7, 8), slice(0, 1))):
                        last = nc.tensor.matmul(acc[:, cols, :].rearrange("p b w -> p (b w)"), m[:, b, :],
                                                o[:, t, hots, :].rearrange("p b w -> p (b w)"),
                                                start=(t == 0 and b == 0), stop=(t == TPG - 1 and b == 5),
                                                skip_group_check=True)
                    last.then_inc(sum_made.sem, 1)

                def through_w1(slot, it):
                    sum_copied.wait(pe, it)
                    added.wait(pe, it - 1)
                    s = sums[slot % 2]
                    w1 = keep["w1"]
                    nc.tensor.matmul(ps_out[:, 0, :], w1[:, 0, :], s[:, 0, :], start=True, stop=False, skip_group_check=True)
                    nc.tensor.matmul(ps_out[:, 0, :], w1[:, 1, :], s[:, 1, :], start=False, stop=False, skip_group_check=True)
                    v = ps_out[:, 1:4, :].rearrange("p b w -> p (b w)")
                    nc.tensor.matmul(v, w1[:, 2, :], s[:, 2:5, :].rearrange("p b w -> p (b w)"), start=False, stop=False,
                                     skip_group_check=True)
                    nc.tensor.matmul(v, w1[:, 3, :], s[:, 5:8, :].rearrange("p b w -> p (b w)"), start=False, stop=True,
                                     skip_group_check=True).then_inc(out_made.sem, 1)

                hidden(item(k, 0, 0, NG))

                def body(gr):
                    for t in range(TPG):
                        weights(gr, t)
                        if t >= 2:
                            add_up(gr.slot, gr.it, t - 2)
                        elif not gr.first:
                            add_up(gr.slot + 1, gr.it - 1, t + 2)
                        if t == 0 and gr.later(1):
                            hidden(gr.later(1))
                        if t == 2 and not gr.first:
                            through_w1(gr.slot + 1, gr.it - 1)
                over(pe, k, NG, 2, body)
                for t in (2, 3):
                    add_up(1, k * NG + NG - 1, t)
                through_w1(1, k * NG + NG - 1)

        @block.vector
        def _(dve):
            for s in (num_made, hot_made, msg_made, added):
                s.start(dve)
            nc.vector.memset(keep["node_sums"][:, 0:2, :], 0.0).then_inc(s_zero_v, 1)
            dve.wait_ge(s_zero_v, 1)
            dve.wait_ge(s_zero, 1)
            with passes(dve) as k:
                def numbers(gr):
                    dve.wait_ge(s_rows[gr.slot], gr.use * 16 + 16)
                    c, r = gr.slot % 2, rows[gr.slot]
                    nc.vector.tensor_copy(cut[c][:, :, 0:1], r[:, :, RCUT:RCUT + 1])
                    nc.vector.tensor_tensor(cut[c][:, :, 1:4], r[:, :, UNIT:UNIT + 3], r[:, :, RCUT:RCUT + 1].to_broadcast([P, TPG, 3]),
                                            ALU.mult)
                    nc.vector.tensor_tensor(col[c][:, :], r[:, :, SRC], keep["base_all"][:, bass.ds(gr.g, 1)].to_broadcast([P, TPG]),
                                            ALU.subtract).then_inc(num_made.sem, 1)

                def one_hots(gr):
                    num_made.wait(dve, gr.it)
                    nc.vector.tensor_tensor(eq[:, :, :], keep["win_iota"][:, :].unsqueeze(1).to_broadcast([P, TPG, WIN]),
                                            col[gr.slot % 2][:, :].unsqueeze(2).to_broadcast([P, TPG, WIN]),
                                            ALU.is_equal).then_inc(eq_made.sem, 1)

                def scale_hots(gr):
                    eq_made.wait(dve, gr.it)
                    sum_made.wait(dve, (gr.it - 2) * TPG + 3)
                    c = gr.slot % 2
                    nc.vector.tensor_tensor(hot[c][:, :, :, :], eq[:, :, :].unsqueeze(2).to_broadcast([P, TPG, 4, WIN]),
                                            cut[c][:, :, :].unsqueeze(3).to_broadcast([P, TPG, 4, WIN]),
                                            ALU.mult).then_inc(hot_made.sem, 1)

                def messages(gr, t):
                    if t == 0:
                        dve.wait_ge(s_got[gr.slot], gr.use * 64 + 64)
                        dot_made.wait(dve, gr.it)
                    w_made.wait(dve, gr.it * TPG + t)
                    sum_made.wait(dve, (gr.it - 1) * TPG + t)
                    m, w, x = msg[t], ps_w[t], got[gr.slot]
                    nc.vector.tensor_tensor(m[:, 0:2, :], w[:, 0:2, :], x[:, t, 0:1, :].to_broadcast([P, 2, C]), ALU.mult)
                    nc.vector.tensor_tensor(m[:, 2, :], w[:, 2, :], dot[gr.slot % 2][:, t, :], ALU.mult)
                    nc.vector.tensor_tensor(m[:, 3:6, :], w[:, 3:4, :].to_broadcast([P, 3, C]), x[:, t, 1:4, :],
                                            ALU.mult).then_inc(msg_made.sem, 1)

                def add_window(g, it):
                    start = dve.value_load(keep["base"][0:1, bass.ds(g, 1)] if not isinstance(g, int) else keep["base"][0:1, g:g + 1],
                                           min_val=0, max_val=N)
                    out_made.wait(dve, it)
                    added.wait(dve, it - 1)
                    part = keep["node_sums"][:, :, bass.ds(start, WIN)]
                    nc.vector.tensor_tensor(part, ps_out[:, 0:4, :], part, ALU.add).then_inc(added.sem, 1)

                g0 = item(k, 0, 0, NG)
                numbers(g0)
                one_hots(g0)
                scale_hots(g0)

                def body(gr):
                    for t in range(TPG):
                        messages(gr, t)
                        if gr.later(1) and t < 3:
                            (numbers, one_hots, scale_hots)[t](gr.later(1))
                    if not gr.first:
                        add_window(gr.g - 1, gr.it - 1)
                over(dve, k, NG, 2, body)
                add_window(NG - 1, k * NG + NG - 1)
                e, b = keep["base_all"], keep["base"]
                nc.vector.tensor_scalar(e[:, :], e[:, :], float(WIN), None, ALU.add).then_inc(s_base, 1)
                nc.vector.tensor_scalar(b[:, :], b[:, :], float(WIN), float(N), ALU.add, ALU.min).then_inc(s_base, 1)
                dve.wait_ge(s_base, k * 2 + 2)


NCH = 25
TPC = NT // NCH
NC_ = TPC * P
SOFT = 5 * NC_
GE_DIM = 160
HI = GE_DIM - C
RESULT, CARRY_OUT = 100, 101
FLAG = 105
FLAG_IN = 35
NIB = 16
OUTPUT = 128
N_WEIGHTS = 36
NF = 5


def finish(nc, a, keep):
    with ExitStack() as ctx:
        sb, ps, sem = alloc(nc, ctx)
        x = sb("x", [P, 4, TPC, D])
        xl = sb("xl", [P, 4, TPC, D])
        st = [sb(f"st{s}", [C, 4, NC_]) for s in range(4)]
        soft = [sb(f"fsoft{s}", [C, SOFT]) for s in range(2)]
        stats = sb("fstats", [P, 4, TPC, 6])
        mv = sb("fmv", [P, 4, TPC, 2])
        std = sb("fstd", [P, 4, TPC])
        rstd = sb("frstd", [P, 4, TPC])
        eps = sb("feps", [P, 1])
        weight16 = sb("weight16", [P, 4, 16])
        iota16 = sb("iota16", [P, 16])
        iota16_int = sb("iota16_int", [P, 16], I32)
        score = sb("score", [P, 2, TPC, 4, 16])
        best = sb("best", [P, 2, TPC, 4])
        any16 = sb("any16", [P, 2, TPC, 4])
        flags = sb("flags", [P, 2, TPC, 3])
        feats = sb("feats", [P, 2, TPC, 2, NF])
        mask = sb("mask", [P, 4, TPC, 4])
        fT = sb("ffT", [C, 2, 4 * P])
        h1 = sb("h1", [C, 3, 4 * P])
        h2 = sb("h2", [C, 2, 3, 4 * P])
        b3 = sb("b3", [P, 4])
        y = sb("y", [P, TPC, 2, 4])
        yy = sb("yy", [P, TPC, 2, 4])
        ym = sb("ym", [P, TPC, 2, 2])
        yr = sb("yr", [P, TPC, 2])
        yc = sb("yc", [P, TPC])
        hot = sb("fhot", [P, TPC, 2, 16])
        l1 = sb("l1", [C, 3, C])
        l2 = sb("l2", [C, 7, C])
        l3 = sb("l3", [C, 3, 4])
        b2 = sb("b2", [C, 3])
        ps_x = [ps(f"ps_x{t}", [P, 4, C]) for t in range(TPC)]
        ps_f = ps("ps_f", [C, 512])
        ps_l = [ps(f"ps_l{b}", [C, 512]) for b in range(4)]
        ps_y = ps("ps_y", [P, 512])
        y_ps = ps_y[:, 0:TPC * 2 * 4].rearrange("p (t q o) -> p t q o", q=2, o=4)

        s_zero = sem("f_zero")
        s_w = sem("f_w")
        s_iota = sem("f_iota")
        s_gate = sem("f_gate")
        s_gate_v = sem("f_gate_v")
        s_v = sem("f_v")
        s_x = [sem(f"f_x{s}") for s in range(4)]
        s_out = [sem(f"f_out{s}") for s in range(4)]
        sums_here = Steps(sem("sums_here"))
        s_abs = sem("act_abs")
        s_exp = sem("act_exp")
        s_ln = sem("act_ln")
        s_soft = sem("soft_done")
        w2_done = Steps(sem("w2_done"), 4)
        x1_done = Steps(sem("x1_done"), 1)
        stat = Steps(sem("f_stat"))
        var = Steps(sem("f_var"))
        root = Steps(sem("f_root"))
        inv = Steps(sem("f_inv"))
        normed = Steps(sem("f_normed"))
        feats_done = Steps(sem("feats_done"))
        turned = Steps(sem("f_turned"), 2)
        f_copied = Steps(sem("f_copied"), 1)
        layer_made = Steps(sem("layer_made"), 12)
        relu_made = Steps(sem("relu_made"), 4)
        l3_done = Steps(sem("l3_done"), 2)
        y_read = Steps(sem("y_read"), 1)
        added = Steps(sem("f_added"))
        done = Steps(sem("f_done"))
        dve_front = Steps(sem("dve_front"))
        dve_tail = Steps(sem("dve_tail"))

        s_hot = sem("f_hot")
        s_hot_scaled = sem("f_hot_scaled")

        block = ctx.enter_context(nc.Block())
        rows_of = a["x"].rearrange("(n t p) d -> n p t d", t=TPC, p=P)
        out_rows = a["out"].rearrange("(n t p) d -> n p t d", t=TPC, p=P)

        @block.sync
        def _(sp):
            for s in range(4):
                sp.dma_start(x[:, s, :, :], rows_of[s]).then_inc(s_x[s], 16)
            sp.wait_ge(s_zero, 1)
            wa, ws = a["Wa"], a["Ws"]
            weights = []
            for w, col in ((wa, (0, 0, C, 2, 0)), (ws, (1, 1, C, 2, HI))):
                first_block, _, _, rest_block, at = col
                for r, rows in ((0, slice(0, 2)), (2, slice(FLAG_IN, FLAG_IN + 2))):
                    weights.append((l1[r:r + 2, first_block, :], w[0, rows, 0:C]))
                    weights.append((l1[r:r + 2, rest_block, at:at + HI], w[0, rows, C:GE_DIM]))
            for m, bias in ((0, a["ba"]), (1, a["bs"])):
                weights.append((l1[4:5, m, :], bias[0:1, 0:C]))
                weights.append((l1[4:5, 2, m * HI:(m + 1) * HI], bias[0:1, C:GE_DIM]))
                weights.append((b2[:, m:m + 1], bias[1:2, 0:C].rearrange("a c -> c a")))
                weights.append((b2[m * HI:(m + 1) * HI, 2:3], bias[1:2, C:GE_DIM].rearrange("a c -> c a")))
                for o, q in ((0, RESULT), (2, CARRY_OUT)):
                    weights.append((b3[:, o + m:o + m + 1], bias[2:3, q:q + 1].to_broadcast([P, 1])))
            for m, w in ((0, wa), (1, ws)):
                weights.append((l2[:, 2 * m, :], w[1, 0:C, 0:C]))
                weights.append((l2[m * HI:(m + 1) * HI, 2 * m + 1, :], w[1, C:GE_DIM, 0:C]))
                weights.append((l2[:, 4 + m, m * HI:(m + 1) * HI], w[1, 0:C, C:GE_DIM]))
                weights.append((l2[m * HI:(m + 1) * HI, 6, m * HI:(m + 1) * HI], w[1, C:GE_DIM, C:GE_DIM]))
                for o, q in ((0, RESULT), (2, CARRY_OUT)):
                    weights.append((l3[:, m, o + m:o + m + 1], w[2, 0:C, q:q + 1]))
                    weights.append((l3[m * HI:(m + 1) * HI, 2, o + m:o + m + 1], w[2, C:GE_DIM, q:q + 1]))
            with nc.allow_non_contiguous_dma(reason="a few columns of the weights"):
                for dst, src in weights:
                    sp.dma_start(dst, src).then_inc(s_w, 16)
            assert len(weights) == N_WEIGHTS

            def move(ch):
                done.wait(sp, ch.it)
                sp.dma_start(out_rows[bass.ds(ch.g, 1)].rearrange("a p t d -> (a p) t d") if not isinstance(ch.g, int) else out_rows[ch.g],
                             x[:, ch.slot, :, :]).then_inc(s_out[ch.slot], 16)
                nxt = ch.later(4)
                if nxt:
                    sp.wait_ge(s_out[ch.slot], ch.use * 16 + 16)
                    sp.dma_start(x[:, ch.slot, :, :],
                                 rows_of[bass.ds(nxt.g, 1)].rearrange("a p t d -> (a p) t d") if not isinstance(nxt.g, int) else rows_of[nxt.g]
                                 ).then_inc(s_x[ch.slot], 16)
            over(sp, 0, NCH, 4, move)
            for s in range(4):
                sp.wait_ge(s_out[s], 16 * (NCH // 4 + (s < NCH % 4)))

        @block.gpsimd
        def _(pool):
            def wait(steps, step):
                steps.wait_apart(pool, step, s_gate)

            pool.iota(iota16_int[:, :], pattern=[[1, 16]], base=0, channel_multiplier=0).then_inc(s_iota, 1)

            def fetch(ch):
                wait(w2_done, ch.it - 4)
                pool.tensor_copy(st[ch.slot][:, :, :], keep["node_sums"][:, :, bass.ds(ch.g * NC_, NC_)]).then_inc(sums_here.sem, 1)

            def body(ch):
                if ch.later(3):
                    fetch(ch.later(3))
                wait(normed, ch.it)
                pool.tensor_tensor(x[:, ch.slot, :, :], x[:, ch.slot, :, :], xl[:, ch.slot, :, :], ALU.add).then_inc(added.sem, 1)
            pool.wait_ge(s_soft, 1)
            for s in range(3):
                fetch(item(0, 0, s, NCH))
            pool.wait_ge(s_soft, N // SOFT)
            over(pool, 0, NCH, 4, body)

        @block.scalar
        def _(act):
            f_copied.start(act)
            relu_made.start(act)

            nc.scalar.preload_act_table_set("natural_log_exp_and_others")
            for n in range(N // SOFT):
                b = soft[n % 2]
                if n >= 2:
                    act.wait_ge(s_soft, n - 1)
                nc.scalar.activation(b[:, :], keep["node_sums"][:, 0, n * SOFT:(n + 1) * SOFT], ACT.Abs).then_inc(s_abs, 1)
                act.wait_ge(s_abs, n + 1)
                nc.scalar.activation(b[:, :], b[:, :], ACT.Exp, scale=-1.0).then_inc(s_exp, 1)
                act.wait_ge(s_exp, n + 1)
                nc.scalar.activation(b[:, :], b[:, :], ACT.Ln, scale=0.5, bias=keep["half"][:, 0:1]).then_inc(s_ln, 1)

            def roots(ch):
                var.wait(act, ch.it)
                nc.scalar.activation(std[:, ch.slot, :], mv[:, ch.slot, :, 1], ACT.Sqrt, bias=eps[:, 0:1]).then_inc(root.sem, 1)

            def copy_feats(ch):
                turned.wait(act, ch.it)
                layer_made.wait(act, (ch.it - 2) * 6 + 2)
                nc.scalar.copy(fT[0:NF, ch.slot % 2, :], ps_f[0:NF, 0:4 * P]).then_inc(f_copied.sem, 1)

            def relus1(ch):
                layer_made.wait(act, (ch.it - 1) * 6 + 5)
                for b in range(3):
                    layer_made.wait(act, ch.it * 6 + b)
                    nc.scalar.activation(h1[:, b, :], ps_l[(ch.slot * 6 + b) % 4][:, 0:4 * P], ACT.Relu).then_inc(relu_made.sem, 1)

            def relus2(ch):
                l3_done.wait(act, ch.it - 2)
                for b in range(3):
                    layer_made.wait(act, ch.it * 6 + 3 + b)
                    nc.scalar.activation(h2[:, ch.slot % 2, b, :], ps_l[(ch.slot * 6 + 3 + b) % 4][:, 0:4 * P], ACT.Relu,
                                         bias=b2[:, b:b + 1]).then_inc(relu_made.sem, 1)

            for s in range(2):
                roots(item(0, 0, s, NCH))
            copy_feats(item(0, 0, 0, NCH))

            def body(ch):
                relus1(ch)
                if ch.later(1):
                    copy_feats(ch.later(1))
                if ch.later(2):
                    roots(ch.later(2))
                relus2(ch)
            act.wait_ge(s_w, 16 * N_WEIGHTS)
            over(act, 0, NCH, 4, body)

        @block.tensor
        def _(pe):
            for s in (w2_done, turned, layer_made, l3_done):
                s.start(pe)

            def through_w2(ch):
                sums_here.wait(pe, ch.it)
                x1_done.wait(pe, ch.it - 1)
                for t in range(TPC):
                    for b in range(4):
                        last = nc.tensor.matmul(ps_x[t][:, b, :], st[ch.slot][:, b, t * P:(t + 1) * P],
                                                keep["w2"][:, min(b, 1), :], start=True, stop=True)
                last.then_inc(w2_done.sem, 1)

            def turn(ch):
                feats_done.wait(pe, ch.it)
                f_copied.wait(pe, ch.it - 1)
                for q in range(2):
                    for t in range(TPC):
                        last = nc.tensor.transpose(ps_f[0:NF, (q * TPC + t) * P:(q * TPC + t + 1) * P],
                                                   feats[:, ch.slot % 2, t, q, :], keep["ident"][0:P, 0:P])
                last.then_inc(turned.sem, 1)

            def layer1(ch):
                f_copied.wait(pe, ch.it)
                for b in range(3):
                    relu_made.wait(pe, ch.it * 6 + b - 4)
                    nc.tensor.matmul(ps_l[(ch.slot * 6 + b) % 4][:, 0:4 * P], l1[:, b, :], fT[:, ch.slot % 2, :],
                                     start=True, stop=True).then_inc(layer_made.sem, 1)

            def layer2(ch):
                relu_made.wait(pe, ch.it * 6 + 2)
                for b, ins in enumerate((((0, 0), (2, 1)), ((1, 2), (2, 3)), ((0, 4), (1, 5), (2, 6)))):
                    for n, (i, w) in enumerate(ins):
                        last = nc.tensor.matmul(ps_l[(ch.slot * 6 + 3 + b) % 4][:, 0:4 * P], l2[:, w, :], h1[:, i, :],
                                                start=(n == 0), stop=(n == len(ins) - 1))
                    last.then_inc(layer_made.sem, 1)

            def layer3(ch):
                relu_made.wait(pe, ch.it * 6 + 5)
                y_read.wait(pe, ch.it - 1)
                for q in range(2):
                    for t in range(TPC):
                        for b in range(3):
                            at = (q * TPC + t) * P
                            last = nc.tensor.matmul(y_ps[:, t, q, :], h2[:, ch.slot % 2, b, at:at + P], l3[:, b, :],
                                                    start=(b == 0), stop=(b == 2))
                last.then_inc(l3_done.sem, 1)

            def before(ch):
                s = (ch.slot - 1) % 4
                return Item(None, ch.it - 1, s, None, NCH)

            def body(ch):
                layer1(ch)
                if ch.later(2):
                    through_w2(ch.later(2))
                if ch.later(1):
                    turn(ch.later(1))
                if not ch.first:
                    layer3(before(ch))
                layer2(ch)

            pe.wait_ge(s_w, 16 * N_WEIGHTS)
            pe.wait_ge(s_zero, 2)
            through_w2(item(0, 0, 0, NCH))
            through_w2(item(0, 0, 1, NCH))
            turn(item(0, 0, 0, NCH))
            over(pe, 0, NCH, 4, body)
            layer3(item(0, NCH // 4, 0, NCH))

        @block.vector
        def _(dve):
            for s in (x1_done, y_read):
                s.start(dve)
            for t in (l1, l2, l3):
                nc.vector.memset(t[:, :, :], 0.0)
            nc.vector.memset(b2[:, :], 0.0).then_inc(s_zero, 1)
            nc.vector.memset(feats[:, :, :, :, :], 1.0)
            nc.vector.memset(eps[:, :], EPS)
            nc.vector.memset(fT[:, :, :], 0.0).then_inc(s_zero, 1)
            dve.wait_ge(s_zero, 2)
            for n in range(N // SOFT):
                dve.wait_ge(s_ln, n + 1)
                v = keep["node_sums"][:, 0, n * SOFT:(n + 1) * SOFT]
                nc.vector.scalar_tensor_tensor(out=v, in0=v, scalar=0.0, in1=soft[n % 2][:, :], op0=ALU.max,
                                               op1=ALU.add).then_inc(s_soft, 1)
            dve.wait_ge(s_iota, 1)
            nc.vector.tensor_copy(iota16[:, :], iota16_int[:, :]).then_inc(s_v, 1)
            dve.wait_ge(s_v, 1)
            nc.vector.tensor_scalar(weight16[:, :, :], iota16[:, :].unsqueeze(1).to_broadcast([P, 4, 16]), -1.0, 16.0,
                                    ALU.mult, ALU.add).then_inc(s_v, 1)
            dve.wait_ge(s_v, 2)
            dve.wait_ge(s_w, 16 * N_WEIGHTS)
            FRONT, TAIL = 4, 5

            def add_rows(ch):
                c = ch.slot
                dve.wait_ge(s_x[c], ch.use * 16 + 16)
                w2_done.wait(dve, ch.it)
                for t in range(TPC):
                    nc.vector.tensor_tensor(x[:, c, t, 0:C], x[:, c, t, 0:C], ps_x[t][:, 0, :], ALU.add)
                    v = x[:, c, t, C:D].rearrange("p (d i) -> p d i", i=3)
                    last = nc.vector.tensor_tensor(v, v, ps_x[t][:, 1:4, :].rearrange("p i d -> p d i"), ALU.add)
                last.then_inc(x1_done.sem, 1)
                x1_done.wait(dve, ch.it)
                for t in range(TPC):
                    last = nc.vector.bn_stats(stats[:, c, t, :], x[:, c, t, :])
                last.then_inc(stat.sem, 1)
                stat.wait_apart(dve, ch.it, s_gate_v)
                for t in range(TPC):
                    last = nc.vector.bn_aggr(mv[:, c, t, :], stats[:, c, t, :])
                last.then_inc(var.sem, 1)

            def decode(ch):
                c, h = ch.slot, ch.slot % 2
                root.wait(dve, ch.it)
                nc.vector.reciprocal(rstd[:, c, :], std[:, c, :]).then_inc(inv.sem, 1)
                inv.wait(dve, ch.it)
                for t in range(TPC):
                    last = nc.vector.tensor_scalar(xl[:, c, t, :], x[:, c, t, :], mv[:, c, t, 0:1], rstd[:, c, t:t + 1],
                                                   ALU.subtract, ALU.mult)
                last.then_inc(normed.sem, 1)
                normed.wait(dve, ch.it)
                nc.vector.scalar_tensor_tensor(out=score[:, h].rearrange("p t n j -> p t (n j)"), in0=xl[:, c, :, NIB:NIB + 64],
                                               scalar=0.5, in1=weight16[:, :, :].rearrange("p n j -> p (n j)").unsqueeze(1).to_broadcast([P, TPC, 64]),
                                               op0=ALU.is_gt, op1=ALU.mult)
                nc.vector.tensor_scalar(flags[:, h], xl[:, c, :, 0:3], 0.5, None, ALU.is_gt)
                turned.wait(dve, ch.it - 2)
                nc.vector.tensor_copy(feats[:, h, :, :, 2:4], xl[:, c, :, FLAG:FLAG + 2].unsqueeze(2).to_broadcast([P, TPC, 2, 2])
                                      ).then_inc(dve_front.sem, 1)
                dve_front.wait(dve, ch.it * FRONT)
                nc.vector.tensor_reduce(best[:, h], score[:, h], AX.X, ALU.max)
                nc.vector.tensor_tensor(mask[:, c, :, 0], flags[:, h, :, 0], flags[:, h, :, 1], ALU.mult).then_inc(dve_front.sem, 1)
                dve_front.wait(dve, ch.it * FRONT + 1)
                nc.vector.tensor_scalar(any16[:, h], best[:, h], 0.0, 16.0, ALU.is_gt, ALU.mult)
                nc.vector.tensor_tensor(mask[:, c, :, 3], flags[:, h, :, 0], mask[:, c, :, 0], ALU.subtract).then_inc(dve_front.sem, 1)
                dve_front.wait(dve, ch.it * FRONT + 2)
                nc.vector.tensor_tensor(mask[:, c, :, 1], mask[:, c, :, 3], flags[:, h, :, 2], ALU.mult).then_inc(dve_front.sem, 1)
                dve_front.wait(dve, ch.it * FRONT + 3)
                nc.vector.tensor_tensor(mask[:, c, :, 2], mask[:, c, :, 0], mask[:, c, :, 1], ALU.add)
                nc.vector.tensor_tensor(feats[:, h, :, :, 0:2].rearrange("p t q f -> p t f q"),
                                        any16[:, h].rearrange("p t (f q) -> p t f q", q=2),
                                        best[:, h].rearrange("p t (f q) -> p t f q", q=2), ALU.subtract).then_inc(feats_done.sem, 1)

            def outputs(it, c):
                def step(n, ins):
                    ins.then_inc(dve_tail.sem, 1)
                    dve_tail.wait(dve, it * TAIL + n)

                l3_done.wait(dve, it)
                nc.vector.tensor_tensor(y[:, :, :, :], y_ps, b3[:, :].unsqueeze(1).unsqueeze(1).to_broadcast([P, TPC, 2, 4]),
                                        ALU.add).then_inc(y_read.sem, 1)
                y_read.wait(dve, it)
                for t in range(TPC):
                    ins = nc.vector.tensor_tensor(yy[:, t].rearrange("p q (o m) -> p q o m", m=2), y[:, t].rearrange("p q (o m) -> p q o m", m=2),
                                                  mask[:, c, t, 0:2].unsqueeze(1).unsqueeze(1).to_broadcast([P, 2, 2, 2]), ALU.mult)
                step(0, ins)
                step(1, nc.vector.tensor_tensor(ym[:, :, :, :], yy[:, :, :, 0:4:2], yy[:, :, :, 1:4:2], ALU.add))
                nc.vector.tensor_scalar(yr[:, :, :], ym[:, :, :, 0], 0.0, 15.0, ALU.max, ALU.min)
                step(2, nc.vector.scalar_tensor_tensor(out=yc[:, :], in0=ym[:, :, 1, 1], scalar=0.5, in1=mask[:, c, :, 2],
                                                       op0=ALU.is_gt, op1=ALU.mult))
                nc.vector.tensor_scalar(yr[:, :, :], yr[:, :, :], float(2 ** 23), None, ALU.add).then_inc(dve_tail.sem, 1)
                dve_tail.wait(dve, it * TAIL + 3)
                nc.vector.tensor_scalar(yr[:, :, :], yr[:, :, :], float(2 ** 23), None, ALU.subtract).then_inc(dve_tail.sem, 1)
                dve_tail.wait(dve, it * TAIL + 4)
                nc.vector.tensor_tensor(hot[:, :, :, :], iota16[:, :].unsqueeze(1).unsqueeze(1).to_broadcast([P, TPC, 2, 16]),
                                        yr[:, :, :].unsqueeze(3).to_broadcast([P, TPC, 2, 16]), ALU.is_equal).then_inc(hot_made.sem, 1)
                hot_made.wait(dve, it)
                for t in range(TPC):
                    ins = nc.vector.tensor_scalar(hot[:, t, :, :], hot[:, t, :, :], mask[:, c, t, 2:3], 2.0, ALU.mult, ALU.mult)
                ins.then_inc(hot_scaled.sem, 1)
                hot_scaled.wait(dve, it)
                added.wait(dve, it)
                o = x[:, c, :, OUTPUT:OUTPUT + 32]
                nc.vector.tensor_tensor(o, o, hot[:, :, :, :].rearrange("p t q j -> p t (q j)"), ALU.add)
                o = x[:, c, :, OUTPUT + 32]
                nc.vector.tensor_tensor(o, o, yc[:, :], ALU.add).then_inc(done.sem, 1)

            hot_made = Steps(s_hot)
            hot_scaled = Steps(s_hot_scaled)
            c0, c1 = (item(0, 0, s, NCH) for s in range(2))
            add_rows(c0)
            add_rows(c1)
            decode(c0)

            def body(ch):
                if ch.later(1):
                    decode(ch.later(1))
                if ch.later(2):
                    add_rows(ch.later(2))
                if not ch.first:
                    outputs(ch.it - 1, (ch.slot - 1) % 4)
            over(dve, 0, NCH, 4, body)
            outputs(NCH - 1, (NCH - 1) % 4)


def build(nc, a):
    with ExitStack() as ctx:
        sb, ps, sem = alloc(nc, ctx)
        keep = {
            "ident": sb("ident", [C, C]),
            "w2": sb("w2", [C, 2, C]),
            "half": sb("half", [C, 1]),
        }
        keep.update({
            "base": sb("base", [1, NG], I32),
            "base_all": sb("base_all", [P, NG]),
            "passes": sb("passes", [1, 1], I32),
            "win_iota_int": sb("win_iota_int", [P, WIN], I32),
            "win_iota": sb("win_iota", [P, WIN]),
            "wf2": sb("wf2", [C, 4, C]),
            "bias3": sb("bias3", [C, D], BF16),
            "ones3": sb("ones3", [C, P], BF16),
            "w1": sb("w1", [C, 4, C]),
        })
        with ExitStack() as place_ctx:
            sb, ps, sem = alloc(nc, place_ctx)
            keep.update({
                "edge": sb("edge", [P, E // P, ROW - C]),
                "keys": sb("keys", [P, E // P, 2], F16),
                "low_hot": sb("low_hot", [P, E // P, LOWS], BF16),
                "places": sb("places", [HIGHS, LOWS, E // P]),
                "wf1": sb("wf1", [NRBF + 1, C]),
                "ident16": sb("ident16", [C, C], F16),
                "earlier": sb("earlier", [C, C]),
                "lower": sb("lower", [C, C]),
                "row_iota_int": sb("row_iota_int", [C, C], I32),
                "row_iota": sb("row_iota", [C, C], F16),
                "part_iota_int": sb("part_iota_int", [C, 1], I32),
                "part_iota": sb("part_iota", [C, 1]),
                "ends_iota_int": sb("ends_iota_int", [C, 2, NG], I32),
                "ends_iota": sb("ends_iota", [C, 2, NG]),
            })
            setup_and_nodes(nc, a, keep)
            count_edges(nc, a, keep)
            place_edges(nc, a, keep)
        sb, ps, sem = alloc(nc, ctx)
        keep["node_sums"] = ctx.enter_context(nc.sbuf_tensor("node_sums", [C, 4, NP], F32))
        sum_edges(nc, a, keep)
        finish(nc, a, keep)


def kernel(**inputs):
    import concourse.bacc as bacc
    from concourse.bass_utils import run_bass_kernel_spmd

    def tiles(v):
        v = np.asarray(v).reshape(E // P, P, -1)
        return np.ascontiguousarray(v.transpose(1, 2, 0).squeeze(1) if v.shape[2] == 1 else v.transpose(1, 2, 0))

    given = {
        "x": np.asarray(inputs["x"]),
        "src": tiles(inputs["src"]),
        "dst": tiles(inputs["dst"]),
        "edge_attr_20": np.ascontiguousarray(np.asarray(inputs["edge_attr_20"]).T),
        "edge_attr_3": tiles(inputs["edge_attr_3"]),
        "edge_weight": tiles(inputs["edge_weight"]),
    }
    for name in ("W_in2f_s", "W_in2f_v", "Wf1", "Wf2", "W1_s", "W1_v", "W2_s", "W2_v"):
        given[name] = np.asarray(inputs["L0_gnn_" + name])
    for name in ("bf1", "bf2"):
        given[name] = np.asarray(inputs["L0_gnn_" + name]).reshape(1, -1)
    for name in ("Wa", "Ws"):
        given[name] = np.ascontiguousarray(np.asarray(inputs["L0_ffn_" + name]).transpose(0, 2, 1))
    for name in ("ba", "bs"):
        given[name] = np.asarray(inputs["L0_ffn_" + name])

    nc = bacc.Bacc("TRN2", target_bir_lowering=False, num_devices=1)
    arrays, a = {}, {}
    for name, value in given.items():
        arrays["in_" + name] = value
        a[name] = nc.dram_tensor("in_" + name, value.shape, mybir.dt.from_np(value.dtype), kind="ExternalInput").ap()
    a["out"] = nc.dram_tensor("out", (N, D), F32, kind="ExternalOutput").ap()
    a["table"] = nc.dram_tensor("table", (N, D), F32, kind="Internal").ap()
    a["sorted"] = nc.dram_tensor("sorted", (E, ROW), F32, kind="Internal").ap()
    build(nc, a)
    r = run_bass_kernel_spmd(nc, [arrays], core_ids=[0])
    return r.results[0]["out"]
```

```python
from contextlib import ExitStack

import numpy as np

import concourse.bass as bass
from concourse import mybir

F32 = mybir.dt.float32
BF16 = mybir.dt.bfloat16
F16 = mybir.dt.float16
I32 = mybir.dt.int32
ALU = mybir.AluOpType
ACT = mybir.ActivationFunctionType
AX = mybir.AxisListType

N = 6250
E = 100000
C = 128
D = 4 * C
NRBF = 20
P = 125
TPG = 4
GE = TPG * P
NG = E // GE
NT = N // P
WIN = 48
MAXP = (N + WIN - 1) // WIN
NP = N + WIN
EPS = 1e-5
Y0 = float(1.0 / np.sqrt(4.0 * np.pi))
Y1 = float(np.sqrt(3.0 / (4.0 * np.pi)))
RC = float(1.0 / np.sqrt(C))
R2F = float(1.0 / np.sqrt(2 * C))
BUCKET_BITS = 3
BUCKET = 1 << BUCKET_BITS
LOW_BITS = 3
LOWS = 1 << LOW_BITS
HIGHS = ((N - 1) >> (BUCKET_BITS + LOW_BITS)) + 1
SRC, RCUT, UNIT, DST = C, C + 1, C + 2, C + 5
ROW = C + 6


class Steps:

    def __init__(self, sem, ahead=0):
        self.sem, self.ahead = sem, ahead

    def start(self, eng):
        if self.ahead:
            eng.sem_inc(self.sem, self.ahead)

    def wait(self, eng, step):
        eng.wait_ge(self.sem, step + 1 + self.ahead)

    def wait_apart(self, eng, step, passed):
        self.wait(eng, step)
        eng.sem_inc(passed, 1)


class Item:

    def __init__(self, g, it, slot, use, total):
        self.g, self.it, self.slot, self.use, self.total = g, it, slot, use, total
        self.first = isinstance(g, int) and g == 0
        self.fresh = isinstance(g, int) and g < 4

    def later(self, n):
        if isinstance(self.g, int) and self.g + n >= self.total:
            return None
        s = self.slot + n
        return Item(self.g + n, self.it + n, s % 4, self.use + s // 4, self.total)

    def pair(self, n=0):
        return self.use * 2 + (self.slot + n) // 2


def item(k, i, s, total):
    return Item(i * 4 + s, k * total + i * 4 + s, s % 4, k * (total // 4) + i + s // 4, total)


def over(eng, k, total, reach, body, lead=1):
    for s in range(lead):
        body(item(k, 0, s, total))
    turns = (total - lead - reach) // 4
    with eng.Fori(0, turns) as i:
        for s in range(4):
            body(item(k, i, s + lead, total))
    for s in range(total - lead - 4 * turns):
        body(item(k, turns, s + lead, total))


def alloc(nc, ctx):
    def sb(name, shape, dt=F32):
        return ctx.enter_context(nc.sbuf_tensor(name, shape, dt))

    def ps(name, shape, dt=F32):
        return ctx.enter_context(nc.psum_tensor(name, shape, dt))

    def sem(name):
        return ctx.enter_context(nc.semaphore(name))

    return sb, ps, sem


def setup(nc, a, keep):
    with ExitStack() as ctx:
        sb, ps, sem = alloc(nc, ctx)
        src = sb("src", [P, E // P], I32)
        dst = sb("dst", [P, E // P], I32)
        bucket = sb("bucket", [P, E // P], I32)
        high = sb("high", [P, E // P], I32)
        low = sb("low", [P, E // P], I32)
        rcut = sb("rcut", [P, E // P])
        wf2_raw = sb("wf2_raw", [C, D])
        bf2_raw = sb("bf2_raw", [P, D])
        w_in = sb("w_in", [C, 2, C])
        w1_raw = sb("w1_raw", [C, 4, C])
        w2_raw = sb("w2_raw", [C, 2, C])
        ident = keep["ident"]

        s_edge = sem("s_edge")
        s_w_in = sem("s_w_in")
        s_w = sem("s_w")
        s_src = sem("s_src")
        s_shift = sem("s_shift")
        s_ready = sem("s_ready")
        s_id = sem("s_id")
        s_win = sem("s_win")

        block = ctx.enter_context(nc.Block())

        @block.sync
        def _(sp):
            sp.dma_start(src[:, :], a["src"]).then_inc(s_src, 16)
            sp.dma_start(dst[:, :], a["dst"]).then_inc(s_edge, 16)
            sp.dma_start(rcut[:, :], a["edge_weight"]).then_inc(s_edge, 16)
            sp.dma_start(w_in[:, 0, :], a["W_in2f_s"]).then_inc(s_w_in, 16)
            sp.dma_start(w_in[:, 1, :], a["W_in2f_v"]).then_inc(s_w_in, 16)

        @block.gpsimd
        def _(pool):
            pool.memset(ident[:, :], 0.0).then_inc(s_id, 1)
            pool.wait_ge(s_id, 1)
            pool.affine_select(out=ident[:, :], in_=ident[:, :], compare_op=ALU.not_equal, fill=1.0, base=0,
                               pattern=[[-1, C]], channel_multiplier=1).then_inc(s_id, 1)
            pool.iota(keep["win_iota_int"][:, :], pattern=[[1, WIN]], base=0, channel_multiplier=0).then_inc(s_win, 1)
            for name, pattern, mult in (("earlier", [[-1, C]], 1), ("lower", [[1, C]], -1)):
                pool.memset(keep[name][:, :], 1.0).then_inc(s_id, 1)
            pool.wait_ge(s_id, 4)
            for name, pattern, mult in (("earlier", [[-1, C]], 1), ("lower", [[1, C]], -1)):
                pool.affine_select(out=keep[name][:, :], in_=keep[name][:, :], compare_op=ALU.is_gt, fill=0.0, base=0,
                                   pattern=pattern, channel_multiplier=mult).then_inc(s_id, 1)
            pool.iota(keep["row_iota_int"][:, :], pattern=[[1, C]], base=0, channel_multiplier=0).then_inc(s_win, 1)
            pool.iota(keep["part_iota_int"][:, :], pattern=[[0, 1]], base=0, channel_multiplier=1).then_inc(s_win, 1)
            pool.iota(keep["ends_iota_int"][:, :, :], pattern=[[GE - 1, 2], [GE, NG]], base=0, channel_multiplier=0).then_inc(s_win, 1)
            pool.dma_start(keep["wf1"][0:NRBF, :], a["Wf1"]).then_inc(s_ready, 16)
            pool.dma_start(keep["wf1"][NRBF:NRBF + 1, :], a["bf1"]).then_inc(s_ready, 16)
            pool.wait_ge(s_ready, 32)

        @block.scalar
        def _(act):
            act.dma_start(wf2_raw[:, :], a["Wf2"][:, 0:D]).then_inc(s_w, 16)
            act.dma_start(bf2_raw[:, :], a["bf2"][:, 0:D].to_broadcast([P, D])).then_inc(s_w, 16)
            act.dma_start(w1_raw[:, 0:2, :], a["W1_s"].rearrange("(f h) c -> f h c", h=2)).then_inc(s_w, 16)
            act.dma_start(w1_raw[:, 2:4, :], a["W1_v"].rearrange("(f h) c -> f h c", h=2)).then_inc(s_w, 16)
            act.dma_start(w2_raw[:, 0, :], a["W2_s"]).then_inc(s_w, 16)
            act.dma_start(w2_raw[:, 1, :], a["W2_v"]).then_inc(s_w, 16)
            act.wait_ge(s_w_in, 32)
            nc.scalar.mul(keep["w_in"][:, :, :], w_in[:, :, :], RC)
            act.wait_ge(s_w, 16 * 6)
            for n, first in enumerate((0, 2 * C, 1, 2 * C + 1)):
                nc.scalar.copy(keep["wf2"][:, n, :], wf2_raw[:, first:first + 2 * C - 1:2])
                nc.scalar.copy(keep["bias"][:, n, :], bf2_raw[:, first:first + 2 * C - 1:2])
            for n, f in enumerate((Y0 * R2F, Y1 * R2F / float(np.sqrt(3.0)), Y1 * R2F, Y0 * R2F)):
                nc.scalar.mul(keep["w1"][:, n, :], w1_raw[:, n, :], f)
            nc.scalar.mul(keep["w2"][:, :, :], w2_raw[:, :, :], RC)

        @block.vector
        def _(dve):
            nc.vector.memset(keep["half"][:, :], 0.5)
            nc.vector.memset(keep["eps"][:, :], EPS)
            dve.wait_ge(s_win, 4)
            nc.vector.tensor_copy(keep["win_iota"][:, :], keep["win_iota_int"][:, :])
            nc.vector.tensor_copy(keep["row_iota"][:, :], keep["row_iota_int"][:, :])
            nc.vector.tensor_copy(keep["part_iota"][:, :], keep["part_iota_int"][:, :])
            nc.vector.tensor_copy(keep["ends_iota"][:, :, :], keep["ends_iota_int"][:, :, :])
            dve.wait_ge(s_id, 2)
            nc.vector.tensor_copy(keep["ident16"][:, :], ident[:, :])
            dve.wait_ge(s_src, 16)
            for out, shift in ((bucket, BUCKET_BITS), (high, BUCKET_BITS + LOW_BITS)):
                nc.vector.tensor_scalar(out[:, :], src[:, :], shift, None, ALU.arith_shift_right).then_inc(s_shift, 1)
            nc.vector.tensor_scalar(low[:, :], src[:, :], BUCKET_BITS, LOWS - 1, ALU.arith_shift_right,
                                    ALU.bitwise_and).then_inc(s_shift, 1)
            dve.wait_ge(s_shift, 3)
            nc.vector.tensor_copy(keep["keys"][:, :, 0], bucket[:, :])
            nc.vector.tensor_copy(keep["keys"][:, :, 1], high[:, :])
            for j in range(LOWS):
                nc.vector.tensor_scalar(keep["low_hot"][:, :, j], low[:, :], float(j), None, ALU.is_equal)
            nc.vector.tensor_copy(keep["edge"][:, :, SRC - C], src[:, :])
            dve.wait_ge(s_edge, 32)
            nc.vector.tensor_copy(keep["edge"][:, :, DST - C], dst[:, :])
            nc.vector.tensor_copy(keep["edge"][:, :, RCUT - C], rcut[:, :])


def count_edges(nc, a, keep):
    with ExitStack() as ctx:
        sb, ps, sem = alloc(nc, ctx)
        CT = 16
        STEPS = E // P // CT
        high_hot = [sb(f"high_hot{s}", [P, CT, HIGHS], BF16) for s in range(4)]
        counts = sb("counts", [HIGHS, LOWS, E // P])
        BLK = 8
        NB = E // P // BLK
        sum_to = [sb(f"sum_to{s}", [HIGHS, LOWS, NB]) for s in range(2)]
        away = sb("away", [P, CT, HIGHS], BF16)
        size = sb("away_size", [P, CT, HIGHS], BF16)
        one = sb("one", [P, 1])
        rvec = sb("rvec", [P, 3, E // P])
        rsq = sb("rsq", [P, 3, E // P])
        rnorm = sb("rnorm", [P, E // P])
        rinv = sb("rinv", [P, E // P])
        low4 = [sb(f"low4{s}", [P, CT, LOWS], BF16) for s in range(4)]
        total = sb("total", [HIGHS, LOWS])
        row_total = sb("row_total", [HIGHS, 1])
        start = sb("start", [HIGHS, LOWS])
        end = sb("end", [HIGHS, LOWS])
        ended = sb("ended", [HIGHS, 2, NG])
        ones = sb("ones", [HIGHS, P])
        first_bucket = sb("first_bucket", [1, NG])
        spread = sb("spread", [1, NG])
        widest = sb("widest", [1, 1], I32)
        scaled = sb("scaled", [1, 1], I32)
        widest_div = sb("widest_div", [1, 1], I32)
        ps_c = [ps(f"ps_c{s}", [HIGHS, 512]) for s in range(4)]
        ps_start = ps("ps_start", [HIGHS, 512])
        ps_base = ps("ps_base", [P, 512])
        hot_made = [Steps(sem(f"c_hot_made{s}")) for s in range(4)]
        away_made = Steps(sem("c_away_made"))
        away_size = Steps(sem("c_away_size"), 1)
        low_made = Steps(sem("c_low_made"))
        counted = Steps(sem("counted"), 4)
        stored = Steps(sem("stored"), 4)
        s_rvec = sem("c_rvec")
        s_sq = sem("c_sq")
        s_sqrt = sem("c_sqrt")
        s_rinv = sem("c_rinv")
        s_unit = sem("c_unit")
        s_gate = sem("c_gate")
        s_gate_p = sem("c_gate_p")
        s_one = sem("c_one")
        s_v = sem("c_v")
        s_row = sem("c_row")
        s_start = sem("c_start")
        s_ended = sem("c_ended")
        s_base = sem("c_base")
        block = ctx.enter_context(nc.Block())

        @block.sync
        def _(sp):
            sp.dma_start(rvec[:, :, :], a["edge_attr_3"]).then_inc(s_rvec, 16)

        @block.scalar
        def _(act):
            stored.start(act)
            away_size.start(act)

            def copy_low(step):
                counted.wait_apart(act, step.it - 4, s_gate)
                nc.scalar.copy(low4[step.slot][:, :, :], keep["low_hot"][:, bass.ds(step.g * CT, CT), :]).then_inc(low_made.sem, 1)

            def high_one_hots(step):
                away_made.wait_apart(act, step.use, s_gate)
                nc.scalar.activation(size[:, :, :], away[:, :, :], ACT.Abs).then_inc(away_size.sem, 1)
                away_size.wait_apart(act, step.use, s_gate)
                counted.wait_apart(act, step.it - 4, s_gate)
                nc.scalar.activation(high_hot[3][:, :, :], size[:, :, :], ACT.Relu, bias=one[:, :],
                                     scale=-1.0).then_inc(hot_made[3].sem, 1)

            def store(step):
                if step.later(2):
                    copy_low(step.later(2))
                if step.later(3) and step.later(3).slot == 3:
                    high_one_hots(step.later(3))
                counted.wait_apart(act, step.it, s_gate)
                nc.scalar.copy(counts[:, :, bass.ds(step.g * CT, CT)],
                               ps_c[step.slot][:, 0:CT * LOWS].rearrange("p (t l) -> p l t", l=LOWS)).then_inc(stored.sem, 1)
            act.wait_ge(s_one, 1)
            copy_low(item(0, 0, 0, STEPS))
            copy_low(item(0, 0, 1, STEPS))
            over(act, 0, STEPS, 3, store)
            act.wait_ge(s_sq, 3)
            nc.scalar.activation(rnorm[:, :], rsq[:, 0, :], ACT.Sqrt).then_inc(s_sqrt, 1)

        @block.gpsimd
        def _(pool):
            def distances(step):
                if step.slot == 3:
                    away_size.wait_apart(pool, step.use - 1, s_gate_p)
                    nc.gpsimd.tensor_tensor(away[:, :, :],
                                            keep["keys"][:, bass.ds(step.g * CT, CT), 1:2].to_broadcast([P, CT, HIGHS]),
                                            keep["row_iota"][0:P, 0:HIGHS].unsqueeze(1).to_broadcast([P, CT, HIGHS]),
                                            ALU.subtract).then_inc(away_made.sem, 1)
            over(pool, 0, STEPS, 3, distances)
            pool.wait_ge(s_rvec, 16)
            pool.tensor_tensor(rsq[:, :, :], rvec[:, :, :], rvec[:, :, :], ALU.mult).then_inc(s_sq, 1)
            pool.wait_ge(s_sq, 1)
            pool.tensor_tensor(rsq[:, 0, :], rsq[:, 0, :], rsq[:, 1, :], ALU.add).then_inc(s_sq, 1)
            pool.wait_ge(s_sq, 2)
            pool.tensor_tensor(rsq[:, 0, :], rsq[:, 0, :], rsq[:, 2, :], ALU.add).then_inc(s_sq, 1)
            pool.wait_ge(s_rinv, 1)
            for i in range(3):
                pool.tensor_tensor(keep["edge"][:, :, UNIT - C + i], rvec[:, i, :], rinv[:, :], ALU.mult).then_inc(s_unit, 1)

        @block.tensor
        def _(pe):
            counted.start(pe)

            def count(step):
                hot_made[step.slot].wait(pe, step.use)
                low_made.wait(pe, step.it)
                stored.wait(pe, step.it - 4)
                for t in range(CT):
                    last = nc.tensor.matmul(ps_c[step.slot][:, t * LOWS:(t + 1) * LOWS], high_hot[step.slot][:, t, :],
                                            low4[step.slot][:, t, :], start=True, stop=True)
                last.then_inc(counted.sem, 1)
            over(pe, 0, STEPS, 3, count)
            pe.wait_ge(s_row, 1)
            nc.tensor.matmul(ps_start[:, 0:1], keep["lower"][0:HIGHS, 0:HIGHS], row_total[:, :], start=True, stop=True).then_inc(s_start, 1)
            pe.wait_ge(s_ended, 1)
            nc.tensor.matmul(ps_base[:, 0:2 * NG], ones[:, :], ended[:, :, :].rearrange("p e g -> p (e g)"),
                             start=True, stop=True).then_inc(s_base, 1)

        @block.vector
        def _(dve):
            chain = [0]

            def link(ins):
                chain[0] += 1
                ins.then_inc(s_v, 1)
                dve.wait_ge(s_v, chain[0])

            nc.vector.memset(one[:, :], 1.0).then_inc(s_one, 1)
            nc.vector.memset(ones[:, :], 1.0)
            nc.vector.memset(ended[:, :, :], 0.0)

            def one_hots(step):
                if step.slot != 3:
                    counted.wait(dve, step.it - 4)
                    nc.vector.tensor_tensor(high_hot[step.slot][:, :, :],
                                            keep["keys"][:, bass.ds(step.g * CT, CT), 1:2].to_broadcast([P, CT, HIGHS]),
                                            keep["row_iota"][0:P, 0:HIGHS].unsqueeze(1).to_broadcast([P, CT, HIGHS]),
                                            ALU.is_equal).then_inc(hot_made[step.slot].sem, 1)
            over(dve, 0, STEPS, 3, one_hots)

            stored.wait(dve, STEPS - 1)
            c4 = counts[:, :, :].rearrange("p l (b j) -> p l b j", j=BLK)
            for j in range(BLK - 1):
                link(nc.vector.tensor_tensor(c4[:, :, :, j + 1], c4[:, :, :, j + 1], c4[:, :, :, j], ALU.add))
            nc.vector.memset(sum_to[0][:, :, 0:1], 0.0)
            link(nc.vector.tensor_copy(sum_to[0][:, :, 1:NB], c4[:, :, 0:NB - 1, BLK - 1]))
            reach, now = 1, 0
            while reach < NB:
                old, new = sum_to[now], sum_to[1 - now]
                nc.vector.tensor_copy(new[:, :, 0:reach], old[:, :, 0:reach])
                link(nc.vector.tensor_tensor(new[:, :, reach:NB], old[:, :, reach:NB], old[:, :, 0:NB - reach], ALU.add))
                reach, now = 2 * reach, 1 - now
            of_block = sum_to[now]
            dve.wait_ge(s_sqrt, 1)
            nc.vector.reciprocal(rinv[:, :], rnorm[:, :]).then_inc(s_rinv, 1)
            link(nc.vector.tensor_tensor(total[:, :], of_block[:, :, NB - 1], c4[:, :, NB - 1, BLK - 1], ALU.add))
            nc.vector.tensor_reduce(row_total[:, :], total[:, :], AX.X, ALU.add).then_inc(s_row, 1)
            dve.wait_ge(s_start, 1)
            link(nc.vector.tensor_copy(start[:, 0:1], ps_start[:, 0:1]))
            for j in range(1, LOWS):
                link(nc.vector.tensor_tensor(start[:, j:j + 1], start[:, j - 1:j], total[:, j - 1:j], ALU.add))
            link(nc.vector.tensor_tensor(end[:, :], start[:, :], total[:, :], ALU.add))
            for j in range(LOWS):
                ins = nc.vector.scalar_tensor_tensor(out=ended[:, :, :], in0=keep["ends_iota"][0:HIGHS, :, :], scalar=end[:, j:j + 1],
                                                     in1=ended[:, :, :], op0=ALU.is_ge, op1=ALU.add)
                if j < LOWS - 1:
                    link(ins)
            ins.then_inc(s_ended, 1)
            link(nc.vector.tensor_tensor(of_block[:, :, :], of_block[:, :, :], start[:, :].unsqueeze(2).to_broadcast([HIGHS, LOWS, NB]), ALU.add))
            p4 = keep["places"][:, :, :].rearrange("p l (b j) -> p l b j", j=BLK)
            nc.vector.tensor_copy(p4[:, :, :, 0], of_block[:, :, :])
            for j in range(LOWS):
                nc.vector.tensor_tensor(p4[:, j, :, 1:BLK], c4[:, j, :, 0:BLK - 1],
                                        of_block[:, j, :].unsqueeze(2).to_broadcast([HIGHS, NB, BLK - 1]), ALU.add)
            dve.wait_ge(s_base, 1)
            nc.vector.tensor_scalar(keep["base_all"][:, :], ps_base[:, 0:NG], float(BUCKET), None, ALU.mult)
            nc.vector.tensor_scalar(keep["base"][:, :], ps_base[0:1, 0:NG], float(BUCKET), None, ALU.mult)
            link(nc.vector.tensor_copy(first_bucket[:, :], ps_base[0:1, 0:NG]))
            link(nc.vector.tensor_tensor(spread[:, :], ps_base[0:1, NG:2 * NG], first_bucket[:, :], ALU.subtract))
            link(nc.vector.tensor_reduce(widest[:, :], spread[:, :], AX.X, ALU.max))
            link(nc.vector.tensor_scalar(scaled[:, :], widest[:, :], 683.0, None, ALU.mult))
            link(nc.vector.tensor_scalar(widest_div[:, :], scaled[:, :], 12, None, ALU.arith_shift_right))
            link(nc.vector.tensor_scalar(keep["passes"][:, :], widest_div[:, :], 1.0, None, ALU.add))
            assert WIN == 6 * BUCKET and N <= 2048 * BUCKET


def place_edges(nc, a, keep):
    with ExitStack() as ctx:
        sb, ps, sem = alloc(nc, ctx)
        fT = [sb(f"fT{s}", [NRBF + 1, GE]) for s in range(4)]
        size = [sb(f"size{s}", [P, TPG, C]) for s in range(2)]
        keys4 = [sb(f"keys4{s}", [P, TPG, 2], F16) for s in range(4)]
        keyf = [sb(f"keyf{s}", [P, TPG]) for s in range(4)]
        places4 = [sb(f"places4{s}", [HIGHS, TPG, LOWS]) for s in range(4)]
        split4 = [sb(f"split4{s}", [HIGHS, TPG, 2, LOWS], F16) for s in range(4)]
        high_T = [sb(f"high_T{s}", [HIGHS, GE], F16) for s in range(2)]
        same = [sb(f"same{s}", [P, TPG, P], BF16) for s in range(2)]
        rank = [sb(f"rank{s}", [P, TPG]) for s in range(2)]
        picked = [sb(f"picked{s}", [P, TPG, 2, LOWS]) for s in range(2)]
        first_parts = [sb(f"first_parts{s}", [P, TPG, 2]) for s in range(2)]
        first_of = [sb(f"first_of{s}", [P, TPG]) for s in range(2)]
        place = [sb(f"place{s}", [P, TPG], I32) for s in range(4)]
        rows = [sb(f"rows{s}", [P, TPG, ROW]) for s in range(4)]
        ps_h = [ps(f"p_h{s}", [P, TPG, C]) for s in range(2)]
        ps_key = [ps(f"ps_key{s}", [C, 512]) for s in range(2)]
        ps_high = [ps(f"ps_high{s}", [C, 512]) for s in range(2)]
        ps_look = ps("ps_look", [P, 512])
        ps_n = ps("ps_n", [C, 4, C])
        x_t = sb("x_t", [P, D])
        xn = sb("xn", [P, D])
        xT = sb("xT", [C, 4, P])
        table_rows = sb("table_rows", [P, D])
        stats = sb("stats", [P, 6])
        mv = sb("mv", [P, 2])
        std = sb("std", [P, 1])
        rstd = sb("rstd", [P, 1])

        s_f = [sem(f"p_f{s}") for s in range(4)]
        s_out = [sem(f"p_out{s}") for s in range(4)]
        s_gate = sem("p_gate")
        s_ones = sem("p_ones")
        keys_made = Steps(sem("keys_made"), 4)
        keyf_made = Steps(sem("keyf_made"))
        places_here = Steps(sem("places_here"))
        places_high = Steps(sem("places_high"))
        parts_made = Steps(sem("parts_made"))
        spread_out = Steps(sem("spread_out"), 4)
        high_made = Steps(sem("high_made"), 2)
        size_made = Steps(sem("size_made"))
        hidden_read = Steps(sem("hidden_read"), 2)
        exp_made = Steps(sem("exp_made"))
        log_made = Steps(sem("log_made"))
        ranked = Steps(sem("ranked"), 2)
        looked = Steps(sem("looked"), 4)
        picked_made = Steps(sem("picked_made"), 2)
        first_made = Steps(sem("first_made"))
        row_made = Steps(sem("row_made"), 2)

        s_x = sem("s_x")
        s_table = sem("s_table")
        s_gate_n = sem("n_gate")
        stat = Steps(sem("stat"))
        var = Steps(sem("var"))
        root = Steps(sem("root"))
        inv = Steps(sem("inv"))
        normed = Steps(sem("normed"))
        turned = Steps(sem("turned"), 1)
        copied = Steps(sem("copied"))
        projected = Steps(sem("projected"))
        drained = Steps(sem("drained"), 1)

        block = ctx.enter_context(nc.Block())

        @block.sync
        def _(sp):
            sp.wait_ge(s_ones, 1)

            def load(gr):
                spread_out.wait(sp, gr.it - 4)
                sp.dma_start(fT[gr.slot][0:NRBF, :], a["edge_attr_20"][:, bass.ds(gr.g * GE, GE)]).then_inc(s_f[gr.slot], 16)
            over(sp, 0, NG, 2, load)

        @block.gpsimd
        def _(pool):
            def scatter(gr):
                row_made.wait_apart(pool, gr.it, s_gate)
                for t in range(TPG):
                    pool.indirect_dma_start(a["sorted"], bass.IndirectOffsetOnAxis(ap=place[gr.slot][:, t:t + 1], axis=0),
                                            rows[gr.slot][:, t, :], None).then_inc(s_out[gr.slot], 16)
            over(pool, 0, NG, 2, scatter)
            for s in range(4):
                pool.wait_ge(s_out[s], 64 * (NG // 4))

        @block.scalar
        def _(act):
            hidden_read.start(act)
            drained.start(act)
            act.dma_start(x_t[:, :], a["x"][0:P, :]).then_inc(s_x, 16)
            nc.scalar.preload_act_table_set("natural_log_exp_and_others")

            def body(gr):
                b, c = size[gr.slot % 2], gr.slot % 2
                spread_out.wait(act, gr.it)
                row_made.wait(act, gr.it - 2)
                nc.scalar.activation(b[:, :, :], ps_h[c][:, :, :], ACT.Abs).then_inc(size_made.sem, 1)
                if not gr.fresh:
                    act.wait_ge(s_out[gr.slot], gr.use * 64)
                nc.scalar.activation(rows[gr.slot][:, :, 0:C], ps_h[c][:, :, :], ACT.Relu).then_inc(hidden_read.sem, 1)
                size_made.wait(act, gr.it)
                nc.scalar.activation(b[:, :, :], b[:, :, :], ACT.Exp, scale=-1.0).then_inc(exp_made.sem, 1)
                exp_made.wait(act, gr.it)
                nc.scalar.activation(b[:, :, :], b[:, :, :], ACT.Ln, scale=0.5, bias=keep["half"][0:P, 0:1]).then_inc(log_made.sem, 1)
                if gr.slot == 0 and not gr.fresh:
                    copy(gr.use - 1)
                if gr.slot == 1:
                    root_of(gr.use)
                if gr.slot == 2 and not gr.fresh:
                    drain(gr.use - 1)
                if gr.slot == 3 and gr.later(1):
                    normed.wait(act, gr.use)
                    act.dma_start(x_t[:, :], a["x"][bass.ds((gr.use + 1) * P, P), :]).then_inc(s_x, 16)

            def root_of(tile):
                var.wait(act, tile)
                nc.scalar.activation(std[:, 0:1], mv[:, 1:2], ACT.Sqrt, bias=keep["eps"][0:P, 0:1]).then_inc(root.sem, 1)
                nc.scalar.preload_act_table_set("natural_log_exp_and_others")

            def copy(tile):
                turned.wait(act, tile)
                nc.scalar.copy(xT[:, :, :], ps_n[:, :, 0:P]).then_inc(copied.sem, 1)

            def drain(tile):
                projected.wait(act, tile)
                if not (isinstance(tile, int) and tile == 0):
                    act.wait_ge(s_table, tile * 16)
                nc.scalar.copy(table_rows[:, :], ps_n[0:P, :, :].rearrange("p b c -> p (b c)")).then_inc(drained.sem, 1)
                drained.wait(act, tile)
                act.dma_start(a["table"][bass.ds(tile * P, P), :], table_rows[:, :]).then_inc(s_table, 16)

            over(act, 0, NG, 2, body, lead=4)
            copy(NT - 1)
            drain(NT - 1)
            act.wait_ge(s_table, 16 * NT)

        @block.tensor
        def _(pe):
            spread_out.start(pe)
            looked.start(pe)
            turned.start(pe)

            def spread(gr):
                pe.wait_ge(s_f[gr.slot], gr.use * 16 + 16)
                hidden_read.wait(pe, gr.it - 2)
                for t in range(TPG):
                    nc.tensor.matmul(ps_h[gr.slot % 2][:, t, :], fT[gr.slot][:, t * P:(t + 1) * P], keep["wf1"][:, :],
                                     start=True, stop=True)
                keys_made.wait(pe, gr.it)
                ranked.wait(pe, gr.it - 2)
                high_made.wait(pe, gr.it - 2)
                for i, out in enumerate((ps_key[gr.slot % 2], ps_high[gr.slot % 2])):
                    for t in range(TPG):
                        last = nc.tensor.matmul(out[:, t * P:(t + 1) * P], keys4[gr.slot][:, t, i:i + 1].to_broadcast([P, C]),
                                                keep["ident16"][0:P, 0:P], start=True, stop=True)
                last.then_inc(spread_out.sem, 1)

            def look_up(gr):
                high_made.wait(pe, gr.it)
                picked_made.wait(pe, gr.it - 1)
                for t in range(TPG):
                    last = nc.tensor.matmul(ps_look[:, t * 2 * LOWS:(t + 1) * 2 * LOWS], high_T[gr.slot % 2][:, t * P:(t + 1) * P],
                                            split4[gr.slot][:, t, :, :].rearrange("p h l -> p (h l)"), start=True, stop=True)
                last.then_inc(looked.sem, 1)

            spread(item(0, 0, 0, NG))

            def body(gr):
                if gr.later(1):
                    spread(gr.later(1))
                look_up(gr)
                if gr.slot == 1 and not gr.fresh:
                    project(gr.use - 1)
                if gr.slot == 3:
                    turn(gr.use)

            def turn(tile):
                normed.wait(pe, tile)
                drained.wait(pe, tile - 1)
                for b in range(4):
                    part = xn[:, 0:C] if b == 0 else xn[:, C + b - 1:C + b - 1 + 3 * C - 2:3]
                    last = nc.tensor.transpose(ps_n[:, b, 0:P], part, keep["ident"][0:P, 0:P])
                last.then_inc(turned.sem, 1)

            def project(tile):
                copied.wait(pe, tile)
                for b in range(4):
                    last = nc.tensor.matmul(ps_n[0:P, b, :], xT[:, b, :], keep["w_in"][:, min(b, 1), :], start=True, stop=True)
                last.then_inc(projected.sem, 1)

            over(pe, 0, NG, 2, body, lead=4)
            project(NT - 1)

        @block.vector
        def _(dve):
            for st in (keys_made, high_made, ranked, picked_made, row_made):
                st.start(dve)
            for s in range(4):
                ins = nc.vector.memset(fT[s][:, :], 1.0)
            ins.then_inc(s_ones, 1)

            def keys(gr):
                spread_out.wait(dve, gr.it - 4)
                looked.wait(dve, gr.it - 4)
                nc.vector.tensor_copy(places4[gr.slot][:, :, :],
                                      keep["places"][:, :, bass.ds(gr.g * TPG, TPG)].rearrange("p l t -> p t l")
                                      ).then_inc(places_here.sem, 1)
                nc.vector.tensor_copy(keyf[gr.slot][:, :], keep["keys"][:, bass.ds(gr.g * TPG, TPG), 0]).then_inc(keyf_made.sem, 1)
                places_here.wait(dve, gr.it)
                nc.vector.tensor_scalar(split4[gr.slot][:, :, 0, :], places4[gr.slot][:, :, :], 1.0 / 64.0, None,
                                        ALU.mult).then_inc(places_high.sem, 1)
                nc.vector.tensor_copy(keys4[gr.slot][:, :, :], keep["keys"][:, bass.ds(gr.g * TPG, TPG), :])
                places_high.wait(dve, gr.it)
                nc.vector.scalar_tensor_tensor(out=split4[gr.slot][:, :, 1, :], in0=split4[gr.slot][:, :, 0, :], scalar=-64.0,
                                               in1=places4[gr.slot][:, :, :], op0=ALU.mult, op1=ALU.add).then_inc(keys_made.sem, 1)

            def from_psum(gr):
                c = gr.slot % 2
                spread_out.wait(dve, gr.it)
                looked.wait(dve, gr.it - 2)
                nc.vector.tensor_scalar(high_T[c][:, :], ps_high[c][0:HIGHS, 0:GE], keep["part_iota"][0:HIGHS, 0:1], None,
                                        ALU.is_equal).then_inc(high_made.sem, 1)
                keyf_made.wait(dve, gr.it)
                row_made.wait(dve, gr.it - 2)
                for t in range(TPG):
                    ins = nc.vector.scalar_tensor_tensor(out=same[c][:, t, :], in0=ps_key[c][0:P, t * P:(t + 1) * P],
                                                         scalar=keyf[gr.slot][:, t:t + 1], in1=keep["earlier"][0:P, 0:P],
                                                         op0=ALU.is_equal, op1=ALU.mult, accum_out=rank[c][:, t:t + 1])
                ins.then_inc(ranked.sem, 1)

            def to_row(gr):
                c = gr.slot % 2
                looked.wait(dve, gr.it)
                nc.vector.tensor_tensor(picked[c][:, :, :, :],
                                        ps_look[:, 0:TPG * 2 * LOWS].rearrange("p (t h l) -> p t h l", h=2, l=LOWS),
                                        keep["low_hot"][:, bass.ds(gr.g * TPG, TPG), :].unsqueeze(2).to_broadcast([P, TPG, 2, LOWS]),
                                        ALU.mult).then_inc(picked_made.sem, 1)
                picked_made.wait(dve, gr.it)
                nc.vector.tensor_reduce(first_parts[c][:, :, :], picked[c][:, :, :, :], AX.X, ALU.add).then_inc(parts_made.sem, 1)
                log_made.wait(dve, gr.it)
                r = rows[gr.slot]
                nc.vector.tensor_tensor(r[:, :, 0:C], r[:, :, 0:C], size[c][:, :, :], ALU.add)
                parts_made.wait(dve, gr.it)
                nc.vector.scalar_tensor_tensor(out=first_of[c][:, :], in0=first_parts[c][:, :, 0], scalar=64.0,
                                               in1=first_parts[c][:, :, 1], op0=ALU.mult, op1=ALU.add).then_inc(first_made.sem, 1)
                nc.vector.tensor_copy(r[:, :, C:ROW], keep["edge"][:, bass.ds(gr.g * TPG, TPG), :])
                ranked.wait(dve, gr.it)
                first_made.wait(dve, gr.it)
                nc.vector.tensor_tensor(place[gr.slot][:, :], first_of[c][:, :], rank[c][:, :], ALU.add).then_inc(row_made.sem, 1)

            keys(item(0, 0, 0, NG))
            keys(item(0, 0, 1, NG))
            from_psum(item(0, 0, 0, NG))

            def body(gr):
                if gr.later(2):
                    keys(gr.later(2))
                if gr.later(1):
                    from_psum(gr.later(1))
                to_row(gr)
                if gr.slot == 0:
                    moments(gr.use)
                if gr.slot == 2:
                    normalise(gr.use)

            def moments(tile):
                dve.wait_ge(s_x, tile * 16 + 16)
                nc.vector.bn_stats(stats[:, :], x_t[:, :]).then_inc(stat.sem, 1)
                stat.wait_apart(dve, tile, s_gate_n)
                nc.vector.bn_aggr(mv[:, :], stats[:, :]).then_inc(var.sem, 1)

            def normalise(tile):
                root.wait(dve, tile)
                nc.vector.reciprocal(rstd[:, 0:1], std[:, 0:1]).then_inc(inv.sem, 1)
                inv.wait(dve, tile)
                turned.wait(dve, tile - 1)
                nc.vector.tensor_scalar(xn[:, :], x_t[:, :], mv[:, 0:1], rstd[:, 0:1], ALU.subtract, ALU.mult
                                        ).then_inc(normed.sem, 1)

            over(dve, 0, NG, 2, body, lead=4)


def sum_edges(nc, a, keep):
    with ExitStack() as ctx:
        sb, ps, sem = alloc(nc, ctx)
        rows = [sb(f"erows{s}", [P, TPG, ROW]) for s in range(4)]
        hT = [sb(f"hT{s}", [C, GE]) for s in range(2)]
        dst4 = [sb(f"dst4{s}", [P, TPG], I32) for s in range(4)]
        got = [sb(f"got{s}", [P, TPG, 4, C]) for s in range(4)]
        col = [sb(f"col{s}", [P, TPG]) for s in range(2)]
        cut = [sb(f"cut{s}", [P, TPG, 4]) for s in range(2)]
        eq = sb("eq", [P, TPG, WIN])
        vu = sb("vu", [P, TPG, 3, C])
        dot2 = sb("dot2", [P, TPG, C])
        dot = [sb(f"dot{s}", [P, TPG, C]) for s in range(2)]
        hot = [sb(f"hot{s}", [P, TPG, 4, WIN]) for s in range(2)]
        wb = [sb(f"wb{s}", [P, 4, C]) for s in range(2)]
        msg = [sb(f"msg{s}", [P, 6, C]) for s in range(TPG)]
        sums = [sb(f"sums{s}", [C, 8, 2, WIN]) for s in range(2)]
        ps_h = ps("ps_h", [C, 512])
        ps_w = [ps(f"ps_w{t}", [P, 4, C]) for t in range(TPG)]
        ps_sum = [ps(f"ps_sum{s}", [C, 8, WIN]) for s in range(2)]
        ps_out = ps("ps_out", [C, 4, 2, WIN])

        s_rows = [sem(f"s_rows{s}") for s in range(4)]
        s_got = [sem(f"s_got{s}") for s in range(4)]
        s_gate = sem("s_gate")
        s_base = sem("s_base")
        s_zero = sem("s_zero")
        s_zero_v = sem("s_zero_v")
        h_turned = Steps(sem("h_turned"), 2)
        h_done = Steps(sem("h_done"), 2)
        w_made = Steps(sem("w_made"), 8)
        biased = Steps(sem("biased"), 8)
        num_made = Steps(sem("num_made"), 4)
        dst_made = Steps(sem("dst_made"))
        eq_made = Steps(sem("eq_made"))
        hot_made = Steps(sem("hot_made"), 4)
        vu_made = Steps(sem("vu_made"), 4)
        dot_half = Steps(sem("dot_half"))
        dot_made = Steps(sem("dot_made"), 1)
        msg_made = Steps(sem("msg_made"), 16)
        sum_made = Steps(sem("sum_made"), 16)
        sum_copied = Steps(sem("sum_copied"), 2)
        out_made = Steps(sem("out_made"), 2)
        added = Steps(sem("added"), 1)

        block = ctx.enter_context(nc.Block())

        def passes(eng):
            return eng.Fori(0, eng.value_load(keep["passes"][0:1, 0:1], min_val=1, max_val=MAXP))

        @block.sync
        def _(sp):
            by_group = a["sorted"].rearrange("(g p t) r -> p g (t r)", p=P, t=TPG)
            with passes(sp) as k:
                def load(gr):
                    sum_made.wait(sp, (gr.it - 4) * TPG + 3)
                    sp.dma_start(rows[gr.slot][:, :, :].rearrange("p t r -> p (t r)"),
                                 by_group[:, bass.ds(gr.g, 1), :].rearrange("p a r -> p (a r)")).then_inc(s_rows[gr.slot], 16)
                over(sp, k, NG, 3, load)

        @block.gpsimd
        def _(pool):
            nc.gpsimd.memset(keep["node_sums"][:, 2:4, :], 0.0).then_inc(s_zero, 1)
            pool.wait_ge(s_zero, 1)
            dot_made.start(pool)

            def wait(steps, step):
                steps.wait_apart(pool, step, s_gate)

            with passes(pool) as k:
                def gather(gr):
                    wait(msg_made, (gr.it - 4) * TPG + 3)
                    pool.wait_ge(s_rows[gr.slot], gr.use * 16 + 16)
                    pool.sem_inc(s_gate, 1)
                    pool.tensor_copy(dst4[gr.slot][:, :], rows[gr.slot][:, :, DST]).then_inc(dst_made.sem, 1)
                    wait(dst_made, gr.it)
                    for t in range(TPG):
                        pool.indirect_dma_start(got[gr.slot][:, t, :, :].rearrange("p b c -> p (b c)"), None, a["table"],
                                                bass.IndirectOffsetOnAxis(ap=dst4[gr.slot][:, t:t + 1], axis=0)
                                                ).then_inc(s_got[gr.slot], 16)

                def dots(gr):
                    wait(vu_made, gr.it)
                    wait(msg_made, (gr.it - 2) * TPG + 3)
                    pool.tensor_tensor(dot2[:, :, :], vu[:, :, 0, :], vu[:, :, 1, :], ALU.add).then_inc(dot_half.sem, 1)
                    wait(dot_half, gr.it)
                    pool.tensor_tensor(dot[gr.slot % 2][:, :, :], dot2[:, :, :], vu[:, :, 2, :], ALU.add).then_inc(dot_made.sem, 1)

                g0 = item(k, 0, 0, NG)
                gather(g0)
                gather(g0.later(1))
                dots(g0)

                def body(gr):
                    if gr.later(2):
                        gather(gr.later(2))
                    if gr.later(1):
                        dots(gr.later(1))
                over(pool, k, NG, 2, body)

        @block.scalar
        def _(act):
            vu_made.start(act)
            h_done.start(act)
            sum_copied.start(act)
            with passes(act) as k:
                def copy_hidden(gr):
                    h_turned.wait(act, gr.it)
                    w_made.wait(act, (gr.it - 2) * TPG + 3)
                    nc.scalar.copy(hT[gr.slot % 2][:, :], ps_h[:, 0:GE]).then_inc(h_done.sem, 1)

                def turn(gr):
                    act.wait_ge(s_got[gr.slot], gr.use * 64 + 64)
                    act.wait_ge(s_rows[gr.slot], gr.use * 16 + 16)
                    dot_made.wait(act, gr.it - 1)
                    for t in range(TPG):
                        for i in range(3):
                            last = nc.scalar.activation(vu[:, t, i, :], got[gr.slot][:, t, 1 + i, :], ACT.Copy,
                                                        scale=rows[gr.slot][:, t, UNIT + i:UNIT + i + 1])
                    last.then_inc(vu_made.sem, 1)

                def copy_sums(after):
                    sum_made.wait(act, (after.it - 1) * TPG + 3)
                    out_made.wait(act, after.pair(-1) - 2)
                    of = (after.slot - 1) % 4
                    nc.scalar.copy(sums[of // 2][:, :, of % 2, :], ps_sum[of % 2][:, :, :]).then_inc(sum_copied.sem, 1)

                g0 = item(k, 0, 0, NG)
                turn(g0)
                copy_hidden(g0)

                def body(gr):
                    nxt = gr.later(1)
                    if nxt:
                        copy_hidden(nxt)
                    if not gr.first:
                        copy_sums(gr)
                    if nxt:
                        turn(nxt)
                over(act, k, NG, 2, body)
                copy_sums(item(k, NG // 4, 0, NG))

        @block.tensor
        def _(pe):
            h_turned.start(pe)
            w_made.start(pe)
            sum_made.start(pe)
            out_made.start(pe)
            with passes(pe) as k:
                def hidden(gr):
                    pe.wait_ge(s_rows[gr.slot], gr.use * 16 + 16)
                    h_done.wait(pe, gr.it - 1)
                    for t in range(TPG):
                        last = nc.tensor.transpose(ps_h[:, t * P:(t + 1) * P], rows[gr.slot][:, t, 0:C], keep["ident"][0:P, 0:P])
                    last.then_inc(h_turned.sem, 1)

                def weights(gr, t):
                    if t == 0:
                        h_done.wait(pe, gr.it)
                    biased.wait(pe, (gr.it - 1) * TPG + t)
                    w = ps_w[t][:, :, :].rearrange("p b c -> p (b c)")
                    nc.tensor.matmul(w, hT[gr.slot % 2][:, t * P:(t + 1) * P],
                                     keep["wf2"][:, :, :].rearrange("p b c -> p (b c)"),
                                     start=True, stop=True).then_inc(w_made.sem, 1)

                def add_up(slot, it, t):
                    msg_made.wait(pe, it * TPG + t)
                    if t == 0:
                        hot_made.wait(pe, it)
                        sum_copied.wait(pe, it - 2)
                    m, o, acc = msg[t], hot[slot % 2], ps_sum[slot % 2]
                    for b, cols, hots in ((0, slice(0, 1), slice(0, 1)), (1, slice(2, 5), slice(1, 4)),
                                          (2, slice(1, 2), slice(0, 1)), (3, slice(5, 6), slice(0, 1)),
                                          (4, slice(6, 7), slice(0, 1)), (5, slice(7, 8), slice(0, 1))):
                        last = nc.tensor.matmul(acc[:, cols, :].rearrange("p b w -> p (b w)"), m[:, b, :],
                                                o[:, t, hots, :].rearrange("p b w -> p (b w)"),
                                                start=(t == 0 and b == 0), stop=(t == TPG - 1 and b == 5),
                                                skip_group_check=True)
                    last.then_inc(sum_made.sem, 1)

                def through_w1(after):
                    sum_copied.wait(pe, after.it - 1)
                    added.wait(pe, after.it - 3)
                    s = sums[(after.slot - 1) % 4 // 2]
                    w1 = keep["w1"]

                    def flat(t):
                        return t.rearrange("p b g w -> p (b g w)")

                    nc.tensor.matmul(flat(ps_out[:, 0:1]), w1[:, 0, :], flat(s[:, 0:1]), start=True, stop=False, skip_group_check=True)
                    nc.tensor.matmul(flat(ps_out[:, 0:1]), w1[:, 1, :], flat(s[:, 1:2]), start=False, stop=False, skip_group_check=True)
                    nc.tensor.matmul(flat(ps_out[:, 1:4]), w1[:, 2, :], flat(s[:, 2:5]), start=False, stop=False, skip_group_check=True)
                    nc.tensor.matmul(flat(ps_out[:, 1:4]), w1[:, 3, :], flat(s[:, 5:8]), start=False, stop=True,
                                     skip_group_check=True).then_inc(out_made.sem, 1)

                hidden(item(k, 0, 0, NG))

                def body(gr):
                    for t in range(TPG):
                        weights(gr, t)
                        if t >= 2:
                            add_up(gr.slot, gr.it, t - 2)
                        elif not gr.first:
                            add_up(gr.slot + 1, gr.it - 1, t + 2)
                        if t == 0 and gr.later(1):
                            hidden(gr.later(1))
                        if t == 2 and gr.slot % 2 == 0 and not gr.first:
                            through_w1(gr)
                over(pe, k, NG, 2, body)
                for t in (2, 3):
                    add_up(1, k * NG + NG - 1, t)
                through_w1(item(k, NG // 4, 0, NG))

        @block.vector
        def _(dve):
            for s in (biased, num_made, hot_made, msg_made, added):
                s.start(dve)
            nc.vector.memset(keep["node_sums"][:, 0:2, :], 0.0).then_inc(s_zero_v, 1)
            dve.wait_ge(s_zero_v, 1)
            dve.wait_ge(s_zero, 1)
            with passes(dve) as k:
                def numbers(gr):
                    dve.wait_ge(s_rows[gr.slot], gr.use * 16 + 16)
                    c, r = gr.slot % 2, rows[gr.slot]
                    nc.vector.tensor_copy(cut[c][:, :, 0:1], r[:, :, RCUT:RCUT + 1])
                    nc.vector.tensor_tensor(cut[c][:, :, 1:4], r[:, :, UNIT:UNIT + 3], r[:, :, RCUT:RCUT + 1].to_broadcast([P, TPG, 3]),
                                            ALU.mult)
                    nc.vector.tensor_tensor(col[c][:, :], r[:, :, SRC], keep["base_all"][:, bass.ds(gr.g, 1)].to_broadcast([P, TPG]),
                                            ALU.subtract).then_inc(num_made.sem, 1)

                def one_hots(gr):
                    num_made.wait(dve, gr.it)
                    nc.vector.tensor_tensor(eq[:, :, :], keep["win_iota"][:, :].unsqueeze(1).to_broadcast([P, TPG, WIN]),
                                            col[gr.slot % 2][:, :].unsqueeze(2).to_broadcast([P, TPG, WIN]),
                                            ALU.is_equal).then_inc(eq_made.sem, 1)

                def scale_hots(gr):
                    eq_made.wait(dve, gr.it)
                    sum_made.wait(dve, (gr.it - 2) * TPG + 3)
                    c = gr.slot % 2
                    nc.vector.tensor_tensor(hot[c][:, :, :, :], eq[:, :, :].unsqueeze(2).to_broadcast([P, TPG, 4, WIN]),
                                            cut[c][:, :, :].unsqueeze(3).to_broadcast([P, TPG, 4, WIN]),
                                            ALU.mult).then_inc(hot_made.sem, 1)

                def add_bias(gr, t):
                    w_made.wait(dve, gr.it * TPG + t)
                    msg_made.wait(dve, gr.it * TPG + t - 2)
                    nc.vector.tensor_tensor(wb[t % 2][:, :, :], ps_w[t][:, :, :], keep["bias"][:, :, :],
                                            ALU.add).then_inc(biased.sem, 1)

                def messages(gr, t):
                    if t == 0:
                        dve.wait_ge(s_got[gr.slot], gr.use * 64 + 64)
                        dot_made.wait(dve, gr.it)
                    biased.wait(dve, gr.it * TPG + t)
                    sum_made.wait(dve, (gr.it - 1) * TPG + t)
                    m, w, x = msg[t], wb[t % 2], got[gr.slot]
                    nc.vector.tensor_tensor(m[:, 0:2, :], w[:, 0:2, :], x[:, t, 0:1, :].to_broadcast([P, 2, C]), ALU.mult)
                    nc.vector.tensor_tensor(m[:, 2, :], w[:, 2, :], dot[gr.slot % 2][:, t, :], ALU.mult)
                    nc.vector.tensor_tensor(m[:, 3:6, :], w[:, 3:4, :].to_broadcast([P, 3, C]), x[:, t, 1:4, :],
                                            ALU.mult).then_inc(msg_made.sem, 1)

                def add_windows(after):
                    for n in range(2):
                        g = after.g - 2 + n
                        at = keep["base"][0:1, g:g + 1] if isinstance(g, int) else keep["base"][0:1, bass.ds(g, 1)]
                        start = dve.value_load(at, min_val=0, max_val=N)
                        if n == 0:
                            out_made.wait(dve, after.pair() - 1)
                        added.wait(dve, after.it - 3 + n)
                        part = keep["node_sums"][:, :, bass.ds(start, WIN)]
                        nc.vector.tensor_tensor(part, ps_out[:, :, n, :], part, ALU.add).then_inc(added.sem, 1)

                g0 = item(k, 0, 0, NG)
                numbers(g0)
                one_hots(g0)
                scale_hots(g0)

                def body(gr):
                    for t in range(TPG):
                        add_bias(gr, t)
                        if t == TPG - 1 and gr.slot % 2 == 0 and not gr.first:
                            add_windows(gr)
                        if t < 3 and gr.later(1):
                            (numbers, one_hots, scale_hots)[t](gr.later(1))
                        messages(gr, t)
                over(dve, k, NG, 2, body)
                add_windows(item(k, NG // 4, 0, NG))
                e, b = keep["base_all"], keep["base"]
                nc.vector.tensor_scalar(e[:, :], e[:, :], float(WIN), None, ALU.add).then_inc(s_base, 1)
                nc.vector.tensor_scalar(b[:, :], b[:, :], float(WIN), float(N), ALU.add, ALU.min).then_inc(s_base, 1)
                dve.wait_ge(s_base, k * 2 + 2)


NCH = 25
TPC = NT // NCH
NC_ = TPC * P
SOFT = 5 * NC_
GE_DIM = 160
HI = GE_DIM - C
RESULT, CARRY_OUT = 100, 101
FLAG = 105
FLAG_IN = 35
NIB = 16
OUTPUT = 128
NF = 9
N_FIRST, N_WEIGHTS = 20, 24
PARTS = 3
STEP = 32
KF = STEP * PARTS


def finish(nc, a, keep):
    with ExitStack() as ctx:
        sb, ps, sem = alloc(nc, ctx)
        x = sb("x", [P, 4, TPC, D])
        xl = sb("xl", [P, 4, TPC, D])
        st = [sb(f"st{s}", [C, 4, NC_]) for s in range(4)]
        soft = [sb(f"fsoft{s}", [C, SOFT]) for s in range(2)]
        stats = sb("fstats", [P, 4, TPC, 6])
        mv = sb("fmv", [P, 4, TPC, 2])
        std = sb("fstd", [P, 4, TPC])
        rstd = sb("frstd", [P, 4, TPC])
        eps = sb("feps", [P, 1])
        weight16 = sb("weight16", [P, 4, 16])
        iota16 = sb("iota16", [P, 16])
        iota16_int = sb("iota16_int", [P, 16], I32)
        score = sb("score", [P, 2, TPC, 4, 16])
        best = sb("best", [P, 2, TPC, 4])
        any16 = sb("any16", [P, 2, TPC, 4])
        flags = sb("flags", [P, 2, TPC, 3])
        feats = sb("feats", [P, 2, TPC, 2, NF])
        feats3 = sb("feats3", [P, 2, TPC, 2, PARTS, STEP])
        fpart = sb("fpart", [P, 2, PARTS, TPC, 2], BF16)
        frest = sb("frest", [P, 2, 2, TPC, 2])
        mask = sb("mask", [P, 4, TPC, 4])
        fT = sb("ffT", [KF, 2, 4 * P], BF16)
        h1 = sb("h1", [C, 3, 4 * P])
        h2 = sb("h2", [C, 2, 3, 4 * P])
        b3 = sb("b3", [P, 4])
        yT = sb("yT", [4, 2, 4 * P])
        y = sb("y", [P, TPC, 2, 4])
        yy = sb("yy", [P, TPC, 2, 4])
        ym = sb("ym", [P, TPC, 2, 2])
        yr = sb("yr", [P, TPC, 2])
        yc = sb("yc", [P, TPC])
        hot = sb("fhot", [P, TPC, 2, 16])
        l1_raw = sb("l1_raw", [NF, 3, C])
        l1_rest = sb("l1_rest", [NF, 2, 3, C])
        l1_part = sb("l1_part", [NF, PARTS, 3, C], BF16)
        l1 = sb("l1", [KF, 3, C], BF16)
        l2 = sb("l2", [C, 7, C])
        l3 = sb("l3", [C, 3, 4])
        b2 = sb("b2", [C, 3])
        ps_x = [ps(f"ps_x{t}", [P, 4, C]) for t in range(TPC)]
        ps_f = ps("ps_f", [C, 512])
        ps_l = [ps(f"ps_l{b}", [C, 512]) for b in range(4)]
        ps_y = ps("ps_y", [P, 512])
        y_ps = ps_y[:, 0:TPC * 2 * 4].rearrange("p (t q o) -> p t q o", q=2, o=4)

        s_zero = sem("f_zero")
        s_w1 = sem("f_w1")
        s_w = sem("f_w")
        s_parts = sem("f_parts")
        s_l1 = sem("f_l1")
        s_iota = sem("f_iota")
        s_gate = sem("f_gate")
        s_gate_v = sem("f_gate_v")
        s_v = sem("f_v")
        s_x = [sem(f"f_x{s}") for s in range(4)]
        s_out = [sem(f"f_out{s}") for s in range(4)]
        sums_here = Steps(sem("sums_here"))
        s_abs = sem("dve_abs")
        s_exp = sem("act_exp")
        s_ln = sem("act_ln")
        s_soft = sem("soft_done")
        w2_done = Steps(sem("w2_done"), 4)
        x1_done = Steps(sem("x1_done"), 1)
        stat = Steps(sem("f_stat"))
        var = Steps(sem("f_var"))
        root = Steps(sem("f_root"))
        inv = Steps(sem("f_inv"))
        normed = Steps(sem("f_normed"))
        feats_done = Steps(sem("feats_done"))
        turned = Steps(sem("f_turned"), 2)
        f_copied = Steps(sem("f_copied"), 1)
        layer_made = Steps(sem("layer_made"), 14)
        layer_read = Steps(sem("layer_read"), 7)
        l3_done = Steps(sem("l3_done"), 2)
        y_read = Steps(sem("y_read"), 1)
        added = Steps(sem("f_added"))
        done = Steps(sem("f_done"))
        dve_front = Steps(sem("dve_front"))
        dve_tail = Steps(sem("dve_tail"))

        s_hot = sem("f_hot")
        s_hot_scaled = sem("f_hot_scaled")

        OUTS = 7

        def bank(ch, n):
            return ps_l[(ch.slot * OUTS + n) % 4]

        block = ctx.enter_context(nc.Block())
        rows_of = a["x"].rearrange("(n t p) d -> n p t d", t=TPC, p=P)
        out_rows = a["out"].rearrange("(n t p) d -> n p t d", t=TPC, p=P)

        @block.sync
        def _(sp):
            for s in range(4):
                sp.dma_start(x[:, s, :, :], rows_of[s]).then_inc(s_x[s], 16)
            sp.wait_ge(s_zero, 1)
            wa, ws = a["Wa"], a["Ws"]
            first, weights = [], []
            for w, col in ((wa, (0, 0, C, 2, 0)), (ws, (1, 1, C, 2, HI))):
                first_block, _, _, rest_block, at = col
                for r, rows in ((0, slice(0, 2)),) + tuple((3 + 2 * n, slice(FLAG_IN, FLAG_IN + 2)) for n in range(PARTS)):
                    first.append((l1_raw[r:r + 2, first_block, :], w[0, rows, 0:C]))
                    first.append((l1_raw[r:r + 2, rest_block, at:at + HI], w[0, rows, C:GE_DIM]))
            for m, bias in ((0, a["ba"]), (1, a["bs"])):
                first.append((l1_raw[2:3, m, :], bias[0:1, 0:C]))
                first.append((l1_raw[2:3, 2, m * HI:(m + 1) * HI], bias[0:1, C:GE_DIM]))
                weights.append((b2[:, m:m + 1], bias[1:2, 0:C].rearrange("a c -> c a")))
                weights.append((b2[m * HI:(m + 1) * HI, 2:3], bias[1:2, C:GE_DIM].rearrange("a c -> c a")))
                for o, q in ((0, RESULT), (2, CARRY_OUT)):
                    weights.append((b3[:, o + m:o + m + 1], bias[2:3, q:q + 1].to_broadcast([P, 1])))
            for m, w in ((0, wa), (1, ws)):
                weights.append((l2[:, 2 * m, :], w[1, 0:C, 0:C]))
                weights.append((l2[m * HI:(m + 1) * HI, 2 * m + 1, :], w[1, C:GE_DIM, 0:C]))
                weights.append((l2[:, 4 + m, m * HI:(m + 1) * HI], w[1, 0:C, C:GE_DIM]))
                weights.append((l2[m * HI:(m + 1) * HI, 6, m * HI:(m + 1) * HI], w[1, C:GE_DIM, C:GE_DIM]))
                for o, q in ((0, RESULT), (2, CARRY_OUT)):
                    weights.append((l3[:, m, o + m:o + m + 1], w[2, 0:C, q:q + 1]))
                    weights.append((l3[m * HI:(m + 1) * HI, 2, o + m:o + m + 1], w[2, C:GE_DIM, q:q + 1]))
            with nc.allow_non_contiguous_dma(reason="a few columns of the weights"):
                for dst, src in first:
                    sp.dma_start(dst, src).then_inc(s_w1, 16)
                for dst, src in weights:
                    sp.dma_start(dst, src).then_inc(s_w, 16)
            assert (len(first), len(weights)) == (N_FIRST, N_WEIGHTS)
            sp.wait_ge(s_parts, 1)
            for n in range(PARTS):
                sp.dma_start(l1[n * STEP:n * STEP + NF, :, :], l1_part[:, n, :, :]).then_inc(s_l1, 16)

            def move(ch):
                done.wait(sp, ch.it)
                sp.dma_start(out_rows[bass.ds(ch.g, 1)].rearrange("a p t d -> (a p) t d") if not isinstance(ch.g, int) else out_rows[ch.g],
                             x[:, ch.slot, :, :]).then_inc(s_out[ch.slot], 16)
                nxt = ch.later(4)
                if nxt:
                    sp.wait_ge(s_out[ch.slot], ch.use * 16 + 16)
                    sp.dma_start(x[:, ch.slot, :, :],
                                 rows_of[bass.ds(nxt.g, 1)].rearrange("a p t d -> (a p) t d") if not isinstance(nxt.g, int) else rows_of[nxt.g]
                                 ).then_inc(s_x[ch.slot], 16)
            over(sp, 0, NCH, 4, move)
            for s in range(4):
                sp.wait_ge(s_out[s], 16 * (NCH // 4 + (s < NCH % 4)))

        @block.gpsimd
        def _(pool):
            def wait(steps, step):
                steps.wait_apart(pool, step, s_gate)

            pool.iota(iota16_int[:, :], pattern=[[1, 16]], base=0, channel_multiplier=0).then_inc(s_iota, 1)

            def fetch(ch):
                wait(w2_done, ch.it - 4)
                pool.tensor_copy(st[ch.slot][:, :, :], keep["node_sums"][:, :, bass.ds(ch.g * NC_, NC_)]).then_inc(sums_here.sem, 1)

            def body(ch):
                if ch.later(3):
                    fetch(ch.later(3))
                wait(normed, ch.it)
                pool.tensor_tensor(x[:, ch.slot, :, :], x[:, ch.slot, :, :], xl[:, ch.slot, :, :], ALU.add).then_inc(added.sem, 1)
            pool.wait_ge(s_soft, 1)
            for s in range(3):
                fetch(item(0, 0, s, NCH))
            pool.wait_ge(s_soft, N // SOFT)
            over(pool, 0, NCH, 4, body)

        @block.scalar
        def _(act):
            f_copied.start(act)
            layer_read.start(act)

            nc.scalar.preload_act_table_set("natural_log_exp_and_others")
            for n in range(N // SOFT):
                b = soft[n % 2]
                act.wait_ge(s_abs, n + 1)
                nc.scalar.activation(b[:, :], b[:, :], ACT.Exp, scale=-1.0).then_inc(s_exp, 1)
                act.wait_ge(s_exp, n + 1)
                nc.scalar.activation(b[:, :], b[:, :], ACT.Ln, scale=0.5, bias=keep["half"][:, 0:1]).then_inc(s_ln, 1)

            def roots(ch):
                var.wait(act, ch.it)
                nc.scalar.activation(std[:, ch.slot, :], mv[:, ch.slot, :, 1], ACT.Sqrt, bias=eps[:, 0:1]).then_inc(root.sem, 1)

            def copy_feats(ch):
                turned.wait(act, ch.it)
                layer_made.wait(act, (ch.it - 2) * OUTS + 2)
                nc.scalar.copy(fT[:, ch.slot % 2, :], ps_f[0:KF, 0:4 * P]).then_inc(f_copied.sem, 1)

            def relus1(ch):
                layer_made.wait(act, (ch.it - 1) * OUTS + 6)
                for b in range(3):
                    layer_made.wait(act, ch.it * OUTS + b)
                    nc.scalar.activation(h1[:, b, :], bank(ch, b)[:, 0:4 * P], ACT.Relu).then_inc(layer_read.sem, 1)

            def copy_y(ch, n=3):
                l3_done.wait(act, ch.it - 3)
                layer_made.wait(act, ch.it * OUTS + n)
                nc.scalar.copy(yT[:, (ch.slot - 1) % 2, :], bank(ch, n)[0:4, 0:4 * P]).then_inc(layer_read.sem, 1)

            def relus2(ch):
                layer_made.wait(act, (ch.it - 1) * OUTS + 3)
                for b in range(3):
                    layer_made.wait(act, ch.it * OUTS + 4 + b)
                    nc.scalar.activation(h2[:, ch.slot % 2, b, :], bank(ch, 4 + b)[:, 0:4 * P], ACT.Relu,
                                         bias=b2[:, b:b + 1]).then_inc(layer_read.sem, 1)

            for s in range(2):
                roots(item(0, 0, s, NCH))
            copy_feats(item(0, 0, 0, NCH))

            def body(ch):
                relus1(ch)
                if ch.later(1):
                    copy_feats(ch.later(1))
                if ch.first:
                    layer_read.wait(act, 2)
                    act.sem_inc(layer_read.sem, 1)
                else:
                    copy_y(ch)
                if ch.later(2):
                    roots(ch.later(2))
                relus2(ch)
            act.wait_ge(s_w, 16 * N_WEIGHTS)
            over(act, 0, NCH, 4, body)
            copy_y(item(0, NCH // 4, NCH % 4, NCH), 0)

        @block.tensor
        def _(pe):
            for s in (w2_done, turned, layer_made, l3_done):
                s.start(pe)

            def through_w2(ch):
                sums_here.wait(pe, ch.it)
                x1_done.wait(pe, ch.it - 1)
                for t in range(TPC):
                    for b in range(4):
                        last = nc.tensor.matmul(ps_x[t][:, b, :], st[ch.slot][:, b, t * P:(t + 1) * P],
                                                keep["w2"][:, min(b, 1), :], start=True, stop=True)
                last.then_inc(w2_done.sem, 1)

            def turn(ch):
                feats_done.wait(pe, ch.it)
                f_copied.wait(pe, ch.it - 1)
                for q in range(2):
                    for t in range(TPC):
                        last = nc.tensor.transpose(ps_f[0:KF, (q * TPC + t) * P:(q * TPC + t + 1) * P],
                                                   feats3[:, ch.slot % 2, t, q, :, :].rearrange("p r f -> p (r f)"), keep["ident"][0:P, 0:P])
                last.then_inc(turned.sem, 1)

            def layer1(ch):
                f_copied.wait(pe, ch.it)
                for b in range(3):
                    layer_read.wait(pe, ch.it * OUTS + b - 4)
                    nc.tensor.matmul(bank(ch, b)[:, 0:4 * P], l1[:, b, :], fT[:, ch.slot % 2, :],
                                     start=True, stop=True).then_inc(layer_made.sem, 1)

            def layer2(ch, b):
                layer_read.wait(pe, ch.it * OUTS + 2)
                ins = (((0, 0), (2, 1)), ((1, 2), (2, 3)), ((0, 4), (1, 5), (2, 6)))[b]
                for n, (i, w) in enumerate(ins):
                    last = nc.tensor.matmul(bank(ch, 4 + b)[:, 0:4 * P], l2[:, w, :], h1[:, i, :],
                                            start=(n == 0), stop=(n == len(ins) - 1))
                last.then_inc(layer_made.sem, 1)

            def layer3(ch, n=3):
                layer_read.wait(pe, ch.it * OUTS - 1)
                for b in range(3):
                    last = nc.tensor.matmul(bank(ch, n)[0:4, 0:4 * P], l3[:, b, :], h2[:, (ch.slot - 1) % 2, b, :],
                                            start=(b == 0), stop=(b == 2))
                last.then_inc(layer_made.sem, 1)

            def turn_back(ch, n=3):
                layer_read.wait(pe, ch.it * OUTS + n)
                y_read.wait(pe, ch.it - 2)
                for q in range(2):
                    for t in range(TPC):
                        at = (q * TPC + t) * P
                        last = nc.tensor.matmul(y_ps[:, t, q, :], yT[:, (ch.slot - 1) % 2, at:at + P], keep["ident"][0:4, 0:4],
                                                start=True, stop=True)
                last.then_inc(l3_done.sem, 1)

            def body(ch):
                layer1(ch)
                if ch.later(2):
                    through_w2(ch.later(2))
                if ch.later(1):
                    turn(ch.later(1))
                if ch.first:
                    layer_made.wait(pe, 2)
                    pe.sem_inc(layer_made.sem, 1)
                else:
                    layer3(ch)
                layer2(ch, 0)
                if not ch.first:
                    turn_back(ch)
                layer2(ch, 1)
                layer2(ch, 2)

            through_w2(item(0, 0, 0, NCH))
            through_w2(item(0, 0, 1, NCH))
            pe.wait_ge(s_zero, 2)
            turn(item(0, 0, 0, NCH))
            pe.wait_ge(s_w, 16 * N_WEIGHTS)
            pe.wait_ge(s_l1, 16 * PARTS)
            over(pe, 0, NCH, 4, body)
            layer3(item(0, NCH // 4, NCH % 4, NCH), 0)
            turn_back(item(0, NCH // 4, NCH % 4, NCH), 0)

        @block.vector
        def _(dve):
            for s in (x1_done, y_read):
                s.start(dve)
            for t in (l1_raw, l1, l2, l3):
                nc.vector.memset(t[:, :, :], 0.0)
            nc.vector.memset(b2[:, :], 0.0).then_inc(s_zero, 1)
            nc.vector.memset(feats[:, :, :, :, :], 1.0)
            nc.vector.memset(eps[:, :], EPS)
            nc.vector.memset(feats3[:, :, :, :, :, :], 0.0).then_inc(s_zero, 1)
            dve.wait_ge(s_zero, 2)
            def sizes(n):
                nc.vector.tensor_scalar(soft[n % 2][:, :].bitcast(I32), block_of(n).bitcast(I32), 0x7FFFFFFF, None,
                                        ALU.bitwise_and).then_inc(s_abs, 1)

            def block_of(n):
                return keep["node_sums"][:, 0, n * SOFT:(n + 1) * SOFT]

            sizes(0)
            sizes(1)
            for n in range(N // SOFT):
                v = block_of(n)
                dve.wait_ge(s_ln, n + 1)
                nc.vector.scalar_tensor_tensor(out=v, in0=v, scalar=0.0, in1=soft[n % 2][:, :], op0=ALU.max,
                                               op1=ALU.add).then_inc(s_soft, 1)
                if n + 2 < N // SOFT:
                    dve.wait_ge(s_soft, n + 1)
                    sizes(n + 2)
            dve.wait_ge(s_w1, 16 * N_FIRST)
            left = l1_raw[:, :, :]
            for n in range(PARTS):
                ins = nc.vector.tensor_copy(l1_part[:, n, :, :], left)
                if n < PARTS - 1:
                    ins.then_inc(s_v, 1)
                    dve.wait_ge(s_v, 2 * n + 1)
                    nc.vector.tensor_tensor(l1_rest[:, n, :, :], left, l1_part[:, n, :, :], ALU.subtract).then_inc(s_v, 1)
                    dve.wait_ge(s_v, 2 * n + 2)
                    left = l1_rest[:, n, :, :]
            ins.then_inc(s_parts, 1)
            dve.wait_ge(s_iota, 1)
            nc.vector.tensor_copy(iota16[:, :], iota16_int[:, :]).then_inc(s_v, 1)
            dve.wait_ge(s_v, 5)
            nc.vector.tensor_scalar(weight16[:, :, :], iota16[:, :].unsqueeze(1).to_broadcast([P, 4, 16]), -1.0, 16.0,
                                    ALU.mult, ALU.add).then_inc(s_v, 1)
            dve.wait_ge(s_v, 6)
            FRONT, TAIL = 6, 5

            def add_rows(ch):
                c = ch.slot
                dve.wait_ge(s_x[c], ch.use * 16 + 16)
                w2_done.wait(dve, ch.it)
                for t in range(TPC):
                    nc.vector.tensor_tensor(x[:, c, t, 0:C], x[:, c, t, 0:C], ps_x[t][:, 0, :], ALU.add)
                    v = x[:, c, t, C:D].rearrange("p (d i) -> p d i", i=3)
                    last = nc.vector.tensor_tensor(v, v, ps_x[t][:, 1:4, :].rearrange("p i d -> p d i"), ALU.add)
                last.then_inc(x1_done.sem, 1)
                x1_done.wait(dve, ch.it)
                for t in range(TPC):
                    last = nc.vector.bn_stats(stats[:, c, t, :], x[:, c, t, :])
                last.then_inc(stat.sem, 1)
                stat.wait_apart(dve, ch.it, s_gate_v)
                for t in range(TPC):
                    last = nc.vector.bn_aggr(mv[:, c, t, :], stats[:, c, t, :])
                last.then_inc(var.sem, 1)

            def decode(ch):
                c, h = ch.slot, ch.slot % 2
                root.wait(dve, ch.it)
                nc.vector.reciprocal(rstd[:, c, :], std[:, c, :]).then_inc(inv.sem, 1)
                inv.wait(dve, ch.it)
                for t in range(TPC):
                    last = nc.vector.tensor_scalar(xl[:, c, t, :], x[:, c, t, :], mv[:, c, t, 0:1], rstd[:, c, t:t + 1],
                                                   ALU.subtract, ALU.mult)
                last.then_inc(normed.sem, 1)
                normed.wait(dve, ch.it)
                nc.vector.scalar_tensor_tensor(out=score[:, h].rearrange("p t n j -> p t (n j)"), in0=xl[:, c, :, NIB:NIB + 64],
                                               scalar=0.5, in1=weight16[:, :, :].rearrange("p n j -> p (n j)").unsqueeze(1).to_broadcast([P, TPC, 64]),
                                               op0=ALU.is_gt, op1=ALU.mult)
                nc.vector.tensor_scalar(flags[:, h], xl[:, c, :, 0:3], 0.5, None, ALU.is_gt)
                flag, part, rest = xl[:, c, :, FLAG:FLAG + 2], fpart[:, h], frest[:, h]

                def step(n, ins):
                    ins.then_inc(dve_front.sem, 1)
                    dve_front.wait(dve, ch.it * FRONT + n)

                step(0, nc.vector.tensor_copy(part[:, 0], flag))
                nc.vector.tensor_reduce(best[:, h], score[:, h], AX.X, ALU.max)
                nc.vector.tensor_tensor(mask[:, c, :, 0], flags[:, h, :, 0], flags[:, h, :, 1], ALU.mult)
                step(1, nc.vector.tensor_tensor(rest[:, 0], flag, part[:, 0], ALU.subtract))
                nc.vector.tensor_scalar(any16[:, h], best[:, h], 0.0, 16.0, ALU.is_gt, ALU.mult)
                nc.vector.tensor_tensor(mask[:, c, :, 3], flags[:, h, :, 0], mask[:, c, :, 0], ALU.subtract)
                step(2, nc.vector.tensor_copy(part[:, 1], rest[:, 0]))
                nc.vector.tensor_tensor(mask[:, c, :, 1], mask[:, c, :, 3], flags[:, h, :, 2], ALU.mult)
                nc.vector.tensor_tensor(feats[:, h, :, :, 0:2].rearrange("p t q f -> p t f q"),
                                        any16[:, h].rearrange("p t (f q) -> p t f q", q=2),
                                        best[:, h].rearrange("p t (f q) -> p t f q", q=2), ALU.subtract)
                step(3, nc.vector.tensor_tensor(rest[:, 1], rest[:, 0], part[:, 1], ALU.subtract))
                nc.vector.tensor_tensor(mask[:, c, :, 2], mask[:, c, :, 0], mask[:, c, :, 1], ALU.add)
                for n in range(2):
                    nc.vector.tensor_copy(feats[:, h, :, :, 3 + 2 * n:5 + 2 * n],
                                          part[:, n].unsqueeze(2).to_broadcast([P, TPC, 2, 2]))
                step(4, nc.vector.tensor_copy(part[:, 2], rest[:, 1]))
                step(5, nc.vector.tensor_copy(feats[:, h, :, :, 7:9], part[:, 2].unsqueeze(2).to_broadcast([P, TPC, 2, 2])))
                turned.wait(dve, ch.it - 2)
                nc.vector.tensor_copy(feats3[:, h, :, :, :, 0:NF].rearrange("p t q r f -> p (t q) r f"),
                                      feats[:, h].rearrange("p t q f -> p (t q) f").unsqueeze(2).to_broadcast([P, TPC * 2, PARTS, NF])
                                      ).then_inc(feats_done.sem, 1)

            def outputs(it, c):
                def step(n, ins):
                    ins.then_inc(dve_tail.sem, 1)
                    dve_tail.wait(dve, it * TAIL + n)

                l3_done.wait(dve, it)
                nc.vector.tensor_tensor(y[:, :, :, :], y_ps, b3[:, :].unsqueeze(1).unsqueeze(1).to_broadcast([P, TPC, 2, 4]),
                                        ALU.add).then_inc(y_read.sem, 1)
                y_read.wait(dve, it)
                for t in range(TPC):
                    ins = nc.vector.tensor_tensor(yy[:, t].rearrange("p q (o m) -> p q o m", m=2), y[:, t].rearrange("p q (o m) -> p q o m", m=2),
                                                  mask[:, c, t, 0:2].unsqueeze(1).unsqueeze(1).to_broadcast([P, 2, 2, 2]), ALU.mult)
                step(0, ins)
                step(1, nc.vector.tensor_tensor(ym[:, :, :, :], yy[:, :, :, 0:4:2], yy[:, :, :, 1:4:2], ALU.add))
                nc.vector.tensor_scalar(yr[:, :, :], ym[:, :, :, 0], 0.0, 15.0, ALU.max, ALU.min)
                step(2, nc.vector.scalar_tensor_tensor(out=yc[:, :], in0=ym[:, :, 1, 1], scalar=0.5, in1=mask[:, c, :, 2],
                                                       op0=ALU.is_gt, op1=ALU.mult))
                nc.vector.tensor_scalar(yr[:, :, :], yr[:, :, :], float(2 ** 23), None, ALU.add).then_inc(dve_tail.sem, 1)
                dve_tail.wait(dve, it * TAIL + 3)
                nc.vector.tensor_scalar(yr[:, :, :], yr[:, :, :], float(2 ** 23), None, ALU.subtract).then_inc(dve_tail.sem, 1)
                dve_tail.wait(dve, it * TAIL + 4)
                nc.vector.tensor_tensor(hot[:, :, :, :], iota16[:, :].unsqueeze(1).unsqueeze(1).to_broadcast([P, TPC, 2, 16]),
                                        yr[:, :, :].unsqueeze(3).to_broadcast([P, TPC, 2, 16]), ALU.is_equal).then_inc(hot_made.sem, 1)
                hot_made.wait(dve, it)
                for t in range(TPC):
                    ins = nc.vector.tensor_scalar(hot[:, t, :, :], hot[:, t, :, :], mask[:, c, t, 2:3], 2.0, ALU.mult, ALU.mult)
                ins.then_inc(hot_scaled.sem, 1)
                hot_scaled.wait(dve, it)
                added.wait(dve, it)
                o = x[:, c, :, OUTPUT:OUTPUT + 32]
                nc.vector.tensor_tensor(o, o, hot[:, :, :, :].rearrange("p t q j -> p t (q j)"), ALU.add)
                o = x[:, c, :, OUTPUT + 32]
                nc.vector.tensor_tensor(o, o, yc[:, :], ALU.add).then_inc(done.sem, 1)

            hot_made = Steps(s_hot)
            hot_scaled = Steps(s_hot_scaled)
            c0, c1 = (item(0, 0, s, NCH) for s in range(2))
            add_rows(c0)
            add_rows(c1)
            decode(c0)

            def body(ch):
                if ch.later(1):
                    decode(ch.later(1))
                if ch.later(2):
                    add_rows(ch.later(2))
                if not ch.first:
                    outputs(ch.it - 1, (ch.slot - 1) % 4)
            dve.wait_ge(s_w, 16 * N_WEIGHTS)
            over(dve, 0, NCH, 4, body)
            outputs(NCH - 1, (NCH - 1) % 4)


def build(nc, a):
    with ExitStack() as ctx:
        sb, ps, sem = alloc(nc, ctx)
        keep = {
            "ident": sb("ident", [C, C]),
            "w2": sb("w2", [C, 2, C]),
            "half": sb("half", [C, 1]),
        }
        keep.update({
            "base": sb("base", [1, NG], I32),
            "base_all": sb("base_all", [P, NG]),
            "passes": sb("passes", [1, 1], I32),
            "win_iota_int": sb("win_iota_int", [P, WIN], I32),
            "win_iota": sb("win_iota", [P, WIN]),
            "wf2": sb("wf2", [C, 4, C]),
            "bias": sb("bias", [P, 4, C]),
            "w1": sb("w1", [C, 4, C]),
        })
        with ExitStack() as place_ctx:
            sb, ps, sem = alloc(nc, place_ctx)
            keep.update({
                "edge": sb("edge", [P, E // P, ROW - C]),
                "keys": sb("keys", [P, E // P, 2], F16),
                "low_hot": sb("low_hot", [P, E // P, LOWS], BF16),
                "places": sb("places", [HIGHS, LOWS, E // P]),
                "wf1": sb("wf1", [NRBF + 1, C]),
                "w_in": sb("w_in_scaled", [C, 2, C]),
                "eps": sb("epsilon", [C, 1]),
                "ident16": sb("ident16", [C, C], F16),
                "earlier": sb("earlier", [C, C]),
                "lower": sb("lower", [C, C]),
                "row_iota_int": sb("row_iota_int", [C, C], I32),
                "row_iota": sb("row_iota", [C, C], F16),
                "part_iota_int": sb("part_iota_int", [C, 1], I32),
                "part_iota": sb("part_iota", [C, 1]),
                "ends_iota_int": sb("ends_iota_int", [C, 2, NG], I32),
                "ends_iota": sb("ends_iota", [C, 2, NG]),
            })
            setup(nc, a, keep)
            count_edges(nc, a, keep)
            place_edges(nc, a, keep)
        sb, ps, sem = alloc(nc, ctx)
        keep["node_sums"] = ctx.enter_context(nc.sbuf_tensor("node_sums", [C, 4, NP], F32))
        sum_edges(nc, a, keep)
        finish(nc, a, keep)


def kernel(**inputs):
    import concourse.bacc as bacc
    from concourse.bass_utils import run_bass_kernel_spmd

    def tiles(v):
        v = np.asarray(v).reshape(E // P, P, -1)
        return np.ascontiguousarray(v.transpose(1, 2, 0).squeeze(1) if v.shape[2] == 1 else v.transpose(1, 2, 0))

    given = {
        "x": np.asarray(inputs["x"]),
        "src": tiles(inputs["src"]),
        "dst": tiles(inputs["dst"]),
        "edge_attr_20": np.ascontiguousarray(np.asarray(inputs["edge_attr_20"]).T),
        "edge_attr_3": tiles(inputs["edge_attr_3"]),
        "edge_weight": tiles(inputs["edge_weight"]),
    }
    for name in ("W_in2f_s", "W_in2f_v", "Wf1", "Wf2", "W1_s", "W1_v", "W2_s", "W2_v"):
        given[name] = np.asarray(inputs["L0_gnn_" + name])
    for name in ("bf1", "bf2"):
        given[name] = np.asarray(inputs["L0_gnn_" + name]).reshape(1, -1)
    for name in ("Wa", "Ws"):
        given[name] = np.ascontiguousarray(np.asarray(inputs["L0_ffn_" + name]).transpose(0, 2, 1))
    for name in ("ba", "bs"):
        given[name] = np.asarray(inputs["L0_ffn_" + name])

    nc = bacc.Bacc("TRN2", target_bir_lowering=False, num_devices=1)
    arrays, a = {}, {}
    for name, value in given.items():
        arrays["in_" + name] = value
        a[name] = nc.dram_tensor("in_" + name, value.shape, mybir.dt.from_np(value.dtype), kind="ExternalInput").ap()
    a["out"] = nc.dram_tensor("out", (N, D), F32, kind="ExternalOutput").ap()
    a["table"] = nc.dram_tensor("table", (N, D), F32, kind="Internal").ap()
    a["sorted"] = nc.dram_tensor("sorted", (E, ROW), F32, kind="Internal").ap()
    build(nc, a)
    r = run_bass_kernel_spmd(nc, [arrays], core_ids=[0])
    return r.results[0]["out"]
```
